# Optimizing a Trainium2 kernel written in Bass

```python
import numpy as np
import jax
import jax.numpy as jnp

def _softmax(x, axis=-1):
    return jax.nn.softmax(x, axis=axis)

def _gelu(x):
    return jax.nn.gelu(x, approximate=True)

def _silu(x):
    return jax.nn.silu(x)

def _sigmoid(x):
    return jax.nn.sigmoid(x)

def _layernorm(x, axis=-1, eps=1e-05):
    m = jnp.mean(x, axis=axis, keepdims=True)
    v = jnp.var(x, axis=axis, keepdims=True)
    return (x - m) / jnp.sqrt(v + eps)

def _scatter_add(tgt, idx, src, axis=0):
    return tgt.at[idx].add(src)

def _segment_sum(src, seg, n):
    return jax.ops.segment_sum(src, seg, n)
kernel_name = 'mk_gps_d1_gnn_r8_ce2371'

def setup_inputs(seed: int=0):
    np.random.seed(seed)
    _w = jnp.asarray

    def _rec_inputs():
        import jax
        import jax.numpy as jnp
        _gk = jax.random.key(seed)
        x = -0.0003713 + 1 * jax.random.normal(jax.random.fold_in(_gk, 1), (6250, 256), jnp.float32)
        src = jax.random.randint(jax.random.fold_in(_gk, 2), (100000,), 0, 6250, jnp.int32)
        dst = jax.random.randint(jax.random.fold_in(_gk, 3), (100000,), 0, 6250, jnp.int32)
        _o = jnp.argsort(dst, stable=True)
        src = src[_o]
        dst = dst[_o]
        return (x, src, dst)
    x, src, dst = _rec_inputs()

    def _L0_gnn_setup():
        import jax, jax.numpy as jnp
        import numpy as np
        N_NODES = 6250
        N_EDGES = 100000
        D_IN = 256
        D_OUT = 256
        key = jax.random.key(seed)
        k1, k2, k3, k4 = jax.random.split(key, 4)
        bound = 1.0 / np.sqrt(D_IN)
        vertex_features = jax.random.normal(k1, (N_NODES, D_IN), dtype=jnp.float32)
        edge_index = jax.random.randint(k2, (2, N_EDGES), 0, N_NODES, dtype=jnp.int32)
        w0 = jax.random.uniform(k3, (D_IN, D_OUT), minval=-bound, maxval=bound, dtype=jnp.float32)
        w1 = jax.random.uniform(k4, (D_IN, D_OUT), minval=-bound, maxval=bound, dtype=jnp.float32)
        return {'vertex_features': vertex_features, 'edge_index': edge_index, 'w0': w0, 'w1': w1}
    _L0_gnn_all = _L0_gnn_setup()
    _L0_gnn_in = {k: v for k, v in _L0_gnn_all.items() if k in ('w0', 'w1')}
    del _L0_gnn_all

    def _L0_mix_setup():
        import jax, jax.numpy as jnp
        import numpy as np
        NUM_HEADS = 8
        key = jax.random.key(seed)
        ks = jax.random.split(key, 5)
        B, N, C = (8, 2048, 256)
        x = jax.random.normal(ks[0], (B, N, C), dtype=jnp.float32)
        Wq = jax.random.normal(ks[1], (C, C), dtype=jnp.float32) * 0.02
        Wkv = jax.random.normal(ks[2], (2 * C, C), dtype=jnp.float32) * 0.02
        Wproj = jax.random.normal(ks[3], (C, C), dtype=jnp.float32) * 0.02
        bproj = jnp.zeros((C,), dtype=jnp.float32)
        return {'x': x, 'Wq': Wq, 'Wkv': Wkv, 'Wproj': Wproj, 'bproj': bproj}
    _L0_mix_all = _L0_mix_setup()
    _L0_mix_in = {k: v for k, v in _L0_mix_all.items() if k in ('Wq', 'Wkv', 'Wproj', 'bproj')}
    del _L0_mix_all

    def _L0_ffn_setup():
        import jax, jax.numpy as jnp
        import numpy as np
        B, N, D = (16, 512, 256)
        NUM_EXPERTS, TOP_K, HEADS = (4, 2, 4)
        N_EDGES = 131072
        LN_EPS = 1e-05

        def _layernorm(x, g, b):
            mu = x.mean(-1, keepdims=True)
            var = ((x - mu) ** 2).mean(-1, keepdims=True)
            return (x - mu) * jax.lax.rsqrt(var + LN_EPS) * g + b

        def _forward(x, edge_index, W_gat, att_src, att_dst, b_gat, ln_gamma, ln_beta, W1, b1, W2, b2):
            Bc, Nc, Dc = x.shape
            M = Bc * Nc
            x_flat = x.reshape(M, Dc)
            h = (x_flat @ W_gat).reshape(M, HEADS, NUM_EXPERTS)
            loops = jnp.arange(M, dtype=edge_index.dtype)
            src = jnp.concatenate([edge_index[0], loops])
            dst = jnp.concatenate([edge_index[1], loops])
            a_src = (h * att_src).sum(-1)
            a_dst = (h * att_dst).sum(-1)
            e = jax.nn.leaky_relu(a_src[src] + a_dst[dst], negative_slope=0.2)
            e_max = jax.ops.segment_max(e, dst, num_segments=M)
            ee = jnp.exp(e - e_max[dst])
            denom = jax.ops.segment_sum(ee, dst, num_segments=M)
            alpha = ee / (denom[dst] + 1e-16)
            msg = h[src] * alpha[:, :, None]
            agg = jax.ops.segment_sum(msg, dst, num_segments=M).reshape(M, HEADS * NUM_EXPERTS) + b_gat
            scores = _layernorm(agg, ln_gamma, ln_beta).reshape(M, HEADS, NUM_EXPERTS).mean(1)
            scores = scores.reshape(Bc, Nc, NUM_EXPERTS)
            topk_s, topk_i = jax.lax.top_k(scores, TOP_K)
            w = jax.nn.softmax(topk_s, axis=-1)
            out = jnp.zeros_like(x)
            for ei in range(NUM_EXPERTS):
                g = jnp.where(topk_i == ei, w, 0.0).sum(-1)
                hh = jax.nn.gelu(x @ W1[ei] + b1[ei], approximate=False)
                out = out + g[..., None] * (hh @ W2[ei] + b2[ei])
            return out
        key = jax.random.key(seed)
        ks = jax.random.split(key, 8)
        s = 0.05
        return {'x': jax.random.normal(ks[0], (B, N, D), jnp.float32), 'W_gat': jax.random.normal(ks[1], (D, HEADS * NUM_EXPERTS), jnp.float32) * s, 'att_src': jax.random.normal(ks[2], (HEADS, NUM_EXPERTS), jnp.float32) * s, 'att_dst': jax.random.normal(ks[3], (HEADS, NUM_EXPERTS), jnp.float32) * s, 'b_gat': jnp.zeros((HEADS * NUM_EXPERTS,), jnp.float32), 'ln_gamma': jnp.ones((HEADS * NUM_EXPERTS,), jnp.float32), 'ln_beta': jnp.zeros((HEADS * NUM_EXPERTS,), jnp.float32), 'W1': jax.random.normal(ks[4], (NUM_EXPERTS, D, 2 * D), jnp.float32) * s, 'b1': jnp.zeros((NUM_EXPERTS, 2 * D), jnp.float32), 'W2': jax.random.normal(ks[5], (NUM_EXPERTS, 2 * D, D), jnp.float32) * s, 'b2': jnp.zeros((NUM_EXPERTS, D), jnp.float32), 'edge_index': jax.random.randint(ks[6], (2, N_EDGES), 0, B * N, jnp.int32)}
    _L0_ffn_all = _L0_ffn_setup()
    _L0_ffn_in = {k: v for k, v in _L0_ffn_all.items() if k in ('W_gat', 'att_src', 'att_dst', 'b_gat', 'ln_gamma', 'ln_beta', 'W1', 'b1', 'W2', 'b2', 'edge_index')}
    del _L0_ffn_all
    return {'x': x, 'src': src, 'dst': dst, 'L0_gnn_w0': _L0_gnn_in['w0'], 'L0_gnn_w1': _L0_gnn_in['w1'], 'L0_mix_Wq': _L0_mix_in['Wq'], 'L0_mix_Wkv': _L0_mix_in['Wkv'], 'L0_mix_Wproj': _L0_mix_in['Wproj'], 'L0_mix_bproj': _L0_mix_in['bproj'], 'L0_ffn_W_gat': _L0_ffn_in['W_gat'], 'L0_ffn_att_src': _L0_ffn_in['att_src'], 'L0_ffn_att_dst': _L0_ffn_in['att_dst'], 'L0_ffn_b_gat': _L0_ffn_in['b_gat'], 'L0_ffn_ln_gamma': _L0_ffn_in['ln_gamma'], 'L0_ffn_ln_beta': _L0_ffn_in['ln_beta'], 'L0_ffn_W1': _L0_ffn_in['W1'], 'L0_ffn_b1': _L0_ffn_in['b1'], 'L0_ffn_W2': _L0_ffn_in['W2'], 'L0_ffn_b2': _L0_ffn_in['b2'], 'L0_ffn_edge_index': _L0_ffn_in['edge_index']}

def reference(x, src, dst, L0_gnn_w0, L0_gnn_w1, L0_mix_Wq, L0_mix_Wkv, L0_mix_Wproj, L0_mix_bproj, L0_ffn_W_gat, L0_ffn_att_src, L0_ffn_att_dst, L0_ffn_b_gat, L0_ffn_ln_gamma, L0_ffn_ln_beta, L0_ffn_W1, L0_ffn_b1, L0_ffn_W2, L0_ffn_b2, L0_ffn_edge_index):
    import jax
    import jax.numpy as jnp

    def _L0_gnn_ref(vertex_features, edge_index, w0, w1):
        import jax, jax.numpy as jnp
        import numpy as np
        N_NODES = 6250
        N_EDGES = 100000
        D_IN = 256
        D_OUT = 256
        w0_features = vertex_features @ w0
        w1_features = vertex_features @ w1
        dst, src = (edge_index[0], edge_index[1])
        messages = w1_features[src]
        neighbours = jax.ops.segment_sum(messages, dst, num_segments=vertex_features.shape[0])
        return jax.nn.relu(w0_features + neighbours)

    def _L0_mix_ref(x, Wq, Wkv, Wproj, bproj):
        import jax, jax.numpy as jnp
        import numpy as np
        NUM_HEADS = 8
        B, N, C = x.shape
        h = NUM_HEADS
        d = C // h
        q = jnp.einsum('bnc,oc->bno', x, Wq).reshape(B, N, h, d).transpose(0, 2, 1, 3)
        kv = jnp.einsum('bnc,oc->bno', x, Wkv).reshape(B, N, 2, h, d)
        k = kv[:, :, 0].transpose(0, 2, 1, 3)
        v = kv[:, :, 1].transpose(0, 2, 1, 3)
        q = jax.nn.elu(q) + 1.0
        k = jax.nn.elu(k) + 1.0
        k_sum = k.sum(axis=2)
        D_inv = 1.0 / jnp.maximum(jnp.einsum('bhnd,bhd->bhn', q, k_sum), 1e-06)
        context = jnp.einsum('bhnd,bhne->bhde', k, v)
        attn = jnp.einsum('bhnd,bhde->bhne', q, context) * D_inv[..., None]
        out = attn.transpose(0, 2, 1, 3).reshape(B, N, C)
        out = jnp.einsum('bnc,oc->bno', out, Wproj) + bproj
        return out

    def _L0_ffn_ref(x, W_gat, att_src, att_dst, b_gat, ln_gamma, ln_beta, W1, b1, W2, b2, edge_index):
        import jax, jax.numpy as jnp
        import numpy as np
        B, N, D = (16, 512, 256)
        NUM_EXPERTS, TOP_K, HEADS = (4, 2, 4)
        N_EDGES = 131072
        LN_EPS = 1e-05

        def _layernorm(x, g, b):
            mu = x.mean(-1, keepdims=True)
            var = ((x - mu) ** 2).mean(-1, keepdims=True)
            return (x - mu) * jax.lax.rsqrt(var + LN_EPS) * g + b

        def _forward(x, edge_index, W_gat, att_src, att_dst, b_gat, ln_gamma, ln_beta, W1, b1, W2, b2):
            Bc, Nc, Dc = x.shape
            M = Bc * Nc
            x_flat = x.reshape(M, Dc)
            h = (x_flat @ W_gat).reshape(M, HEADS, NUM_EXPERTS)
            loops = jnp.arange(M, dtype=edge_index.dtype)
            src = jnp.concatenate([edge_index[0], loops])
            dst = jnp.concatenate([edge_index[1], loops])
            a_src = (h * att_src).sum(-1)
            a_dst = (h * att_dst).sum(-1)
            e = jax.nn.leaky_relu(a_src[src] + a_dst[dst], negative_slope=0.2)
            e_max = jax.ops.segment_max(e, dst, num_segments=M)
            ee = jnp.exp(e - e_max[dst])
            denom = jax.ops.segment_sum(ee, dst, num_segments=M)
            alpha = ee / (denom[dst] + 1e-16)
            msg = h[src] * alpha[:, :, None]
            agg = jax.ops.segment_sum(msg, dst, num_segments=M).reshape(M, HEADS * NUM_EXPERTS) + b_gat
            scores = _layernorm(agg, ln_gamma, ln_beta).reshape(M, HEADS, NUM_EXPERTS).mean(1)
            scores = scores.reshape(Bc, Nc, NUM_EXPERTS)
            topk_s, topk_i = jax.lax.top_k(scores, TOP_K)
            w = jax.nn.softmax(topk_s, axis=-1)
            out = jnp.zeros_like(x)
            for ei in range(NUM_EXPERTS):
                g = jnp.where(topk_i == ei, w, 0.0).sum(-1)
                hh = jax.nn.gelu(x @ W1[ei] + b1[ei], approximate=False)
                out = out + g[..., None] * (hh @ W2[ei] + b2[ei])
            return out
        return _forward(x, edge_index, W_gat, att_src, att_dst, b_gat, ln_gamma, ln_beta, W1, b1, W2, b2)
    edge_index = jnp.stack([src, dst])
    xn = _layernorm(x, axis=-1)
    x = x + _L0_gnn_ref(xn, edge_index, L0_gnn_w0, L0_gnn_w1) + _L0_mix_ref(xn[None], L0_mix_Wq, L0_mix_Wkv, L0_mix_Wproj, L0_mix_bproj)[0]
    x = x + _L0_ffn_ref(_layernorm(x, axis=-1)[None], L0_ffn_W_gat, L0_ffn_att_src, L0_ffn_att_dst, L0_ffn_b_gat, L0_ffn_ln_gamma, L0_ffn_ln_beta, L0_ffn_W1, L0_ffn_b1, L0_ffn_W2, L0_ffn_b2, L0_ffn_edge_index)[0]
    return x

_drawn_inputs = setup_inputs


def setup_inputs(seed=0):
    import zlib

    import numpy as np

    out = dict(_drawn_inputs(seed))
    spreads = {'L0_mix_bproj': (0.0, 0.1),
     'L0_ffn_b_gat': (0.0, 0.1),
     'L0_ffn_ln_gamma': (1.0, 0.2),
     'L0_ffn_ln_beta': (0.0, 0.1),
     'L0_ffn_b1': (0.0, 0.3),
     'L0_ffn_b2': (0.0, 0.1)}
    factors = {'L0_mix_Wq': 8.0, 'L0_mix_Wkv': 8.0, 'L0_mix_Wproj': 8.0}
    for name, (base, spread) in spreads.items():
        noise = np.random.default_rng([zlib.crc32(name.encode()), seed]).standard_normal(out[name].shape)
        drawn = base * np.exp(spread * noise) if base else spread * noise
        out[name] = jnp.asarray(drawn.astype(out[name].dtype))
    for name, factor in factors.items():
        out[name] = (out[name] * factor).astype(out[name].dtype)
    return out
```

```python
from contextlib import ExitStack

import concourse.bass as bass
from concourse import mybir

F32, I32, F16, BF16, U16 = (mybir.dt.float32, mybir.dt.int32, mybir.dt.float16, mybir.dt.bfloat16,
                            mybir.dt.uint16)
DVE, PE = mybir.EngineType.DVE, mybir.EngineType.PE
ALU, ACT, AX = mybir.AluOpType, mybir.ActivationFunctionType, mybir.AxisListType

P = 128
BANK = 512
N, D = 6250, 256
NB = -(-N // P)
TAIL = N - (NB - 1) * P
NPAD = NB * P
C = D // P
HEAD = 32
EPS = 1e-5
NE, F = 4, 512
FC = F // P
GH, GC = 4, 4
HW = GH * GC
ROW = HW + GH
G = 16
BIG = 1e30
HALF = 8
PER_BANK = 25


class Graph:

    def __init__(self, edges):
        self.E = edges
        self.T = 2 * -(-edges // (2 * P))
        most = (edges + NB * (P - 1)) // P
        self.NT = -(-most // G) * G
        self.chunks = [(a, min(BANK, self.NT - a)) for a in range(0, self.NT, BANK)]
        self.full = edges // self.T
        self.rest = edges - self.full * self.T


CONSTS = 9 + 2 + P // HEAD + 4
CONV, GAT = Graph(100000), Graph(131072)
TM, NTM = max(CONV.T, GAT.T), max(CONV.NT, GAT.NT)


class Carve:

    def __init__(self, tensor, words):
        self.tensor, self.words, self.at = tensor, words, 0

    def take(self, n, dtype=F32):
        words = n if dtype in (F32, I32) else -(-n // 2)
        a = self.at
        self.at += words
        assert self.at <= self.words, (self.at, self.words)
        ap = self.tensor[:, a:a + words]
        return ap if dtype is F32 else ap.bitcast(dtype)[:, 0:n]


class Steps:

    def __init__(self, eng, sem):
        self.eng, self.sem, self.base, self.k, self.turn = eng, sem, 0, 0, None

    def value(self):
        return self.base + self.k if self.turn is None else self.turn + (self.base + self.k)

    def did(self, ins):
        ins.then_inc(self.sem, 1)
        self.k += 1

    def settle(self):
        self.eng.wait_ge(self.sem, self.value())

    def do(self, ins):
        self.did(ins)
        self.settle()

    def enter(self, i, per_turn):
        self.base, self.k, self.turn = self.base + self.k, 0, i * per_turn

    def leave(self, turns, per_turn):
        assert self.k == per_turn, (self.k, per_turn)
        self.base, self.k, self.turn = self.base + turns * per_turn, 0, None


def layer(nc, io):
    ctx = ExitStack()
    with ctx:
        sem_names = []

        def sem(name):
            sem_names.append(name)
            return ctx.enter_context(nc.semaphore(name))

        def sb(name, cols, dtype=F32, rows=P):
            return ctx.enter_context(nc.sbuf_tensor(name, [rows, cols], dtype))

        msg_d = nc.dram_tensor("messages", (NPAD, D), F32, kind="Internal").ap()
        q_d = nc.dram_tensor("q_t", (P, C * NPAD), F32, kind="Internal").ap()
        xt_d = nc.dram_tensor("x2n_t", (P, C * NPAD), F32, kind="Internal").ap()
        row_d = nc.dram_tensor("gat_rows", (NPAD, ROW), F32, kind="Internal").ap()
        q_dv = q_d.rearrange("p (c n) -> p c n", c=C)
        xt_dv = xt_d.rearrange("p (c n) -> p c n", c=C)

        x_sb = sb("x_sb", NB * D)
        arena_words = max(NB * D + 9 * TM + NTM, GAT.NT * ROW)
        arena_t = sb("arena", arena_words)
        arena = Carve(arena_t, arena_words)
        acc = arena.take(NB * D)
        tg, sr, tmp = (arena.take(TM, I32) for _ in range(3))
        bk, oh = arena.take(TM, F16), arena.take(TM, F16)
        cum = arena.take(NTM)
        pos, slo, shi = (arena.take(TM) for _ in range(3))
        hi, lo = arena.take(TM), arena.take(TM)
        rows_all = arena_t[:, 0:GAT.NT * ROW]
        ffn = Carve(arena_t, arena_words)
        w1 = ffn.take(C * NE * F)
        w2 = ffn.take(NE * FC * D)
        xt3 = ffn.take(2 * C * P)
        hT = ffn.take(2 * F)
        outb = ffn.take(D)
        b2_row = ffn.take(NE * D)[0:1, :]

        idx = {CONV: sb("conv_idx", CONV.NT + G, I32), GAT: sb("gat_idx", GAT.NT + G, I32)}
        dlo = {CONV: sb("conv_dlo", CONV.NT + G, F16), GAT: sb("gat_dlo", GAT.NT + G, F16)}
        conv_at = sb("conv_at", CONV.NT, I32, 1)
        dm_at = sb("dm_at", GAT.NT, I32, 1)
        sum_at = sb("sum_at", GAT.NT, I32, 1)
        iota_t = sb("iota_t", NTM, F16)
        slot1h = [sb(f"slot1h{k}", NTM, F16) for k in range(2)]
        put_hi = [sb(f"put_hi{k}", P, F16) for k in range(2)]
        put_lo = [sb(f"put_lo{k}", P, F16) for k in range(2)]
        iota_p = sb("iota_p", P, F16)
        iota_b = sb("iota_b", 64)
        zero16 = sb("zero16", P, F16)
        ident = sb("ident", P)
        ident_b = sb("ident_b", P, BF16)
        ident_big = sb("ident_big", P, BF16)
        ones = sb("ones", P)
        ones16 = sb("ones16", 1, F16)
        before = sb("before", P)
        headmask = sb("headmask", P)
        cnt, off, til, cumt, base, totf = (sb(n, NB) for n in ("cnt", "off", "til", "cumt", "base", "totf"))
        tot = sb("tot", NB, I32)
        bcol = sb("bcol", 1)
        cmpb = slot1h[0]
        signal_word = sb("signal_word", 1)
        stat = sb("stat", NB * 6)
        mean, var, rstd, st1, st2 = (sb(n, NB) for n in ("mean", "var", "rstd", "st1", "st2"))

        shared_words = 7040
        shared_t = sb("shared", shared_words)
        ph = Carve(shared_t, shared_words)
        w_wk = ph.take(C * 512)
        w_kv = ph.take(C * 512)
        w_q = ph.take(C * D)
        w_p = ph.take(C * D)
        xn, xnT, kexp, kk, vv, qexp, qq, msgb = (ph.take(D) for _ in range(8))
        ks, cbt = ph.take(C * P), ph.take(C * P)
        cpw = ph.take(C * D)
        bp_row = ph.take(D)[0:1, :]
        cv = Carve(shared_t, shared_words)
        rows = cv.take(G * D)
        oh1 = [cv.take(P) for _ in range(2)]
        st_conv = cv.take(G, I32)
        ga = Carve(shared_t, shared_words)
        w_g = ga.take(C * HW)
        xn2, xnT2 = ga.take(D), ga.take(D)
        hrow = ga.take(NB * ROW)
        ad_tmp = ga.take(NB * HW)
        dm = ga.take(NB * 2 * GH)
        rg = ga.take(G * ROW)
        st_gat = ga.take(G, I32)
        sbf = ga.take(G * GH, BF16)
        nohb = [ga.take(P, BF16) for _ in range(4)]
        mx = ga.take(4 * GH)
        ohf = [ga.take(HALF * P) for _ in range(2)]
        ohT = ga.take(HALF * P)
        zz, ee = ga.take(HALF * GH), ga.take(HALF * GH)
        msg = ga.take(HALF * ROW)
        den = ga.take(NB * GH)
        eself = ga.take(NB * GH)
        b1_col = sb("b1_col", NE * FC)
        smalls = sb("smalls", 5 * HW)
        gate = sb("gate", NB * NE)

        ps = ctx.enter_context(nc.psum_tensor("ps", [P, 8, BANK], F32))

        def nodes(ap, t, w=D):
            return ap[:, bass.ds(t * w, w)]

        const_ready = sem("const_ready")
        edges_in = {CONV: sem("conv_edges_in"), GAT: sem("gat_edges_in")}
        pads_set = {CONV: sem("conv_pads_set")}
        x_in, w_in, wg_in, ffn_in, small_in = (sem(n) for n in ("x_in", "w_in", "wg_in", "ffn_in", "small_in"))
        x_pad = sem("x_pad")
        dve_step, act_step, marks = sem("dve_step"), sem("act_step"), sem("marks")
        sorts = {}
        for g, nm in ((CONV, "conv"), (GAT, "gat")):
            sorts[g] = {k: sem(f"{nm}_{k}") for k in
                        ("counted", "prefix", "based", "basecol", "compared", "blocks", "block_known",
                         "onehots", "placed", "sorted")}
        var_ready, std_ready = [sem("var1"), sem("var2")], [sem("std1"), sem("std2")]
        xn_ready, xt_psum, xt_ready = sem("xn_ready"), sem("xt_psum"), sem("xt_ready")
        kv_psum, w_psum, q_psum = sem("kv_psum"), sem("w_psum"), sem("q_psum")
        kexp_ready, v_ready, k_ready, qexp_ready, q_ready = (sem(n) for n in (
            "kexp_ready", "v_ready", "k_ready", "qexp_ready", "q_ready"))
        msg_ready, msg_stored, msg_free, q_stored, q_free = (sem(n) for n in (
            "msg_ready", "msg_stored", "msg_free", "q_stored", "q_free"))
        ctx_used, ctx_done = sem("ctx_used"), sem("ctx_done")
        ctx_masked, cp_psum, cp_ready = sem("ctx_masked"), sem("cp_psum"), sem("cp_ready")
        q_back, den_psum, qn_ready, at_psum, at_added = (sem(n) for n in (
            "q_back", "den_psum", "qn_ready", "at_psum", "at_added"))
        conv_staged = sem("conv_staged")
        row_in = [sem(f"row_in{k}") for k in range(G)]
        conv_oh, conv_psum, conv_added = sem("conv_oh"), sem("conv_psum"), sem("conv_added")
        x2_ready = sem("x2_ready")
        xn2_ready, xt2_psum, xt2_ready, xt2_stored, xt2_free, h_psum = (sem(n) for n in (
            "xn2_ready", "xt2_psum", "xt2_ready", "xt2_stored", "xt2_free", "h_psum"))
        hrow_ready, hrow_stored = sem("hrow_ready"), sem("hrow_stored")
        gat_staged, gat_in = sem("gat_staged"), [sem(f"gat_in{k}") for k in range(G)]
        gat_kept, gat_noh, max_psum, max_taken = (sem(n) for n in (
            "gat_kept", "gat_noh", "max_psum", "max_taken"))
        dm_ready = sem("dm_ready")
        oh_ready, ohT_psum, ohT_ready, dm_psum, z_ready, ee_ready, m_ready, sum_done = (sem(n) for n in (
            "oh_ready", "ohT_psum", "ohT_ready", "dm_psum", "z_ready", "ee_ready", "m_ready", "sum_done"))
        self_e, gate_z, gate_e, gvar, gstd, gates_ready = (sem(n) for n in (
            "self_e", "gate_z", "gate_e", "gvar", "gstd", "gates_ready"))
        xt3_in = [sem("xt3_in0"), sem("xt3_in1")]
        hid_psum, hid_ready, y_psum, y_taken, out_free, out_stored = (sem(n) for n in (
            "hid_psum", "hid_ready", "y_psum", "y_taken", "out_free", "out_stored"))

        block = ctx.enter_context(nc.Block())

        def hold(eng, s, value):
            eng.wait_ge(s, value)
            eng.sem_inc(marks, 1)

        def columns(engine, row, at, n, most):
            return nc.values_load_multi_w_load_instructions(
                row[0:1, bass.ds(at, n)], engines=[engine], min_val=0, max_val=most,
                skip_runtime_bounds_check_because="they are columns of blocks, below the last block by construction")[1]

        dm_most = (NB - 1) * 2 * GH
        sum_most = (NB - 1) * ROW + BANK - PER_BANK * ROW

        @block.sync
        def _(sp):
            def load_edges(g):
                t, s = io["edges"][g]
                for dst, src in ((tg, t), (sr, s)):
                    sp.dma_start(dst[0:g.full, 0:g.T],
                                 src[0:g.full * g.T].rearrange("(p t) -> p t", t=g.T)).then_inc(edges_in[g], 16)
                    if g.rest:
                        sp.dma_start(dst[g.full:g.full + 1, 0:g.rest],
                                     src[g.full * g.T:g.E].rearrange("(p t) -> p t", t=g.rest)
                                     ).then_inc(edges_in[g], 16)

            sp.wait_ge(pads_set[CONV], 2)
            load_edges(CONV)
            sp.wait_ge(x_pad, 1)
            sp.dma_start(x_sb[:, 0:(NB - 1) * D].rearrange("p (t f) -> p t f", f=D),
                         io["x"][0:(NB - 1) * P, :].rearrange("(t p) f -> p t f", p=P)).then_inc(x_in, 16)
            sp.dma_start(x_sb[0:TAIL, (NB - 1) * D:], io["x"][(NB - 1) * P:N, :]).then_inc(x_in, 16)
            chunked = "(c p) n -> p c n"
            wk = w_wk.rearrange("p (c n) -> p c n", c=C)
            sp.dma_start(wk[:, :, 0:D], io["w0"].rearrange(chunked, p=P)).then_inc(w_in, 16)
            sp.dma_start(wk[:, :, D:], io["w1"].rearrange(chunked, p=P)).then_inc(w_in, 16)
            for dst, src in ((w_kv, "WkvT"), (w_q, "WqT"), (w_p, "WprojT")):
                sp.dma_start(dst.rearrange("p (c n) -> p c n", c=C), io[src].rearrange(chunked, p=P)).then_inc(w_in, 16)
            sp.dma_start(bp_row[:], io["bproj"].rearrange("(a n) -> a n", a=1)).then_inc(w_in, 16)
            sp.dma_start(b1_col[:], io["b1T"]).then_inc(small_in, 16)
            for k, name in enumerate(("att_src", "att_dst", "b_gat", "gamma", "beta")):
                src = io[name].rearrange("(a n) -> a n", a=1).broadcast_to((P, HW))
                sp.dma_start(smalls[:, k * HW:(k + 1) * HW], src).then_inc(small_in, 16)

            sp.sem_inc(msg_free, 1)
            sp.sem_inc(q_free, 1)
            with sp.Fori(0, NB) as t:
                hold(sp, msg_ready, t + 2)
                sp.dma_start(msg_d[bass.ds(t * P, P), :], msgb).then_inc(msg_stored, 16)
                hold(sp, q_ready, t + 2)
                sp.dma_start(q_dv[:, :, bass.ds(t * P, P)], qq.rearrange("p (c n) -> p c n", c=C)).then_inc(q_stored, 16)
                hold(sp, msg_stored, t * 16 + 16)
                sp.sem_inc(msg_free, 1)
                hold(sp, q_stored, t * 16 + 16)
                sp.sem_inc(q_free, 1)
            with sp.Fori(0, NB) as t:
                hold(sp, qn_ready, t + 1)
                sp.dma_start(qexp.rearrange("p (c n) -> p c n", c=C), q_dv[:, :, bass.ds(t * P, P)]).then_inc(q_back, 16)
            sp.wait_ge(sorts[CONV]["sorted"], 1)
            load_edges(GAT)
            sp.wait_ge(x2_ready, 1)
            sp.dma_start(w_g.rearrange("p (c n) -> p c n", c=C), io["W_gat"].rearrange(chunked, p=P)).then_inc(wg_in, 16)
            sp.sem_inc(xt2_free, 1)
            with sp.Fori(0, NB) as t:
                hold(sp, xt2_ready, t + 1)
                sp.dma_start(xt_dv[:, :, bass.ds(t * P, P)], xnT2.rearrange("p (c n) -> p c n", c=C)).then_inc(xt2_stored, 16)
                hold(sp, xt2_stored, t * 16 + 16)
                sp.sem_inc(xt2_free, 1)
            sp.wait_ge(hrow_ready, 1)
            sp.dma_start(row_d.rearrange("(t p) r -> p t r", p=P), hrow.rearrange("p (t r) -> p t r", r=ROW)).then_inc(hrow_stored, 16)
            sp.wait_ge(m_ready, GAT.NT // HALF)
            sp.dma_start(w1.rearrange("p (c n) -> p c n", c=C), io["W1"].rearrange(chunked, p=P)).then_inc(ffn_in, 16)
            sp.dma_start(w2.rearrange("p (c n) -> p c n", c=NE * FC), io["W2"].rearrange(chunked, p=P)).then_inc(ffn_in, 16)
            sp.dma_start(b2_row[:], io["b2"].rearrange("e n -> (e n)").rearrange("(a n) -> a n", a=1)).then_inc(ffn_in, 16)
            x3 = xt3.rearrange("p (b c n) -> p b c n", b=2, c=C)
            sp.dma_start(x3[:, 0], xt_dv[:, :, 0:P]).then_inc(xt3_in[0], 16)
            sp.sem_inc(out_free, 1)
            with sp.Fori(0, NB // 2) as u:
                for k in range(2):
                    hold(sp, hid_psum, u * (2 * NE) + (k * NE + 1))
                    sp.dma_start(x3[:, 1 - k], xt_dv[:, :, bass.ds(u * (2 * P) + (k + 1) * P, P)]).then_inc(xt3_in[1 - k], 16)
                    hold(sp, y_taken, u * (2 * NE) + (k * NE + NE + 2))
                    sp.dma_start(io["out"][bass.ds(u * (2 * P) + k * P, P), :], outb).then_inc(out_stored, 16)
                    hold(sp, out_stored, u * 32 + (k + 1) * 16)
                    sp.sem_inc(out_free, 1)
            sp.wait_ge(y_taken, NB * NE + 2)
            sp.dma_start(io["out"][(NB - 1) * P:N, :], outb[0:TAIL, :]).then_inc(out_stored, 16)
            sp.wait_ge(out_stored, 16 * NB)

        @block.gpsimd
        def _(pool):
            gp = nc.gpsimd

            def iota(out, n):
                gp.iota(out, pattern=[[1, n]], base=0, channel_multiplier=0,
                        allow_small_or_imprecise_dtypes=True).then_inc(const_ready, 1)

            gp.memset(tg[:], 8191).then_inc(pads_set[CONV], 1)
            gp.memset(sr[:], 0).then_inc(pads_set[CONV], 1)
            gp.memset(x_sb[:, (NB - 1) * D:], 0.0).then_inc(x_pad, 1)
            iota(iota_t[:], NTM)
            iota(iota_p[:], P)
            iota(iota_b[:], 64)
            for ap, val in ((zero16, 0.0), (ones, 1.0), (ones16, 1.0), (headmask, 0.0)):
                gp.memset(ap[:], val).then_inc(const_ready, 1)
            pool.wait_ge(const_ready, 7)
            gp.affine_select(out=before[:], in_=ones[:], compare_op=ALU.is_gt, fill=0.0, base=0,
                             pattern=[[1, P]], channel_multiplier=-1).then_inc(const_ready, 1)
            gp.affine_select(out=ident[:], in_=ones[:], compare_op=ALU.is_equal, fill=0.0, base=0,
                             pattern=[[1, P]], channel_multiplier=-1).then_inc(const_ready, 1)
            pool.wait_ge(const_ready, 9)
            gp.tensor_copy(ident_b[:], ident[:]).then_inc(const_ready, 1)
            gp.tensor_scalar(ident_big[:], ident[:], BIG, None, ALU.mult).then_inc(const_ready, 1)
            for h in range(P // HEAD):
                pool.wait_ge(const_ready, 11 + h)
                gp.memset(headmask[h * HEAD:(h + 1) * HEAD, h * HEAD:(h + 1) * HEAD], 1.0).then_inc(const_ready, 1)

            pool.wait_ge(const_ready, 11 + P // HEAD)
            for g in (CONV, GAT):
                gp.memset(idx[g][:], 0).then_inc(const_ready, 1)
                gp.memset(dlo[g][:], -1.0).then_inc(const_ready, 1)

            def gather(g, table, width, dest, stage, staged, arrived):
                with pool.Fori(0, g.NT // G) as i:
                    for k in range(G):
                        if k % HALF == 0:
                            hold(pool, staged, i * 2 + (k // HALF + 1))
                        gp.indirect_dma_start(
                            out=dest[:, k * width:(k + 1) * width], out_offset=None, in_=table,
                            in_offset=bass.IndirectOffsetOnAxis(ap=stage[:, k:k + 1], axis=0),
                        ).then_inc(arrived[k], 16)

            pool.wait_ge(msg_stored, 16 * NB)
            gather(CONV, msg_d, D, rows, st_conv, conv_staged, row_in)
            pool.wait_ge(hrow_stored, 16)
            gather(GAT, row_d, ROW, rg, st_gat, gat_staged, gat_in)

        @block.vector
        def _(dve):
            V = nc.vector
            st = Steps(dve, dve_step)
            do = st.do

            def sort_prepare(g):
                s, T, NT = sorts[g], g.T, g.NT
                tg_, sr_, tmp_, bk_, oh_ = tg[:, 0:T], sr[:, 0:T], tmp[:, 0:T], bk[:, 0:T], oh[:, 0:T]
                cum_, pos_, slo_, shi_, hi_, lo_ = (a[:, 0:T] for a in (cum, pos, slo, shi, hi, lo))
                dve.wait_ge(edges_in[g], 64 if g.rest else 32)
                do(V.tensor_scalar(tmp_, tg_, 7, None, ALU.logical_shift_right))
                do(V.tensor_copy(bk_, tmp_))
                do(V.tensor_scalar(tg_, tg_, P - 1, None, ALU.bitwise_and))
                do(V.tensor_scalar(lo_, tg_, 1.0, 1 / 2048, ALU.add, ALU.mult))
                do(V.tensor_scalar(sr_, sr_, float(N - 1), None, ALU.min))
                do(V.tensor_scalar(tmp_, sr_, 7, None, ALU.bitwise_and))
                do(V.tensor_scalar(cum_, tmp_, 256 / 2048, None, ALU.mult))
                do(V.tensor_tensor(lo_, lo_, cum_, ALU.add))
                do(V.tensor_scalar(tmp_, sr_, 3, None, ALU.logical_shift_right))
                do(V.tensor_copy(hi_, tmp_))
                do(V.memset(pos_, 0.0))
                with dve.Fori(0, NB) as b:
                    st.enter(b, 1)
                    st.settle()
                    st.did(V.tensor_scalar(oh_, bk_, iota_b[:, bass.ds(b, 1)], 0.0, ALU.is_equal, ALU.add,
                                           accum_out=cnt[:, bass.ds(b, 1)]))
                st.leave(NB, 1)
                st.settle()
                V.tensor_copy(off[:], cnt[:]).then_inc(s["counted"], 1)
                dve.wait_ge(s["prefix"], 1)
                do(V.tensor_scalar(tot[:], ps[:, 6, 64:64 + NB], 127.0, None, ALU.add))
                do(V.tensor_scalar(tot[:], tot[:], 7, None, ALU.logical_shift_right))
                do(V.tensor_copy(til[:], tot[:]))
                do(V.tensor_tensor_scan(cumt[:], til[:], til[:], 0.0, ALU.add, ALU.max))
                do(V.tensor_tensor(base[:], cumt[:], til[:], ALU.subtract))
                V.scalar_tensor_tensor(off[:], base[:], float(P), ps[:, 6, 0:NB], ALU.mult, ALU.add
                                       ).then_inc(s["based"], 1)
                dve.wait_ge(s["based"], 1)
                with dve.Fori(0, NB) as b:
                    st.enter(b, 3)
                    st.settle()
                    do(V.tensor_scalar(oh_, bk_, iota_b[:, bass.ds(b, 1)], None, ALU.is_equal))
                    st.did(V.tensor_tensor_scan(cum_, oh_, oh_, off[:, bass.ds(b, 1)], ALU.add, ALU.max))
                    hold(dve, dve_step, st.value())
                    st.did(V.copy_predicated(pos_, oh_.bitcast(U16), cum_))
                st.leave(NB, 3)
                st.settle()
                do(V.tensor_scalar(tmp_, pos_, -1.0, None, ALU.add))
                do(V.tensor_scalar(tg_, tmp_, P - 1, None, ALU.bitwise_and))
                do(V.tensor_copy(slo_, tg_))
                do(V.tensor_scalar(tmp_, tmp_, 7, None, ALU.arith_shift_right))
                do(V.tensor_copy(shi_, tmp_))
                dve.wait_ge(s["basecol"], 1)
                do(V.tensor_copy(bcol[0:NB, :], ps[0:NB, 6, 128:129]))
                V.tensor_scalar(cmpb[0:NB, 0:NT], iota_t[0:NB, 0:NT], bcol[0:NB, :], None, ALU.is_ge
                                ).then_inc(s["compared"], 1)
                dve.wait_ge(s["blocks"], 1)
                for q, (a, w) in enumerate(g.chunks):
                    blk = ps[0:1, q, 0:w]
                    if g is CONV:
                        do(V.tensor_scalar(conv_at[:, a:a + w], blk, -1.0, float(D), ALU.add, ALU.mult))
                    else:
                        do(V.tensor_scalar(dm_at[:, a:a + w], blk, -1.0, float(2 * GH), ALU.add, ALU.mult))
                        do(V.tensor_scalar(sum_at[:, a:a + w], blk, float(PER_BANK), float(BANK - PER_BANK * ROW),
                                           ALU.is_gt, ALU.mult))
                        do(V.tensor_scalar(cum[0:1, 0:w], blk, -1.0, float(ROW), ALU.add, ALU.mult))
                        do(V.tensor_tensor(sum_at[:, a:a + w], sum_at[:, a:a + w], cum[0:1, 0:w], ALU.add))
                V.memset(signal_word[:], 0.0).then_inc(s["block_known"], 1)

            def sort_place(g):
                s = sorts[g]
                dve.wait_ge(s["block_known"], 1)
                with dve.Fori(0, g.T // 2) as i:
                    for k in range(2):
                        col = bass.ds(i * 2 + k, 1)
                        dve.wait_ge(s["placed"], i * 2 + (k + 1))
                        V.tensor_scalar(slot1h[k][:, 0:g.NT], iota_t[:, 0:g.NT], shi[:, col], None,
                                        ALU.is_equal).then_inc(s["onehots"], 1)
                        V.tensor_scalar(put_hi[k][:], iota_p[:], slo[:, col], hi[:, col], ALU.is_equal,
                                        ALU.mult).then_inc(s["onehots"], 1)
                        V.tensor_scalar(put_lo[k][:], iota_p[:], slo[:, col], lo[:, col], ALU.is_equal,
                                        ALU.mult).then_inc(s["onehots"], 1)
                dve.wait_ge(s["placed"], g.T + 3)
                for q, (a, w) in enumerate(g.chunks):
                    do(V.tensor_scalar(cum[:, a:a + w], ps[:, q, 0:w], 2048.0, None, ALU.mult))
                do(V.tensor_copy(idx[g][:, 0:g.NT], cum[:, 0:g.NT]))
                for a, w in g.chunks:
                    do(V.tensor_scalar(tmp[:, 0:w], idx[g][:, a:a + w], 255, None, ALU.bitwise_and))
                    do(V.tensor_scalar(dlo[g][:, a:a + w], tmp[:, 0:w], -1.0, None, ALU.add))
                V.tensor_scalar(idx[g][:, 0:g.NT], idx[g][:, 0:g.NT], 8, None, ALU.logical_shift_right
                                ).then_inc(s["sorted"], 1)

            def layernorm_stats(n):
                dve_s = stat[:].rearrange("p (t s) -> p t s", s=6)
                with dve.Fori(0, NB) as t:
                    st.enter(t, 1)
                    st.did(V.bn_stats(stat[:, bass.ds(t * 6, 6)], nodes(x_sb, t)))
                st.leave(NB, 1)
                st.settle()
                me, mo, ve, vo = dve_s[:, :, 1], dve_s[:, :, 4], dve_s[:, :, 2], dve_s[:, :, 5]
                do(V.tensor_tensor(st1[:], me, mo, ALU.add))
                do(V.tensor_scalar(mean[:], st1[:], 0.5, None, ALU.mult))
                do(V.tensor_tensor(st1[:], me, mo, ALU.subtract))
                do(V.tensor_scalar(st1[:], st1[:], 0.5, None, ALU.mult))
                do(V.tensor_tensor(st1[:], st1[:], st1[:], ALU.mult))
                do(V.tensor_tensor(st2[:], ve, vo, ALU.add))
                do(V.tensor_scalar(st2[:], st2[:], 1 / D, EPS, ALU.mult, ALU.add))
                V.tensor_tensor(var[:], st2[:], st1[:], ALU.add).then_inc(var_ready[n], 1)
                dve.wait_ge(std_ready[n], 1)
                do(V.reciprocal(rstd[:], st2[:]))

            def normalise(out, t):
                return V.tensor_scalar(out, nodes(x_sb, t), mean[:, bass.ds(t, 1)], rstd[:, bass.ds(t, 1)],
                                       ALU.subtract, ALU.mult)

            dve.wait_ge(const_ready, CONSTS)
            sort_prepare(CONV)

            dve.wait_ge(x_in, 32)
            layernorm_stats(0)
            normalise(xn, 0).then_inc(xn_ready, 1)

            def elu_parts(t, last=False):
                if not last:
                    dve.wait_ge(xt_psum, t + 1)
                    normalise(xn, t + 1).then_inc(xn_ready, 1)
                dve.wait_ge(kexp_ready, t + 1)
                do(V.tensor_scalar(kexp, kexp, 1.0, None, ALU.min))
                dve.wait_ge(ctx_used, t + 1)
                dve.wait_ge(v_ready, t + 1)
                V.scalar_tensor_tensor(kk, ps[:, 5, 0:D], 0.0, kexp, ALU.max, ALU.add).then_inc(k_ready, 1)
                dve.wait_ge(qexp_ready, t + 1)
                do(V.tensor_scalar(qexp, qexp, 1.0, None, ALU.min))
                dve.wait_ge(q_free, t + 1)
                V.scalar_tensor_tensor(qq, ps[:, 7, 0:D], 0.0, qexp, ALU.max, ALU.add).then_inc(q_ready, 1)

            with dve.Fori(0, NB - 1) as t:
                st.enter(t, 2)
                elu_parts(t)
            st.leave(NB - 1, 2)
            elu_parts(NB - 1, last=True)

            sort_place(CONV)

            dve.wait_ge(ctx_done, 1)
            for c in range(C):
                do(V.tensor_tensor(cbt[:, c * P:(c + 1) * P], ps[:, 6, c * P:(c + 1) * P], headmask[:], ALU.mult))
                do(V.tensor_scalar(ks[:, c * P:(c + 1) * P], headmask[:], ps[:, 6, 256 + c:257 + c], None, ALU.mult))
            V.memset(signal_word[:], 0.0).then_inc(ctx_masked, 1)
            dve.wait_ge(cp_psum, 1)
            V.tensor_copy(cpw[:, 0:D], ps[:, 3, 0:D]).then_inc(cp_ready, 1)
            V.tensor_copy(cpw[:, D:], ps[:, 7, 0:D]).then_inc(cp_ready, 1)
            dve.sem_inc(qn_ready, 1)
            with dve.Fori(0, NB) as t:
                st.enter(t, 2)
                dve.wait_ge(den_psum, t + 1)
                do(V.tensor_scalar(xn, ps[:, 5, 0:D], 1e-6, None, ALU.max))
                do(V.reciprocal(xn, xn))
                dve.wait_ge(q_back, t * 16 + 16)
                V.tensor_tensor(kk, qexp, xn, ALU.mult).then_inc(qn_ready, 1)
                dve.wait_ge(at_psum, t + 1)
                V.tensor_tensor(nodes(x_sb, t), nodes(x_sb, t), ps[:, 4, 0:D], ALU.add).then_inc(at_added, 1)
            st.leave(NB, 2)

            dve.sem_inc(conv_added, 2)
            with dve.Fori(0, CONV.NT // G) as i:
                ats = columns(DVE, conv_at, i * G, G, (NB - 1) * D)
                for k in range(G + 1):
                    if k < G:
                        dve.wait_ge(conv_psum, i * G + (k + 1))
                        V.tensor_scalar(oh1[k % 2], iota_p[:], dlo[CONV][:, bass.ds(i * G + k, 1)], None,
                                        ALU.is_equal).then_inc(conv_oh, 1)
                    if k:
                        j = k - 1
                        dst = acc[:, bass.ds(ats[j], D)]
                        dve.wait_ge(conv_psum, i * G + (j + 3))
                        dve.wait_ge(conv_added, i * G + (j + 2))
                        V.tensor_tensor(dst, dst, ps[:, 4 + j % 2, 0:D], ALU.add).then_inc(conv_added, 1)
            dve.wait_ge(conv_added, CONV.NT + 2)
            V.scalar_tensor_tensor(x_sb[:], acc, 0.0, x_sb[:], ALU.max, ALU.add).then_inc(x2_ready, 1)

            sort_prepare(GAT)
            sort_place(GAT)
            dve.wait_ge(x2_ready, 1)
            layernorm_stats(1)
            with dve.Fori(0, NB) as t:
                dve.wait_ge(xt2_psum, t + 1)
                normalise(xn2, t).then_inc(xn2_ready, 1)
            dve.wait_ge(h_psum, NB)
            hr = hrow.rearrange("p (t r) -> p t r", r=ROW)
            split = BANK // HW
            for q, (a, b) in enumerate(((0, split), (split, NB))):
                do(V.tensor_copy(hr[:, a:b, 0:HW], ps[:, q, 0:(b - a) * HW].rearrange("p (t r) -> p t r", r=HW)))
            dve.wait_ge(small_in, 16 * 6)
            tmp3 = ad_tmp.rearrange("p (t r) -> p t r", r=HW)
            tmp4 = ad_tmp.rearrange("p (t h c) -> p t h c", h=GH, c=GC)
            dm2 = dm.rearrange("p (t r) -> p t r", r=2 * GH)

            def param(k):
                return smalls[:, k * HW:(k + 1) * HW].rearrange("p (a r) -> p a r", a=1).broadcast_to((P, NB, HW))

            for k, dst in ((0, hr[:, :, HW:ROW]), (1, dm2[:, :, 0:GH])):
                do(V.tensor_tensor(tmp3, hr[:, :, 0:HW], param(k), ALU.mult))
                do(V.tensor_reduce(dst, tmp4, AX.X, ALU.add))
            V.tensor_copy(dm2[:, :, GH:], hr[:, :, HW:ROW]).then_inc(hrow_ready, 1)
            dve.wait_ge(hrow_ready, 1)

            dve.sem_inc(max_taken, 8)
            with dve.Fori(0, GAT.NT // G) as i:
                ats = columns(DVE, dm_at, i * G, G, dm_most)
                for k in range(G + 1):
                    if k < G:
                        dve.wait_ge(max_psum, i * G + (k + G - 3))
                        V.tensor_scalar(nohb[k % 4], iota_p[:], dlo[GAT][:, bass.ds(i * G + k, 1)], 1.0,
                                        ALU.is_equal, ALU.subtract).then_inc(gat_noh, 1)
                    if k:
                        j = k - 1
                        m4 = mx[:, (j % 4) * GH:(j % 4 + 1) * GH]
                        dst = dm[:, bass.ds(ats[j] + GH, GH)]
                        dve.wait_ge(max_psum, i * G + (j + 1 + G))
                        V.tensor_reduce(m4, ps[:, 4 + j % 4, :].rearrange("p (h e) -> p h e", h=GH), AX.X,
                                        ALU.max).then_inc(max_taken, 1)
                        dve.wait_ge(max_taken, i * (2 * G) + (2 * j + 9))
                        V.tensor_tensor(dst, dst, m4, ALU.max).then_inc(max_taken, 1)
            dve.wait_ge(max_taken, 2 * GAT.NT + 8)
            t4 = ad_tmp[:, 0:NB * GH].rearrange("p (t h) -> p t h", h=GH)
            do(V.tensor_tensor(t4, dm2[:, :, GH:], dm2[:, :, 0:GH], ALU.add))
            do(V.scalar_tensor_tensor(dm2[:, :, GH:], t4, 0.2, t4, ALU.mult, ALU.max))
            do(V.tensor_tensor(t4, hr[:, :, HW:ROW], dm2[:, :, 0:GH], ALU.add))
            do(V.scalar_tensor_tensor(t4, t4, 0.2, t4, ALU.mult, ALU.max))
            V.tensor_tensor(t4, t4, dm2[:, :, GH:], ALU.subtract).then_inc(dm_ready, 1)
            dve.wait_ge(self_e, 1)

            z3, e3 = (a.rearrange("p (j h) -> p j h", h=GH) for a in (zz, ee))
            mg = msg.rearrange("p (j r) -> p j r", r=ROW)
            mg4 = mg[:, :, 0:HW].rearrange("p j (h c) -> p j h c", h=GH)
            dmp = ps[:, 6, 0:HALF * 2 * GH].rearrange("p (j r) -> p j r", r=2 * GH)

            def onehots(par, first):
                for k in range(HALF):
                    V.tensor_scalar(ohf[par][:, k * P:(k + 1) * P], iota_p[:], dlo[GAT][:, bass.ds(first + k, 1)],
                                    None, ALU.is_equal).then_inc(oh_ready, 1)

            onehots(0, 0)
            with dve.Fori(0, GAT.NT // G) as i:
                st.enter(i, 6)
                for b in range(2):
                    dve.wait_ge(sum_done, i * 2 + (b + 1))
                    onehots(1 - b, i * G + (b + 1) * HALF)
                    row3 = rows_all[:, bass.ds(i * (G * ROW) + b * HALF * ROW, HALF * ROW)].rearrange(
                        "p (j r) -> p j r", r=ROW)
                    dve.wait_ge(dm_psum, i * 2 + (b + 1))
                    do(V.tensor_tensor(z3, row3[:, :, HW:ROW], dmp[:, :, 0:GH], ALU.add))
                    do(V.scalar_tensor_tensor(z3, z3, 0.2, z3, ALU.mult, ALU.max))
                    V.tensor_tensor(z3, z3, dmp[:, :, GH:], ALU.subtract).then_inc(z_ready, 1)
                    dve.wait_ge(ee_ready, i * 2 + (b + 1))
                    do(V.tensor_copy(mg[:, :, HW:ROW], e3))
                    V.tensor_tensor(mg4, row3[:, :, 0:HW].rearrange("p j (h c) -> p j h c", h=GH),
                                    e3.rearrange("p j (h a) -> p j h a", a=1).broadcast_to((P, HALF, GH, GC)),
                                    ALU.mult).then_inc(m_ready, 1)
            st.leave(GAT.NT // G, 6)

            dve.wait_ge(sum_done, GAT.NT // HALF + 1)
            es3, den3 = (a.rearrange("p (t h) -> p t h", h=GH) for a in (eself, den))

            def spread(ap):
                return ap.rearrange("p t (h a) -> p t h a", a=1).broadcast_to((P, NB, GH, GC))

            do(V.tensor_tensor(tmp4, hr[:, :, 0:HW].rearrange("p t (h c) -> p t h c", h=GH), spread(es3), ALU.mult))
            for q, (a, b) in enumerate(((0, PER_BANK), (PER_BANK, NB))):
                sums = ps[:, q, 0:(b - a) * ROW].rearrange("p (t r) -> p t r", r=ROW)
                do(V.tensor_tensor(tmp3[:, a:b], tmp3[:, a:b], sums[:, :, 0:HW], ALU.add))
                do(V.tensor_tensor(den3[:, a:b], es3[:, a:b], sums[:, :, HW:ROW], ALU.add))
            do(V.tensor_scalar(den, den, 1e-16, None, ALU.add))
            do(V.reciprocal(den, den))
            do(V.tensor_tensor(tmp4, tmp4, spread(den3), ALU.mult))
            do(V.tensor_tensor(tmp3, tmp3, param(2), ALU.add))

            def per_node(ap):
                return ap.rearrange("p (t a) -> p t a", a=1).broadcast_to((P, NB, HW))

            sq = hrow[:, 0:NB * HW]
            do(V.tensor_reduce(st1[:], tmp3, AX.X, ALU.add))
            do(V.tensor_scalar(st1[:], st1[:], 1 / HW, None, ALU.mult))
            do(V.tensor_tensor(tmp3, tmp3, per_node(st1[:]), ALU.subtract))
            do(V.tensor_tensor(sq, ad_tmp, ad_tmp, ALU.mult))
            do(V.tensor_reduce(st2[:], sq.rearrange("p (t r) -> p t r", r=HW), AX.X, ALU.add))
            V.tensor_scalar(st2[:], st2[:], 1 / HW, EPS, ALU.mult, ALU.add).then_inc(gvar, 1)
            dve.wait_ge(gstd, 1)
            do(V.reciprocal(st1[:], st1[:]))
            do(V.tensor_tensor(tmp3, tmp3, per_node(st1[:]), ALU.mult))
            do(V.tensor_tensor(tmp3, tmp3, param(3), ALU.mult))
            do(V.tensor_tensor(tmp3, tmp3, param(4), ALU.add))
            do(V.tensor_reduce(den3, ad_tmp.rearrange("p (t h c) -> p t c h", h=GH, c=GC), AX.X, ALU.add))
            do(V.tensor_scalar(den, den, 1 / GH, None, ALU.mult))
            do(V.tensor_reduce(st1[:], den3, AX.X, ALU.max))
            ex3 = es3
            do(V.tensor_tensor(ex3, den3, st1[:].rearrange("p (t a) -> p t a", a=1).broadcast_to((P, NB, GH)),
                               ALU.subtract))
            V.memset(signal_word[:], 0.0).then_inc(gate_z, 1)
            rank = hrow[:, 0:NB * NE].rearrange("p (t e) -> p t e", e=NE)
            do(V.memset(hrow[:, 0:NB * NE], 0.0))
            for e in range(NE):
                for j in range(NE):
                    if j != e:
                        do(V.tensor_tensor(st2[:], den3[:, :, j], den3[:, :, e], ALU.is_ge if j < e else ALU.is_gt))
                        do(V.tensor_tensor(rank[:, :, e], rank[:, :, e], st2[:], ALU.add))
            g3 = gate[:].rearrange("p (t e) -> p t e", e=NE)
            dve.wait_ge(gate_e, 1)
            do(V.scalar_tensor_tensor(g3, rank, 2.0, ex3, ALU.is_lt, ALU.mult))
            do(V.tensor_reduce(st1[:], g3, AX.X, ALU.add))
            do(V.reciprocal(st1[:], st1[:]))
            do(V.tensor_tensor(g3, g3, st1[:].rearrange("p (t a) -> p t a", a=1).broadcast_to((P, NB, NE)), ALU.mult))

            dve.sem_inc(y_taken, 2)
            with dve.Fori(0, NB) as t:
                hold(dve, out_free, t + 1)
                for e in range(NE):
                    dve.wait_ge(y_psum, t * NE + (e + 3))
                    if e:
                        dve.wait_ge(y_taken, t * NE + (e + 2))
                    V.scalar_tensor_tensor(outb, ps[:, 6 + e % 2, 0:D], gate[:, bass.ds(t * NE + e, 1)],
                                           outb if e else nodes(x_sb, t), ALU.mult, ALU.add).then_inc(y_taken, 1)

        @block.scalar
        def _(act):
            A = nc.scalar.activation

            def std(n):
                act.wait_ge(var_ready[n], 1)
                A(st2[:], var[:], ACT.Sqrt).then_inc(std_ready[n], 1)

            std(0)

            def take_xt(at_least):
                act.wait_ge(xt_psum, at_least)
                A(xnT, ps[:, 3, 0:D], ACT.Copy).then_inc(xt_ready, 1)

            take_xt(1)

            def take_block(t, last=False):
                act.wait_ge(kv_psum, t + 1)
                act.wait_ge(ctx_used, t + 1)
                A(kexp, ps[:, 5, 0:D], ACT.Exp).then_inc(kexp_ready, 1)
                A(vv, ps[:, 5, D:2 * D], ACT.Copy).then_inc(v_ready, 1)
                hold(act, w_psum, t + 1)
                A(nodes(acc, t), ps[:, 4, 0:D], ACT.Copy)
                act.wait_ge(msg_free, t + 1)
                A(msgb, ps[:, 4, D:2 * D], ACT.Copy).then_inc(msg_ready, 1)
                act.wait_ge(q_psum, t + 1)
                A(qexp, ps[:, 7, 0:D], ACT.Exp).then_inc(qexp_ready, 1)
                if not last:
                    take_xt(t + 2)

            with act.Fori(0, NB - 1) as t:
                take_block(t)
            take_block(NB - 1, last=True)

            act.wait_ge(at_added, NB)
            act.wait_ge(sorts[CONV]["sorted"], 1)

            def stage(st_, g, h, at, staged):
                A(st_[:, h * HALF:(h + 1) * HALF], idx[g][:, bass.ds(at, HALF)], ACT.Copy).then_inc(staged, 1)

            for h in range(2):
                stage(st_conv, CONV, h, h * HALF, conv_staged)
            with act.Fori(0, CONV.NT // G) as i:
                for h in range(2):
                    hold(act, conv_psum, i * G + ((h + 1) * HALF + 2))
                    stage(st_conv, CONV, h, i * G + (G + h * HALF), conv_staged)

            std(1)
            with act.Fori(0, NB) as t:
                act.wait_ge(xt2_psum, t + 2)
                act.wait_ge(xt2_free, t + 1)
                A(xnT2, ps[:, 3, 0:D], ACT.Copy).then_inc(xt2_ready, 1)
            act.wait_ge(hrow_ready, 1)
            for h in range(2):
                stage(st_gat, GAT, h, h * HALF, gat_staged)
            rg3 = rg.rearrange("p (j r) -> p j r", r=ROW)
            sb3 = sbf.rearrange("p (j h) -> p j h", h=GH)
            with act.Fori(0, GAT.NT // G) as i:
                for h in range(2):
                    for k in range(h * HALF, (h + 1) * HALF):
                        hold(act, gat_in[k], i * 16 + 16)
                    w = HALF * ROW
                    A(rows_all[:, bass.ds(i * (G * ROW) + h * w, w)], rg[:, h * w:(h + 1) * w], ACT.Copy)
                    act.wait_ge(max_psum, i * G + (h + 1) * HALF)
                    A(sb3[:, h * HALF:(h + 1) * HALF, :], rg3[:, h * HALF:(h + 1) * HALF, HW:ROW],
                      ACT.Copy).then_inc(gat_kept, 1)
                    stage(st_gat, GAT, h, i * G + (G + h * HALF), gat_staged)
            act.wait_ge(dm_ready, 1)
            A(eself, ad_tmp[:, 0:NB * GH], ACT.Exp).then_inc(self_e, 1)
            with act.Fori(0, GAT.NT // HALF) as b:
                act.wait_ge(ohT_psum, b + 1)
                A(ohT.rearrange("p (b n) -> p b n", b=2), ps[:, 4:6, :], ACT.Copy).then_inc(ohT_ready, 1)
                act.wait_ge(z_ready, b + 1)
                A(ee, zz, ACT.Exp).then_inc(ee_ready, 1)
            act.wait_ge(gvar, 1)
            A(st1[:], st2[:], ACT.Sqrt).then_inc(gstd, 1)
            act.wait_ge(gate_z, 1)
            A(eself, eself, ACT.Exp).then_inc(gate_e, 1)

            act.wait_ge(small_in, 16 * 6)
            with act.Fori(0, NB) as t:
                for e in range(NE):
                    act.wait_ge(hid_psum, t * NE + (e + 1))
                    act.wait_ge(y_psum, t * NE + (e + 1))
                    for c in range(FC):
                        ins = A(hT[:, (e % 2) * F + c * P:(e % 2) * F + (c + 1) * P],
                                ps[:, 4 + e % 2, c * P:(c + 1) * P], ACT.Gelu, bias=b1_col[:, e * FC + c:e * FC + c + 1])
                    ins.then_inc(hid_ready, 1)

        @block.tensor
        def _(pe):
            M = nc.tensor.matmul

            def transposed(src):
                for c in range(C):
                    ins = nc.tensor.transpose(ps[:, 3, c * P:(c + 1) * P], src[:, c * P:(c + 1) * P], ident[:])
                return ins

            def chunks(out, left, right):
                for c in range(C):
                    ins = M(out, left[c], right[c], start=(c == 0), stop=(c == C - 1))
                return ins

            def cut(ap, w):
                return [ap[:, c * w:(c + 1) * w] for c in range(C)]

            def sort_offsets(g):
                s = sorts[g]
                pe.wait_ge(s["counted"], 1)
                M(ps[:, 6, 0:NB], before[:], cnt[:], start=True, stop=True)
                M(ps[:, 6, 64:64 + NB], ones[:], cnt[:], start=True, stop=True).then_inc(s["prefix"], 1)
                pe.wait_ge(s["based"], 1)
                M(ps[0:NB, 6, 128:129], base[0:1, :], ones[0:1, 0:1], start=True, stop=True).then_inc(s["basecol"], 1)
                pe.wait_ge(s["compared"], 1)
                for q, (a, w) in enumerate(g.chunks):
                    ins = M(ps[0:1, q, 0:w], ones16[0:NB, 0:1], cmpb[0:NB, a:a + w], start=True, stop=True)
                ins.then_inc(s["blocks"], 1)

            def clear(bank, w, **kw):
                return M(ps[:, bank, 0:w], zero16[:], iota_t[:, 0:w], start=True, stop=False, skip_group_check=True)

            def sort_place(g):
                s = sorts[g]
                pe.wait_ge(s["block_known"], 1)
                pe.sem_inc(s["placed"], 2)
                for q, (a, w) in enumerate(g.chunks):
                    clear(q, w)
                with pe.Fori(0, g.T // 2) as i:
                    for k in range(2):
                        pe.wait_ge(s["onehots"], i * 6 + 3 * (k + 1))
                        for put in (put_hi[k], put_lo[k]):
                            for q, (a, w) in enumerate(g.chunks):
                                ins = M(ps[:, q, 0:w], put[:], slot1h[k][:, a:a + w], start=False, stop=False,
                                        skip_group_check=True)
                        ins.then_inc(s["placed"], 1)
                M(ps[:, 0, 0:1], zero16[:], iota_t[:, 0:1], start=False, stop=True,
                  skip_group_check=True).then_inc(s["placed"], 1)

            pe.wait_ge(const_ready, CONSTS)
            sort_offsets(CONV)

            pe.wait_ge(w_in, 16 * 6)
            pe.wait_ge(sorts[CONV]["block_known"], 1)
            M(ps[:, 6, :], zero16[:], iota_t[:, 0:BANK], start=True, stop=False, skip_group_check=True)
            pe.sem_inc(ctx_used, 1)
            pe.wait_ge(xn_ready, 1)
            transposed(xn).then_inc(xt_psum, 1)

            def project(t, rows_, last=False):
                pe.wait_ge(xt_ready, t + 1)
                chunks(ps[:, 5, :], cut(xnT, P), cut(w_kv, 512)).then_inc(kv_psum, 1)
                pe.wait_ge(msg_ready, t + 1)
                chunks(ps[:, 4, :], cut(xnT, P), cut(w_wk, 512)).then_inc(w_psum, 1)
                pe.wait_ge(q_ready, t + 1)
                for o in range(C):
                    ins = chunks(ps[:, 7, o * P:(o + 1) * P],
                                 [w_q[:, c * D + o * P:c * D + (o + 1) * P] for c in range(C)], cut(xnT, P))
                ins.then_inc(q_psum, 1)
                if not last:
                    pe.wait_ge(xn_ready, t + 2)
                    transposed(xn).then_inc(xt_psum, 1)
                pe.wait_ge(k_ready, t + 1)
                pe.wait_ge(v_ready, t + 1)
                for c in range(C):
                    one = slice(c * P, (c + 1) * P)
                    M(ps[:, 6, c * P:(c + 1) * P], vv[0:rows_, one], kk[0:rows_, one], start=False, stop=last,
                      skip_group_check=True)
                    ins = M(ps[:, 6, 256 + c:257 + c], kk[0:rows_, one], ones[0:rows_, 0:1], start=False, stop=last,
                            skip_group_check=True)
                ins.then_inc(ctx_used, 1)

            pe.sem_inc(msg_ready, 1)
            pe.sem_inc(q_ready, 1)
            with pe.Fori(0, NB - 1) as t:
                project(t, P)
            project(NB - 1, TAIL, last=True)
            pe.wait_ge(ctx_used, NB + 1)
            pe.sem_inc(ctx_done, 1)

            sort_place(CONV)

            pe.wait_ge(ctx_masked, 1)
            M(ps[:, 3, 0:D], cbt[:, 0:P], w_p[:, 0:D], start=True, stop=True)
            M(ps[:, 7, 0:D], cbt[:, P:2 * P], w_p[:, D:2 * D], start=True, stop=True).then_inc(cp_psum, 1)
            pe.wait_ge(cp_ready, 2)
            with pe.Fori(0, NB) as t:
                pe.wait_ge(q_back, t * 16 + 16)
                for c in range(C):
                    ins = M(ps[:, 5, c * P:(c + 1) * P], ks[:, c * P:(c + 1) * P], qexp[:, c * P:(c + 1) * P],
                            start=True, stop=True)
                ins.then_inc(den_psum, 1)
                pe.wait_ge(qn_ready, t + 2)
                for c in range(C):
                    M(ps[:, 4, 0:D], kk[:, c * P:(c + 1) * P], cpw[:, c * D:(c + 1) * D], start=(c == 0), stop=False)
                M(ps[:, 4, 0:D], ones[0:1, :], bp_row[:], start=False, stop=True).then_inc(at_psum, 1)

            pe.wait_ge(at_added, NB)
            pe.sem_inc(conv_psum, 2)
            with pe.Fori(0, CONV.NT // G) as i:
                for k in range(G):
                    pe.wait_ge(conv_oh, i * G + (k + 1))
                    pe.wait_ge(row_in[k], i * 16 + 16)
                    pe.wait_ge(conv_added, i * G + (k + 1))
                    M(ps[:, 4 + k % 2, 0:D], oh1[k % 2], rows[:, k * D:(k + 1) * D], start=True,
                      stop=True).then_inc(conv_psum, 1)

            sort_offsets(GAT)
            sort_place(GAT)
            flat = ps[:, 0:2, :].rearrange("p b n -> p (b n)")
            pe.wait_ge(wg_in, 16)
            pe.sem_inc(xt2_psum, 1)
            with pe.Fori(0, NB) as t:
                pe.wait_ge(xn2_ready, t + 1)
                transposed(xn2).then_inc(xt2_psum, 1)
                pe.wait_ge(xt2_ready, t + 1)
                out = flat[:, bass.ds(t * HW, HW)]
                chunks(out, cut(xnT2, P), cut(w_g, HW)).then_inc(h_psum, 1)
            pe.wait_ge(hrow_ready, 1)
            clear(0, BANK)
            clear(1, BANK)
            pe.sem_inc(max_psum, G)
            four = ident_big[:].rearrange("p (a n) -> p a n", a=1).broadcast_to((P, GH, P))
            with pe.Fori(0, GAT.NT // G) as i:
                for k in range(G):
                    bank = 4 + k % 4
                    pe.wait_ge(gat_noh, i * G + (k + 1))
                    pe.wait_ge(max_taken, i * (2 * G) + (2 * k + 1))
                    if k % HALF == 0:
                        pe.wait_ge(gat_kept, i * 2 + (k // HALF + 1))
                    M(ps[:, bank, :].rearrange("p (h n) -> p h n", h=GH), nohb[k % 4], four, start=True, stop=False)
                    for h in range(GH):
                        s1 = sbf[:, k * GH + h:k * GH + h + 1].broadcast_to((P, P))
                        ins = M(ps[:, bank, h * P:(h + 1) * P], s1, ident_b[:], start=False, stop=(h == GH - 1))
                    ins.then_inc(max_psum, 1)

            pe.wait_ge(self_e, 1)
            pe.sem_inc(sum_done, 1)

            def turn_onehots(b, par):
                pe.wait_ge(oh_ready, b * HALF + HALF)
                for k in range(HALF):
                    ins = nc.tensor.transpose(ps[:, 4 + k // 4, (k % 4) * P:(k % 4 + 1) * P],
                                              ohf[par][:, k * P:(k + 1) * P], ident[:])
                ins.then_inc(ohT_psum, 1)

            def fetch_targets(b):
                ats = columns(PE, dm_at, b * HALF, HALF, dm_most)
                pe.wait_ge(ohT_ready, b + 1)
                for k in range(HALF):
                    ins = M(ps[:, 6, k * 2 * GH:(k + 1) * 2 * GH], ohT[:, k * P:(k + 1) * P],
                            dm[:, bass.ds(ats[k], 2 * GH)], start=True, stop=True)
                ins.then_inc(dm_psum, 1)

            def sum_messages(b, par):
                ats = columns(PE, sum_at, b * HALF, HALF, sum_most)
                pe.wait_ge(m_ready, b + 1)
                for k in range(HALF):
                    ins = M(flat[:, bass.ds(ats[k], ROW)], ohf[par][:, k * P:(k + 1) * P],
                            msg[:, k * ROW:(k + 1) * ROW], start=False, stop=False, skip_group_check=True)
                ins.then_inc(sum_done, 1)

            halves = GAT.NT // HALF
            turn_onehots(0, 0)
            fetch_targets(0)
            with pe.Fori(0, halves // 2 - 1) as u:
                for k in range(2):
                    b = u * 2 + (k + 1)
                    turn_onehots(b, (k + 1) % 2)
                    sum_messages(u * 2 + k, k)
                    fetch_targets(b)
            turn_onehots(halves - 1, 1)
            sum_messages(halves - 2, 0)
            fetch_targets(halves - 1)
            sum_messages(halves - 1, 1)

            pe.wait_ge(ffn_in, 48)
            pe.sem_inc(y_psum, 2)
            x3 = xt3.rearrange("p (b c n) -> p b c n", b=2, c=C)

            def hidden(e, par):
                for f in range(FC):
                    at = e * F + f * P
                    ins = chunks(ps[:, 4 + e % 2, f * P:(f + 1) * P],
                                 [w1[:, c * NE * F + at:c * NE * F + at + P] for c in range(C)],
                                 [x3[:, par, c, :] for c in range(C)])
                ins.then_inc(hid_psum, 1)

            def outputs(e, n):
                pe.wait_ge(hid_ready, n + 1)
                pe.wait_ge(y_taken, n + 1)
                for f in range(FC):
                    M(ps[:, 6 + e % 2, 0:D], hT[:, (e % 2) * F + f * P:(e % 2) * F + (f + 1) * P],
                      w2[:, (e * FC + f) * D:(e * FC + f + 1) * D], start=(f == 0), stop=False)
                M(ps[:, 6 + e % 2, 0:D], ones[0:1, :], b2_row[:, e * D:(e + 1) * D], start=False,
                  stop=True).then_inc(y_psum, 1)

            pe.wait_ge(xt3_in[0], 16)
            hidden(0, 0)
            with pe.Fori(0, NB // 2) as u:
                for k in range(2):
                    for e in range(NE):
                        if e < NE - 1:
                            hidden(e + 1, k)
                        else:
                            if k == 0:
                                pe.wait_ge(xt3_in[1], u * 16 + 16)
                            else:
                                pe.wait_ge(xt3_in[0], u * 16 + 32)
                            hidden(0, 1 - k)
                        outputs(e, u * (2 * NE) + (k * NE + e))
            for e in range(NE):
                if e < NE - 1:
                    hidden(e + 1, 0)
                outputs(e, (NB - 1) * NE + e)


def kernel(x, src, dst, L0_gnn_w0, L0_gnn_w1, L0_mix_Wq, L0_mix_Wkv, L0_mix_Wproj, L0_mix_bproj, L0_ffn_W_gat,
           L0_ffn_att_src, L0_ffn_att_dst, L0_ffn_b_gat, L0_ffn_ln_gamma, L0_ffn_ln_beta, L0_ffn_W1, L0_ffn_b1,
           L0_ffn_W2, L0_ffn_b2, L0_ffn_edge_index):
    import numpy as np
    import concourse.bacc as bacc
    from concourse.bass_utils import run_bass_kernel_spmd as run

    c = np.ascontiguousarray
    ei = np.asarray(L0_ffn_edge_index)
    w1 = np.asarray(L0_ffn_W1)
    arrays = {
        "x": c(x), "conv_target": c(src), "conv_source": c(dst), "gat_source": c(ei[0]), "gat_target": c(ei[1]),
        "w0": c(L0_gnn_w0), "w1": c(L0_gnn_w1), "WqT": c(np.asarray(L0_mix_Wq).T), "WkvT": c(np.asarray(L0_mix_Wkv).T),
        "WprojT": c(np.asarray(L0_mix_Wproj).T), "bproj": c(L0_mix_bproj), "W_gat": c(L0_ffn_W_gat),
        "att_src": c(L0_ffn_att_src).reshape(-1), "att_dst": c(L0_ffn_att_dst).reshape(-1), "b_gat": c(L0_ffn_b_gat),
        "gamma": c(L0_ffn_ln_gamma), "beta": c(L0_ffn_ln_beta),
        "W1": c(w1.transpose(1, 0, 2).reshape(D, NE * F)), "b1T": c(np.asarray(L0_ffn_b1).reshape(NE * FC, P).T),
        "W2": c(L0_ffn_W2).reshape(NE * F, D), "b2": c(L0_ffn_b2),
    }
    nc = bacc.Bacc("TRN2", target_bir_lowering=False, num_devices=1)
    io = {}
    for name, a in arrays.items():
        io[name] = nc.dram_tensor(f"in_{name}", a.shape, mybir.dt.from_np(a.dtype), kind="ExternalInput").ap()
    io["out"] = nc.dram_tensor("out", (N, D), F32, kind="ExternalOutput").ap()
    io["edges"] = {CONV: (io["conv_target"], io["conv_source"]), GAT: (io["gat_target"], io["gat_source"])}
    layer(nc, io)
    r = run(nc, [{f"in_{k}": a for k, a in arrays.items()}], core_ids=[0])
    return r.results[0]["out"]
```

```python
from contextlib import ExitStack

import concourse.bass as bass
from concourse import mybir

F32, I32, I16, F16, BF16, U16 = (mybir.dt.float32, mybir.dt.int32, mybir.dt.int16, mybir.dt.float16,
                                 mybir.dt.bfloat16, mybir.dt.uint16)
DVE, PE = mybir.EngineType.DVE, mybir.EngineType.PE
ALU, ACT, AX = mybir.AluOpType, mybir.ActivationFunctionType, mybir.AxisListType

P = 128
BANK = 512
N, D = 6250, 256
NB = -(-N // P)
TAIL = N - (NB - 1) * P
NPAD = NB * P
C = D // P
HEAD = 32
EPS = 1e-5
NE, F = 4, 512
FC = F // P
GH, GC = 4, 4
HW = GH * GC
ROW = HW + GH
G = 16
BIG = 1e30
HALF = 8
RING = 4
PARTS = 3
OH_RING = 6
PER_BANK = 25


class Graph:

    def __init__(self, edges, turns):
        self.E = edges
        self.turns = turns
        self.per_turn = 2 * -(-edges // (2 * P * turns))
        self.T = self.per_turn * turns
        most = (edges + NB * (P - 1)) // P
        self.NT = -(-most // G) * G
        self.chunks = [(a, min(BANK, self.NT - a)) for a in range(0, self.NT, BANK)]
        self.full = edges // self.T
        self.rest = edges - self.full * self.T


CONSTS = 9 + 2 + P // HEAD + 4
CONV = Graph(100000, NB)
GAT = Graph(131072, CONV.NT // G)
HALVES = GAT.NT // HALF
PASS2_TURNS = (HALVES - 3 - 2) // OH_RING
TM, NTM = max(CONV.T, GAT.T), max(CONV.NT, GAT.NT)


class Carve:

    def __init__(self, tensor, words):
        self.tensor, self.words, self.at = tensor, words, 0

    def take(self, n, dtype=F32):
        words = n if dtype in (F32, I32) else -(-n // 2)
        a = self.at
        self.at += words
        assert self.at <= self.words, (self.at, self.words)
        ap = self.tensor[:, a:a + words]
        return ap if dtype is F32 else ap.bitcast(dtype)[:, 0:n]


class Steps:

    def __init__(self, eng, sem):
        self.eng, self.sem, self.base, self.k, self.turn = eng, sem, 0, 0, None

    def value(self):
        return self.base + self.k if self.turn is None else self.turn + (self.base + self.k)

    def did(self, ins):
        ins.then_inc(self.sem, 1)
        self.k += 1

    def settle(self):
        self.eng.wait_ge(self.sem, self.value())

    def do(self, ins):
        self.did(ins)
        self.settle()

    def note(self, ins):
        self.did(ins)
        return self.value()

    def after(self, value):
        self.eng.wait_ge(self.sem, value)

    def enter(self, i, per_turn):
        self.base, self.k, self.turn = self.base + self.k, 0, i * per_turn

    def leave(self, turns, per_turn):
        assert self.k == per_turn, (self.k, per_turn)
        self.base, self.k, self.turn = self.base + turns * per_turn, 0, None


def layer(nc, io):
    ctx = ExitStack()
    with ctx:
        sem_names = []

        def sem(name):
            sem_names.append(name)
            return ctx.enter_context(nc.semaphore(name))

        def sb(name, cols, dtype=F32, rows=P):
            return ctx.enter_context(nc.sbuf_tensor(name, [rows, cols], dtype))

        msg_d = nc.dram_tensor("messages", (NPAD, D), F32, kind="Internal").ap()
        q_d = nc.dram_tensor("q_t", (P, C * NPAD), F32, kind="Internal").ap()
        xt_d = nc.dram_tensor("x2n_t", (P, C * NPAD), F32, kind="Internal").ap()
        row_d = nc.dram_tensor("gat_rows", (NPAD, ROW), F32, kind="Internal").ap()
        q_dv = q_d.rearrange("p (c n) -> p c n", c=C)
        xt_dv = xt_d.rearrange("p (c n) -> p c n", c=C)

        x_sb = sb("x_sb", NB * D)
        sort_words = 3 * TM + TM // 2 + NTM + TM + (3 * (CONV.T + GAT.T)) // 2 + 2 * (CONV.T + GAT.T)
        arena_words = max(NB * D + sort_words, GAT.NT * ROW)
        arena_t = sb("arena", arena_words)
        arena = Carve(arena_t, arena_words)
        acc = arena.take(NB * D)
        tg, sr, tmp = (arena.take(TM, I32) for _ in range(3))
        oh = arena.take(TM, F16)
        cum = arena.take(NTM)
        pos = arena.take(TM)
        bk = {g: arena.take(g.T, F16) for g in (CONV, GAT)}
        slo = {g: arena.take(g.T, F16) for g in (CONV, GAT)}
        shi = {g: arena.take(g.T, F16) for g in (CONV, GAT)}
        hi = {g: arena.take(g.T) for g in (CONV, GAT)}
        lo = {g: arena.take(g.T) for g in (CONV, GAT)}
        rows_all = arena_t[:, 0:GAT.NT * ROW]
        ffn = Carve(arena_t, arena_words)
        w1 = ffn.take(C * NE * F)
        w2 = ffn.take(NE * FC * D)
        xt3 = ffn.take(2 * C * P)
        hT = ffn.take(2 * F)
        outb = ffn.take(D)
        b2_row = ffn.take(NE * D)[0:1, :]

        idx = {CONV: sb("conv_idx", CONV.NT + G, I32), GAT: sb("gat_idx", GAT.NT + G, I32)}
        dlo = {CONV: sb("conv_dlo", CONV.NT + G, F16), GAT: sb("gat_dlo", GAT.NT + G, F16)}
        conv_at = sb("conv_at", CONV.NT + 1, I16, 1)
        dm_at = sb("dm_at", GAT.NT, I16, 1)
        sum_at = sb("sum_at", GAT.NT, I16, 1)
        iota_t = sb("iota_t", NTM, F16)
        slot_words = RING * -(-NTM // 2)
        slot_t = sb("slot1h", slot_words)
        slots_ = Carve(slot_t, slot_words)
        slot1h = [slots_.take(NTM, F16) for _ in range(RING)]
        lo1h = [sb(f"lo1h{k}", P, F16) for k in range(RING)]
        put_hi = [sb(f"put_hi{k}", P, F16) for k in range(RING)]
        put_lo = [sb(f"put_lo{k}", P, F16) for k in range(RING)]
        iota_p = sb("iota_p", P, F16)
        iota_b = sb("iota_b", 64)
        zero16 = sb("zero16", P, F16)
        ident = sb("ident", P)
        ident_b = sb("ident_b", P, BF16)
        ident_big = sb("ident_big", P, BF16)
        ones = sb("ones", P)
        ones16 = sb("ones16", 1, F16)
        before = sb("before", P)
        headmask = sb("headmask", P)
        cnt, off, til, cumt, base, totf = (sb(n, NB) for n in ("cnt", "off", "til", "cumt", "base", "totf"))
        tot = sb("tot", NB, I32)
        bcol = sb("bcol", 1)
        cmpb = slot1h[0]
        signal_word = sb("signal_word", 1)
        stat = cum[:, 0:NB * 6]
        mean, var, rstd, st1, st2 = (sb(n, NB) for n in ("mean", "var", "rstd", "st1", "st2"))

        shared_words = 6416
        shared_t = sb("shared", shared_words)
        ph = Carve(shared_t, shared_words)
        xn, kk, qexp = (ph.take(D) for _ in range(3))
        ks = ph.take(C * P)
        cpw = ph.take(C * D)
        bp_row = ph.take(D)[0:1, :]
        cv = Carve(shared_t, shared_words)
        cv.at = ph.at
        w_wk = ph.take(C * 512)
        w_kv = ph.take(C * 512)
        w_q = ph.take(C * D)
        w_p = ph.take(C * D)
        xnT, kexp, vv, qq, msgb = (ph.take(D) for _ in range(5))
        cbt = ph.take(C * P)
        rows = cv.take(G * D)
        oh1 = [cv.take(P) for _ in range(RING)]
        st_conv = cv.take(G, I32)
        ga = Carve(shared_t, shared_words)
        hrow = ga.take(NB * ROW)
        ad_tmp = ga.take(NB * HW)
        dm = ga.take(NB * 2 * GH)
        st_gat = ga.take(G, I32)
        den = ga.take(NB * GH)
        eself = ga.take(NB * GH)
        gate = ga.take(NB * NE)
        g2 = Carve(shared_t, shared_words)
        g2.at = ga.at
        w_g = ga.take(C * HW)
        xn2, xnT2 = ([ga.take(D) for _ in range(2)] for _ in range(2))
        rg = ga.take(G * ROW)
        sbf = ga.take(G * GH, BF16)
        nohb = [ga.take(P, BF16) for _ in range(RING)]
        mx = ga.take(RING * GH)
        zz, ee = ([g2.take(HALF * GH) for _ in range(2)] for _ in range(2))
        msg = [g2.take(HALF * ROW) for _ in range(2)]
        past = Carve(arena_t, arena_words)
        past.at = GAT.NT * ROW
        over_slots = Carve(slot_t, slot_words)
        ohb = [past.take(HALF * P, BF16) for _ in range(OH_RING)]
        ohT = [over_slots.take(HALF * P, BF16) for _ in range(2)]
        dmb = g2.take(PARTS * NB * 2 * GH, BF16)
        dm_rest = g2.take(NB * 2 * GH)
        dsum = [g2.take(HALF * 2 * GH) for _ in range(2)]
        msgb3 = [g2.take(PARTS * HALF * ROW, BF16) for _ in range(2)]
        b1_col = sb("b1_col", NE * FC)
        smalls = sb("smalls", 5 * HW)

        ps = ctx.enter_context(nc.psum_tensor("ps", [P, 8, BANK], F32))

        ps_b = ps[:].bitcast(BF16)

        def nodes(ap, t, w=D):
            return ap[:, bass.ds(t * w, w)]

        const_ready = sem("const_ready")
        edges_in = {CONV: sem("conv_edges_in"), GAT: sem("gat_edges_in")}
        pads_set = {CONV: sem("conv_pads_set"), GAT: sem("gat_pads_set")}
        x_in, w_in, wg_in, ffn_in, small_in = (sem(n) for n in ("x_in", "w_in", "wg_in", "ffn_in", "small_in"))
        x_pad = sem("x_pad")
        dve_step, act_step, marks = sem("dve_step"), sem("act_step"), sem("marks")
        sorts = {}
        for g, nm in ((CONV, "conv"), (GAT, "gat")):
            sorts[g] = {k: sem(f"{nm}_{k}") for k in
                        ("unpacked", "counted", "prefix", "based", "basecol", "compared", "blocks",
                         "block_known", "onehots", "puts", "placed", "sorted")}
        var_ready, std_ready = [sem("var1"), sem("var2")], [sem("std1"), sem("std2")]
        xn_ready, xt_psum, xt_ready = sem("xn_ready"), sem("xt_psum"), sem("xt_ready")
        kv_psum, w_psum, q_psum = sem("kv_psum"), sem("w_psum"), sem("q_psum")
        kexp_ready, v_ready, k_ready, qexp_ready, q_ready = (sem(n) for n in (
            "kexp_ready", "v_ready", "k_ready", "qexp_ready", "q_ready"))
        msg_ready, msg_stored, msg_free, q_stored, q_free = (sem(n) for n in (
            "msg_ready", "msg_stored", "msg_free", "q_stored", "q_free"))
        ctx_used, ctx_done = sem("ctx_used"), sem("ctx_done")
        ctx_masked, cp_psum, cp_ready = sem("ctx_masked"), sem("cp_psum"), sem("cp_ready")
        q_back, den_psum, qn_ready, at_psum, at_added = (sem(n) for n in (
            "q_back", "den_psum", "qn_ready", "at_psum", "at_added"))
        conv_staged = sem("conv_staged")
        row_in = [sem(f"row_in{k}") for k in range(G)]
        conv_oh, conv_psum, conv_added = sem("conv_oh"), sem("conv_psum"), sem("conv_added")
        x2_ready = sem("x2_ready")
        xn2_ready, xt2_psum, xt2_ready, xt2_free, h_psum = (sem(n) for n in (
            "xn2_ready", "xt2_psum", "xt2_ready", "xt2_free", "h_psum"))
        xt2_stored = [sem("xt2_stored0"), sem("xt2_stored1")]
        hrow_ready, hrow_stored = sem("hrow_ready"), sem("hrow_stored")
        gat_staged, gat_in = sem("gat_staged"), [sem(f"gat_in{k}") for k in range(G)]
        gat_kept, gat_noh, max_psum, max_taken = (sem(n) for n in (
            "gat_kept", "gat_noh", "max_psum", "max_taken"))
        dm_ready = sem("dm_ready")
        oh_ready, ohT_psum, ohT_ready, dm_psum, z_ready, ee_ready, m_ready, sum_done = (sem(n) for n in (
            "oh_ready", "ohT_psum", "ohT_ready", "dm_psum", "z_ready", "ee_ready", "m_ready", "sum_done"))
        self_e, gate_z, gate_e, gvar, gstd, gates_ready = (sem(n) for n in (
            "self_e", "gate_z", "gate_e", "gvar", "gstd", "gates_ready"))
        xt3_in = [sem("xt3_in0"), sem("xt3_in1")]
        hid_psum, hid_ready, y_psum, y_taken, out_free, out_stored = (sem(n) for n in (
            "hid_psum", "hid_ready", "y_psum", "y_taken", "out_free", "out_stored"))

        block = ctx.enter_context(nc.Block())

        def hold(eng, s, value):
            eng.wait_ge(s, value)
            eng.sem_inc(marks, 1)

        def columns(engine, row, at, n, most):
            return nc.values_load_multi_w_load_instructions(
                row[0:1, bass.ds(at, n)], engines=[engine], min_val=0, max_val=most,
                skip_runtime_bounds_check_because="they are columns of blocks, below the last block by construction")[1]

        dm_most = (NB - 1) * 2 * GH
        sum_most = (NB - 1) * ROW + BANK - PER_BANK * ROW

        @block.sync
        def _(sp):
            def load_edges(g):
                t, s = io["edges"][g]
                for dst, src in ((tg, t), (sr, s)):
                    sp.dma_start(dst[0:g.full, 0:g.T],
                                 src[0:g.full * g.T].rearrange("(p t) -> p t", t=g.T)).then_inc(edges_in[g], 16)
                    if g.rest:
                        sp.dma_start(dst[g.full:g.full + 1, 0:g.rest],
                                     src[g.full * g.T:g.E].rearrange("(p t) -> p t", t=g.rest)
                                     ).then_inc(edges_in[g], 16)

            sp.wait_ge(pads_set[CONV], 2)
            load_edges(CONV)
            sp.wait_ge(x_pad, 1)
            sp.dma_start(x_sb[:, 0:(NB - 1) * D].rearrange("p (t f) -> p t f", f=D),
                         io["x"][0:(NB - 1) * P, :].rearrange("(t p) f -> p t f", p=P)).then_inc(x_in, 16)
            sp.dma_start(x_sb[0:TAIL, (NB - 1) * D:], io["x"][(NB - 1) * P:N, :]).then_inc(x_in, 16)
            chunked = "(c p) n -> p c n"
            wk = w_wk.rearrange("p (c n) -> p c n", c=C)
            sp.dma_start(wk[:, :, 0:D], io["w0"].rearrange(chunked, p=P)).then_inc(w_in, 16)
            sp.dma_start(wk[:, :, D:], io["w1"].rearrange(chunked, p=P)).then_inc(w_in, 16)
            for dst, src in ((w_kv, "WkvT"), (w_q, "WqT"), (w_p, "WprojT")):
                sp.dma_start(dst.rearrange("p (c n) -> p c n", c=C), io[src].rearrange(chunked, p=P)).then_inc(w_in, 16)
            sp.dma_start(bp_row[:], io["bproj"].rearrange("(a n) -> a n", a=1)).then_inc(w_in, 16)
            sp.dma_start(b1_col[:], io["b1T"]).then_inc(small_in, 16)
            for k, name in enumerate(("att_src", "att_dst", "b_gat", "gamma", "beta")):
                src = io[name].rearrange("(a n) -> a n", a=1).broadcast_to((P, HW))
                sp.dma_start(smalls[:, k * HW:(k + 1) * HW], src).then_inc(small_in, 16)

            sp.wait_ge(pads_set[GAT], 2)
            load_edges(GAT)
            sp.sem_inc(msg_free, 1)
            sp.sem_inc(q_free, 1)
            with sp.Fori(0, NB) as t:
                hold(sp, msg_ready, t + 2)
                sp.dma_start(msg_d[bass.ds(t * P, P), :], msgb).then_inc(msg_stored, 16)
                hold(sp, q_ready, t + 2)
                sp.dma_start(q_dv[:, :, bass.ds(t * P, P)], qq.rearrange("p (c n) -> p c n", c=C)).then_inc(q_stored, 16)
                hold(sp, msg_stored, t * 16 + 16)
                sp.sem_inc(msg_free, 1)
                hold(sp, q_stored, t * 16 + 16)
                sp.sem_inc(q_free, 1)
            with sp.Fori(0, NB) as t:
                hold(sp, qn_ready, t + 1)
                sp.dma_start(qexp.rearrange("p (c n) -> p c n", c=C), q_dv[:, :, bass.ds(t * P, P)]).then_inc(q_back, 16)
                hold(sp, q_back, t * 16 + 16)
            sp.wait_ge(x2_ready, 1)
            sp.dma_start(w_g.rearrange("p (c n) -> p c n", c=C), io["W_gat"].rearrange(chunked, p=P)).then_inc(wg_in, 16)
            sp.sem_inc(xt2_free, 2)

            def store_xt2(t, k, u):
                hold(sp, xt2_ready, t + 1)
                sp.dma_start(xt_dv[:, :, bass.ds(t * P, P)],
                             xnT2[k].rearrange("p (c n) -> p c n", c=C)).then_inc(xt2_stored[k], 16)

            with sp.Fori(0, NB // 2) as u:
                for k in range(2):
                    store_xt2(u * 2 + k, k, u)
                for k in range(2):
                    hold(sp, xt2_stored[k], u * 16 + 16)
                    sp.sem_inc(xt2_free, 1)
            store_xt2(NB - 1, 0, NB // 2)
            sp.wait_ge(xt2_stored[0], 16 * (NB // 2 + 1))
            sp.wait_ge(hrow_ready, 1)
            sp.dma_start(row_d.rearrange("(t p) r -> p t r", p=P), hrow.rearrange("p (t r) -> p t r", r=ROW)).then_inc(hrow_stored, 16)
            sp.wait_ge(m_ready, -(-ffn.at // (HALF * ROW)))
            sp.dma_start(w1.rearrange("p (c n) -> p c n", c=C), io["W1"].rearrange(chunked, p=P)).then_inc(ffn_in, 16)
            sp.dma_start(w2.rearrange("p (c n) -> p c n", c=NE * FC), io["W2"].rearrange(chunked, p=P)).then_inc(ffn_in, 16)
            sp.dma_start(b2_row[:], io["b2"].rearrange("e n -> (e n)").rearrange("(a n) -> a n", a=1)).then_inc(ffn_in, 16)
            x3 = xt3.rearrange("p (b c n) -> p b c n", b=2, c=C)
            sp.dma_start(x3[:, 0], xt_dv[:, :, 0:P]).then_inc(xt3_in[0], 16)
            sp.sem_inc(out_free, 1)
            with sp.Fori(0, NB // 2) as u:
                for k in range(2):
                    hold(sp, hid_psum, u * (2 * NE) + (k * NE + 1))
                    sp.dma_start(x3[:, 1 - k], xt_dv[:, :, bass.ds(u * (2 * P) + (k + 1) * P, P)]).then_inc(xt3_in[1 - k], 16)
                    hold(sp, y_taken, u * (2 * NE) + (k * NE + NE + 2))
                    sp.dma_start(io["out"][bass.ds(u * (2 * P) + k * P, P), :], outb).then_inc(out_stored, 16)
                    hold(sp, out_stored, u * 32 + (k + 1) * 16)
                    sp.sem_inc(out_free, 1)
            sp.wait_ge(y_taken, NB * NE + 2)
            sp.dma_start(io["out"][(NB - 1) * P:N, :], outb[0:TAIL, :]).then_inc(out_stored, 16)
            sp.wait_ge(out_stored, 16 * NB)

        @block.gpsimd
        def _(pool):
            gp = nc.gpsimd

            def iota(out, n):
                gp.iota(out, pattern=[[1, n]], base=0, channel_multiplier=0,
                        allow_small_or_imprecise_dtypes=True).then_inc(const_ready, 1)

            gp.memset(tg[:], 8191).then_inc(pads_set[CONV], 1)
            gp.memset(sr[:], 0).then_inc(pads_set[CONV], 1)
            gp.memset(x_sb[:, (NB - 1) * D:], 0.0).then_inc(x_pad, 1)
            iota(iota_t[:], NTM)
            iota(iota_p[:], P)
            iota(iota_b[:], 64)
            for ap, val in ((zero16, 0.0), (ones, 1.0), (ones16, 1.0), (headmask, 0.0)):
                gp.memset(ap[:], val).then_inc(const_ready, 1)
            pool.wait_ge(const_ready, 7)
            gp.affine_select(out=before[:], in_=ones[:], compare_op=ALU.is_gt, fill=0.0, base=0,
                             pattern=[[1, P]], channel_multiplier=-1).then_inc(const_ready, 1)
            gp.affine_select(out=ident[:], in_=ones[:], compare_op=ALU.is_equal, fill=0.0, base=0,
                             pattern=[[1, P]], channel_multiplier=-1).then_inc(const_ready, 1)
            pool.wait_ge(const_ready, 9)
            gp.tensor_copy(ident_b[:], ident[:]).then_inc(const_ready, 1)
            gp.tensor_scalar(ident_big[:], ident[:], BIG, None, ALU.mult).then_inc(const_ready, 1)
            for h in range(P // HEAD):
                pool.wait_ge(const_ready, 11 + h)
                gp.memset(headmask[h * HEAD:(h + 1) * HEAD, h * HEAD:(h + 1) * HEAD], 1.0).then_inc(const_ready, 1)

            pool.wait_ge(const_ready, 11 + P // HEAD)
            for g in (CONV, GAT):
                gp.memset(idx[g][:], 0).then_inc(const_ready, 1)
                gp.memset(dlo[g][:], -1.0).then_inc(const_ready, 1)

            def gather(g, table, width, dest, stage, staged, arrived):
                with pool.Fori(0, g.NT // G) as i:
                    for k in range(G):
                        if k % HALF == 0:
                            hold(pool, staged, i * 2 + (k // HALF + 1))
                        gp.indirect_dma_start(
                            out=dest[:, k * width:(k + 1) * width], out_offset=None, in_=table,
                            in_offset=bass.IndirectOffsetOnAxis(ap=stage[:, k:k + 1], axis=0),
                        ).then_inc(arrived[k], 16)

            pool.wait_ge(sorts[CONV]["unpacked"], 1)
            gp.memset(tg[:], 8191).then_inc(pads_set[GAT], 1)
            gp.memset(sr[:], 0).then_inc(pads_set[GAT], 1)
            pool.wait_ge(msg_stored, 16 * NB)
            gather(CONV, msg_d, D, rows, st_conv, conv_staged, row_in)
            pool.wait_ge(hrow_stored, 16)
            gather(GAT, row_d, ROW, rg, st_gat, gat_staged, gat_in)

        @block.vector
        def _(dve):
            V = nc.vector
            st = Steps(dve, dve_step)
            do = st.do

            def unpack_edges(g):
                s, T = sorts[g], g.T
                tg_, sr_, tmp_, cum_ = (a[:, 0:T] for a in (tg, sr, tmp, cum))
                dve.wait_ge(edges_in[g], 64 if g.rest else 32)
                do(V.tensor_scalar(tmp_, tg_, 7, None, ALU.logical_shift_right))
                do(V.tensor_copy(bk[g], tmp_))
                do(V.tensor_scalar(tg_, tg_, P - 1, None, ALU.bitwise_and))
                do(V.tensor_scalar(lo[g], tg_, 1.0, 1 / 2048, ALU.add, ALU.mult))
                do(V.tensor_scalar(sr_, sr_, float(N - 1), None, ALU.min))
                do(V.tensor_scalar(tmp_, sr_, 7, None, ALU.bitwise_and))
                do(V.tensor_scalar(cum_, tmp_, 256 / 2048, None, ALU.mult))
                do(V.tensor_tensor(lo[g], lo[g], cum_, ALU.add))
                do(V.tensor_scalar(tmp_, sr_, 3, None, ALU.logical_shift_right))
                V.tensor_copy(hi[g], tmp_).then_inc(s["unpacked"], 1)

            def count_block(g, b):
                st.did(V.tensor_scalar(oh[:, 0:g.T], bk[g], iota_b[:, bass.ds(b, 1)], 0.0, ALU.is_equal, ALU.add,
                                       accum_out=cnt[:, bass.ds(b, 1)]))

            def block_offsets(g):
                s = sorts[g]
                V.tensor_copy(off[:], cnt[:]).then_inc(s["counted"], 1)
                dve.wait_ge(s["prefix"], 1)
                do(V.tensor_scalar(tot[:], ps[:, 2, 64:64 + NB], 127.0, None, ALU.add))
                do(V.tensor_scalar(tot[:], tot[:], 7, None, ALU.logical_shift_right))
                do(V.tensor_copy(til[:], tot[:]))
                do(V.tensor_tensor_scan(cumt[:], til[:], til[:], 0.0, ALU.add, ALU.max))
                do(V.tensor_tensor(base[:], cumt[:], til[:], ALU.subtract))
                V.scalar_tensor_tensor(off[:], base[:], float(P), ps[:, 2, 0:NB], ALU.mult, ALU.add
                                       ).then_inc(s["based"], 1)
                dve.wait_ge(s["based"], 1)
                dve.wait_ge(s["basecol"], 1)
                do(V.tensor_copy(bcol[0:NB, :], ps[0:NB, 2, 128:129]))
                V.tensor_scalar(cmpb[0:NB, 0:g.NT], iota_t[0:NB, 0:g.NT], bcol[0:NB, :], None, ALU.is_ge
                                ).then_inc(s["compared"], 1)
                dve.wait_ge(s["blocks"], 1)
                for q, (a, w) in enumerate(g.chunks):
                    blk = ps[0:1, 3 + q, 0:w]
                    if g is CONV:
                        do(V.tensor_scalar(conv_at[:, a + 1:a + 1 + w], blk, -1.0, float(D), ALU.add, ALU.mult))
                    else:
                        do(V.tensor_scalar(dm_at[:, a:a + w], blk, -1.0, float(2 * GH), ALU.add, ALU.mult))
                        do(V.tensor_scalar(cum[0:1, 0:w], blk, float(PER_BANK), float(BANK - PER_BANK * ROW),
                                           ALU.is_gt, ALU.mult))
                        do(V.tensor_scalar(tmp[0:1, 0:w], blk, -1.0, float(ROW), ALU.add, ALU.mult))
                        do(V.tensor_tensor(sum_at[:, a:a + w], cum[0:1, 0:w], tmp[0:1, 0:w], ALU.add))
                if g is CONV:
                    do(V.memset(conv_at[:, 0:1], 0))
                V.memset(signal_word[:], 0.0).then_inc(s["block_known"], 1)
                do(V.memset(pos[:], 0.0))

            def slots_of_block(g, b):
                oh_, cum_, pos_ = oh[:, 0:g.T], cum[:, 0:g.T], pos[:, 0:g.T]
                st.did(V.tensor_scalar(oh_, bk[g], iota_b[:, bass.ds(b, 1)], None, ALU.is_equal))
                yield
                st.settle()
                st.did(V.tensor_tensor_scan(cum_, oh_, oh_, off[:, bass.ds(b, 1)], ALU.add, ALU.max))
                yield
                hold(dve, dve_step, st.value())
                st.did(V.copy_predicated(pos_, oh_.bitcast(U16), cum_))
                yield

            def split_slots(g):
                T = g.T
                st.settle()
                do(V.tensor_scalar(tmp[:, 0:T], pos[:, 0:T], -1.0, None, ALU.add))
                do(V.tensor_scalar(tg[:, 0:T], tmp[:, 0:T], P - 1, None, ALU.bitwise_and))
                do(V.tensor_copy(slo[g], tg[:, 0:T]))
                do(V.tensor_scalar(tmp[:, 0:T], tmp[:, 0:T], 7, None, ALU.arith_shift_right))
                do(V.tensor_copy(shi[g], tmp[:, 0:T]))

            def place_column(g, n, k):
                s = sorts[g]
                col = bass.ds(n + k, 1)
                dve.wait_ge(s["placed"], n + (k + 1))
                V.tensor_scalar(slot1h[k % RING][:, 0:g.NT], iota_t[:, 0:g.NT], shi[g][:, col], None,
                                ALU.is_equal).then_inc(s["onehots"], 1)
                V.tensor_scalar(lo1h[k % RING][:], iota_p[:], slo[g][:, col], None, ALU.is_equal
                                ).then_inc(s["onehots"], 1)

            def take_sorted(g):
                s = sorts[g]
                dve.wait_ge(s["placed"], g.T + RING + 1)
                for q, (a, w) in enumerate(g.chunks):
                    do(V.tensor_scalar(cum[:, a:a + w], ps[:, q, 0:w], 2048.0, None, ALU.mult))
                do(V.tensor_copy(idx[g][:, 0:g.NT], cum[:, 0:g.NT]))
                for a, w in g.chunks:
                    do(V.tensor_scalar(tmp[:, 0:w], idx[g][:, a:a + w], 255, None, ALU.bitwise_and))
                    do(V.tensor_scalar(dlo[g][:, a:a + w], tmp[:, 0:w], -1.0, None, ALU.add))
                V.tensor_scalar(idx[g][:, 0:g.NT], idx[g][:, 0:g.NT], 8, None, ALU.logical_shift_right
                                ).then_inc(s["sorted"], 1)

            def layernorm_stats(n):
                dve_s = stat.rearrange("p (t s) -> p t s", s=6)
                with dve.Fori(0, NB) as t:
                    st.enter(t, 1)
                    st.did(V.bn_stats(stat[:, bass.ds(t * 6, 6)], nodes(x_sb, t)))
                st.leave(NB, 1)
                st.settle()
                me, mo, ve, vo = dve_s[:, :, 1], dve_s[:, :, 4], dve_s[:, :, 2], dve_s[:, :, 5]
                do(V.tensor_tensor(st1[:], me, mo, ALU.add))
                do(V.tensor_scalar(mean[:], st1[:], 0.5, None, ALU.mult))
                do(V.tensor_tensor(st1[:], me, mo, ALU.subtract))
                do(V.tensor_scalar(st1[:], st1[:], 0.5, None, ALU.mult))
                do(V.tensor_tensor(st1[:], st1[:], st1[:], ALU.mult))
                do(V.tensor_tensor(st2[:], ve, vo, ALU.add))
                do(V.tensor_scalar(st2[:], st2[:], 1 / D, EPS, ALU.mult, ALU.add))
                V.tensor_tensor(var[:], st2[:], st1[:], ALU.add).then_inc(var_ready[n], 1)
                dve.wait_ge(std_ready[n], 1)
                do(V.reciprocal(rstd[:], st2[:]))

            def normalise(out, t):
                return V.tensor_scalar(out, nodes(x_sb, t), mean[:, bass.ds(t, 1)], rstd[:, bass.ds(t, 1)],
                                       ALU.subtract, ALU.mult)

            dve.wait_ge(const_ready, CONSTS)
            unpack_edges(CONV)
            with dve.Fori(0, NB) as b:
                st.enter(b, 1)
                st.settle()
                count_block(CONV, b)
            st.leave(NB, 1)
            st.settle()
            block_offsets(CONV)
            dve.wait_ge(x_in, 32)
            layernorm_stats(0)
            unpack_edges(GAT)
            dve.wait_ge(sorts[GAT]["unpacked"], 1)

            normalise(xn, 0).then_inc(xn_ready, 1)

            def elu_parts(t, last=False):
                if not last:
                    dve.wait_ge(xt_psum, t + 1)
                    normalise(xn, t + 1).then_inc(xn_ready, 1)
                for _ in slots_of_block(CONV, t):
                    pass
                st.settle()
                dve.wait_ge(kexp_ready, t + 1)
                do(V.tensor_scalar(kexp, kexp, 1.0, None, ALU.min))
                dve.wait_ge(ctx_used, t + 1)
                dve.wait_ge(v_ready, t + 1)
                V.scalar_tensor_tensor(kk, ps[:, 5, 0:D], 0.0, kexp, ALU.max, ALU.add).then_inc(k_ready, 1)
                count_block(GAT, t)
                dve.wait_ge(qexp_ready, t + 1)
                do(V.tensor_scalar(qexp, qexp, 1.0, None, ALU.min))
                dve.wait_ge(q_free, t + 1)
                V.scalar_tensor_tensor(qq, ps[:, 7, 0:D], 0.0, qexp, ALU.max, ALU.add).then_inc(q_ready, 1)

            with dve.Fori(0, NB - 1) as t:
                st.enter(t, 6)
                elu_parts(t)
            st.leave(NB - 1, 6)
            elu_parts(NB - 1, last=True)
            split_slots(CONV)
            block_offsets(GAT)

            dve.wait_ge(ctx_done, 1)
            for c in range(C):
                do(V.tensor_tensor(cbt[:, c * P:(c + 1) * P], ps[:, 6, c * P:(c + 1) * P], headmask[:], ALU.mult))
                do(V.tensor_scalar(ks[:, c * P:(c + 1) * P], headmask[:], ps[:, 6, 256 + c:257 + c], None, ALU.mult))
            V.memset(signal_word[:], 0.0).then_inc(ctx_masked, 1)
            dve.wait_ge(cp_psum, 1)
            V.tensor_copy(cpw[:, 0:D], ps[:, 3, 0:D]).then_inc(cp_ready, 1)
            V.tensor_copy(cpw[:, D:], ps[:, 7, 0:D]).then_inc(cp_ready, 1)
            dve.sem_inc(qn_ready, 1)

            with dve.Fori(0, NB) as t:
                st.enter(t, 3)
                slots = slots_of_block(GAT, t)
                for k in range(CONV.per_turn):
                    place_column(CONV, t * CONV.per_turn, k)
                    if k in (1, 6, 11):
                        next(slots)
            st.leave(NB, 3)
            take_sorted(CONV)
            split_slots(GAT)

            dve.wait_ge(msg_stored, 16 * NB)
            dve.wait_ge(q_stored, 16 * NB)
            dve.sem_inc(conv_added, RING - 1)
            dve.sem_inc(at_added, 1)

            def conv_onehot(i, k):
                dve.wait_ge(conv_psum, i * G + (k + 1))
                V.tensor_scalar(oh1[k % RING], iota_p[:], dlo[CONV][:, bass.ds(i * G + k, 1)], None,
                                ALU.is_equal).then_inc(conv_oh, 1)

            def conv_add(i, k, at):
                dst = acc[:, bass.ds(at, D)]
                dve.wait_ge(conv_psum, i * G + (k + 1 + RING))
                dve.wait_ge(conv_added, i * G + (k + RING))
                V.tensor_tensor(dst, dst, ps[:, 4 + k % RING, 0:D], ALU.add).then_inc(conv_added, 1)

            def conv_turn(i, attention):
                ats = columns(DVE, conv_at, i * G, G, (NB - 1) * D)
                sorted_ = 0
                for k in range(G):
                    conv_onehot(i, k + 2)
                    while sorted_ < GAT.per_turn * (k + 1) // G:
                        place_column(GAT, i * GAT.per_turn, sorted_)
                        sorted_ += 1
                    conv_add(i, k - 1, ats[k])
                    if attention and k == 6:
                        dve.wait_ge(den_psum, i + 1)
                        do(V.tensor_scalar(xn, ps[:, 3, 0:D], 1e-6, None, ALU.max))
                        do(V.reciprocal(xn, xn))
                        dve.wait_ge(q_back, i * 16 + 16)
                        V.tensor_tensor(kk, qexp, xn, ALU.mult).then_inc(qn_ready, 1)
                    if attention and k == 14:
                        dve.wait_ge(at_psum, i + 1)
                        V.tensor_tensor(nodes(x_sb, i), nodes(x_sb, i), ps[:, 3, 0:D], ALU.add).then_inc(at_added, 1)

            conv_onehot(0, 0)
            conv_onehot(0, 1)
            with dve.Fori(0, NB) as i:
                st.enter(i, 2)
                conv_turn(i, True)
            st.leave(NB, 2)
            with dve.Fori(NB, GAT.turns) as i:
                conv_turn(i, False)
            last_at = columns(DVE, conv_at, CONV.NT, 1, (NB - 1) * D)
            conv_add(0, CONV.NT - 1, last_at[0])
            dve.wait_ge(conv_added, CONV.NT + RING)
            dve.wait_ge(at_added, NB + 1)
            V.scalar_tensor_tensor(x_sb[:], acc, 0.0, x_sb[:], ALU.max, ALU.add).then_inc(x2_ready, 1)

            take_sorted(GAT)
            dve.wait_ge(x2_ready, 1)
            layernorm_stats(1)

            def normalise_x2(t, k):
                dve.wait_ge(xt2_psum, t + 1)
                normalise(xn2[k], t).then_inc(xn2_ready, 1)

            with dve.Fori(0, NB // 2) as u:
                for k in range(2):
                    normalise_x2(u * 2 + k, k)
            normalise_x2(NB - 1, 0)
            dve.wait_ge(h_psum, NB + 2)
            hr = hrow.rearrange("p (t r) -> p t r", r=ROW)
            split = BANK // HW
            for q, (a, b) in enumerate(((0, split), (split, NB))):
                do(V.tensor_copy(hr[:, a:b, 0:HW], ps[:, q, 0:(b - a) * HW].rearrange("p (t r) -> p t r", r=HW)))
            dve.wait_ge(small_in, 16 * 6)
            tmp3 = ad_tmp.rearrange("p (t r) -> p t r", r=HW)
            tmp4 = ad_tmp.rearrange("p (t h c) -> p t h c", h=GH, c=GC)
            dm2 = dm.rearrange("p (t r) -> p t r", r=2 * GH)

            def param(k):
                return smalls[:, k * HW:(k + 1) * HW].rearrange("p (a r) -> p a r", a=1).broadcast_to((P, NB, HW))

            for k, dst in ((0, hr[:, :, HW:ROW]), (1, dm2[:, :, 0:GH])):
                do(V.tensor_tensor(tmp3, hr[:, :, 0:HW], param(k), ALU.mult))
                do(V.tensor_reduce(dst, tmp4, AX.X, ALU.add))
            V.tensor_copy(dm2[:, :, GH:], hr[:, :, HW:ROW]).then_inc(hrow_ready, 1)
            dve.wait_ge(hrow_ready, 1)

            dve.sem_inc(max_taken, 2 * RING)

            def not_target(at, k):
                V.tensor_scalar(nohb[k % RING], iota_p[:], dlo[GAT][:, bass.ds(at, 1)], 1.0,
                                ALU.is_equal, ALU.subtract).then_inc(gat_noh, 1)

            for k in range(RING):
                not_target(k, k)
            with dve.Fori(0, GAT.NT // G) as i:
                ats = columns(DVE, dm_at, i * G, G, dm_most)
                for k in range(G):
                    m4 = mx[:, (k % RING) * GH:(k % RING + 1) * GH]
                    dst = dm[:, bass.ds(ats[k] + GH, GH)]
                    dve.wait_ge(max_psum, i * G + (k + 1 + G))
                    V.tensor_reduce(m4, ps[:, 4 + k % RING, :].rearrange("p (h e) -> p h e", h=GH), AX.X,
                                    ALU.max).then_inc(max_taken, 1)
                    not_target(i * G + (k + RING), k)
                    dve.wait_ge(max_taken, i * (2 * G) + (2 * k + 1 + 2 * RING))
                    V.tensor_tensor(dst, dst, m4, ALU.max).then_inc(max_taken, 1)
            dve.wait_ge(max_taken, 2 * GAT.NT + 2 * RING)
            t4 = ad_tmp[:, 0:NB * GH].rearrange("p (t h) -> p t h", h=GH)
            do(V.tensor_tensor(t4, dm2[:, :, GH:], dm2[:, :, 0:GH], ALU.add))
            do(V.scalar_tensor_tensor(dm2[:, :, GH:], t4, 0.2, t4, ALU.mult, ALU.max))
            do(V.tensor_tensor(t4, hr[:, :, HW:ROW], dm2[:, :, 0:GH], ALU.add))
            do(V.scalar_tensor_tensor(t4, t4, 0.2, t4, ALU.mult, ALU.max))
            do(V.tensor_tensor(t4, t4, dm2[:, :, GH:], ALU.subtract))
            w = NB * 2 * GH
            rest = dm_rest
            do(V.tensor_copy(dmb[:, 0:w], dm))
            do(V.tensor_tensor(rest, dm, dmb[:, 0:w], ALU.subtract))
            do(V.tensor_copy(dmb[:, w:2 * w], rest))
            V.tensor_tensor(dmb[:, 2 * w:], rest, dmb[:, w:2 * w], ALU.subtract).then_inc(dm_ready, 1)
            dve.wait_ge(self_e, 1)

            z3, e3 = ([a.rearrange("p (j h) -> p j h", h=GH) for a in b] for b in (zz, ee))
            mg = [a.rearrange("p (j r) -> p j r", r=ROW) for a in msg]
            dmp = [ps[:, 6 + k, 0:HALF * PARTS * 2 * GH].rearrange("p (j q r) -> p j r q", q=PARTS, r=2 * GH)
                   for k in range(2)]
            ds3 = [a.rearrange("p (j r) -> p j r", r=2 * GH) for a in dsum]
            part = [[a[:, q * HALF * ROW:(q + 1) * HALF * ROW] for q in range(PARTS)] for a in msgb3]

            def onehots(b, at, ks):
                for k in ks:
                    ins = V.tensor_scalar(ohb[at % OH_RING][:, k * P:(k + 1) * P], iota_p[:],
                                          dlo[GAT][:, bass.ds(b * HALF + k, 1)], None, ALU.is_equal)
                if HALF - 1 in ks:
                    ins.then_inc(oh_ready, 1)

            def rows_of(b):
                return rows_all[:, bass.ds(b * (HALF * ROW), HALF * ROW)].rearrange("p (j r) -> p j r", r=ROW)

            def exponents(b, at):
                z, d = z3[at % 2], ds3[at % 2]
                dve.wait_ge(dm_psum, b + 1)
                v = st.note(V.tensor_reduce(d, dmp[at % 2], AX.X, ALU.add))
                yield
                st.after(v)
                v = st.note(V.tensor_tensor(z, rows_of(b)[:, :, HW:ROW], d[:, :, 0:GH], ALU.add))
                yield
                st.after(v)
                v = st.note(V.scalar_tensor_tensor(z, z, 0.2, z, ALU.mult, ALU.max))
                yield
                st.after(v)
                V.tensor_tensor(z, z, d[:, :, GH:], ALU.subtract).then_inc(z_ready, 1)
                yield

            def messages(b, at):
                e, m, (hi_, mid_, lo_) = e3[at % 2], mg[at % 2], part[at % 2]
                flat_m = msg[at % 2]
                dve.wait_ge(ee_ready, b + 1)
                V.tensor_copy(m[:, :, HW:ROW], e)
                v = st.note(V.tensor_tensor(m[:, :, 0:HW].rearrange("p j (h c) -> p j h c", h=GH),
                                            rows_of(b)[:, :, 0:HW].rearrange("p j (h c) -> p j h c", h=GH),
                                            e.rearrange("p j (h a) -> p j h a", a=1).broadcast_to((P, HALF, GH, GC)),
                                            ALU.mult))
                yield
                st.after(v)
                v = st.note(V.tensor_copy(hi_, flat_m))
                yield
                st.after(v)
                v = st.note(V.tensor_tensor(flat_m, flat_m, hi_, ALU.subtract))
                yield
                st.after(v)
                v = st.note(V.tensor_copy(mid_, flat_m))
                yield
                st.after(v)
                V.tensor_tensor(lo_, flat_m, mid_, ALU.subtract).then_inc(m_ready, 1)
                yield

            def pass2_step(b, at, first=False, last=False):
                z_steps = exponents(b, at)
                next(z_steps)
                dve.wait_ge(sum_done, b + 1)
                m_steps = messages(b - 1, at - 1) if not first else iter(())
                for _ in range(3):
                    next(m_steps, None)
                    next(z_steps)
                next(m_steps, None)
                more = not last or at + 3 < HALVES
                if more:
                    onehots(b + 3, at + 3, range(HALF // 2))
                next(m_steps, None)
                if more:
                    onehots(b + 3, at + 3, range(HALF // 2, HALF))

            for b in range(3):
                onehots(b, b, range(HALF))
            for b in range(2):
                pass2_step(b, b, first=(b == 0))
            with dve.Fori(0, PASS2_TURNS) as u:
                st.enter(u, 7 * OH_RING)
                for k in range(OH_RING):
                    pass2_step(u * OH_RING + (k + 2), k + 2)
            st.leave(PASS2_TURNS, 7 * OH_RING)
            for b in range(2 + PASS2_TURNS * OH_RING, HALVES):
                pass2_step(b, b, last=True)
            dve.wait_ge(sum_done, HALVES + 1)
            for _ in messages(HALVES - 1, HALVES - 1):
                pass

            dve.wait_ge(sum_done, HALVES + 3)
            es3, den3 = (a.rearrange("p (t h) -> p t h", h=GH) for a in (eself, den))

            def spread(ap):
                return ap.rearrange("p t (h a) -> p t h a", a=1).broadcast_to((P, NB, GH, GC))

            do(V.tensor_tensor(tmp4, hr[:, :, 0:HW].rearrange("p t (h c) -> p t h c", h=GH), spread(es3), ALU.mult))
            for q, (a, b) in enumerate(((0, PER_BANK), (PER_BANK, NB))):
                sums = ps[:, q, 0:(b - a) * ROW].rearrange("p (t r) -> p t r", r=ROW)
                do(V.tensor_tensor(tmp3[:, a:b], tmp3[:, a:b], sums[:, :, 0:HW], ALU.add))
                do(V.tensor_tensor(den3[:, a:b], es3[:, a:b], sums[:, :, HW:ROW], ALU.add))
            do(V.tensor_scalar(den, den, 1e-16, None, ALU.add))
            do(V.reciprocal(den, den))
            do(V.tensor_tensor(tmp4, tmp4, spread(den3), ALU.mult))
            do(V.tensor_tensor(tmp3, tmp3, param(2), ALU.add))

            def per_node(ap):
                return ap.rearrange("p (t a) -> p t a", a=1).broadcast_to((P, NB, HW))

            sq = hrow[:, 0:NB * HW]
            do(V.tensor_reduce(st1[:], tmp3, AX.X, ALU.add))
            do(V.tensor_scalar(st1[:], st1[:], 1 / HW, None, ALU.mult))
            do(V.tensor_tensor(tmp3, tmp3, per_node(st1[:]), ALU.subtract))
            do(V.tensor_tensor(sq, ad_tmp, ad_tmp, ALU.mult))
            do(V.tensor_reduce(st2[:], sq.rearrange("p (t r) -> p t r", r=HW), AX.X, ALU.add))
            V.tensor_scalar(st2[:], st2[:], 1 / HW, EPS, ALU.mult, ALU.add).then_inc(gvar, 1)
            dve.wait_ge(gstd, 1)
            do(V.reciprocal(st1[:], st1[:]))
            do(V.tensor_tensor(tmp3, tmp3, per_node(st1[:]), ALU.mult))
            do(V.tensor_tensor(tmp3, tmp3, param(3), ALU.mult))
            do(V.tensor_tensor(tmp3, tmp3, param(4), ALU.add))
            do(V.tensor_reduce(den3, ad_tmp.rearrange("p (t h c) -> p t c h", h=GH, c=GC), AX.X, ALU.add))
            do(V.tensor_scalar(den, den, 1 / GH, None, ALU.mult))
            do(V.tensor_reduce(st1[:], den3, AX.X, ALU.max))
            ex3 = es3
            do(V.tensor_tensor(ex3, den3, st1[:].rearrange("p (t a) -> p t a", a=1).broadcast_to((P, NB, GH)),
                               ALU.subtract))
            V.memset(signal_word[:], 0.0).then_inc(gate_z, 1)
            rank = hrow[:, 0:NB * NE].rearrange("p (t e) -> p t e", e=NE)
            do(V.memset(hrow[:, 0:NB * NE], 0.0))
            for e in range(NE):
                for j in range(NE):
                    if j != e:
                        do(V.tensor_tensor(st2[:], den3[:, :, j], den3[:, :, e], ALU.is_ge if j < e else ALU.is_gt))
                        do(V.tensor_tensor(rank[:, :, e], rank[:, :, e], st2[:], ALU.add))
            g3 = gate.rearrange("p (t e) -> p t e", e=NE)
            dve.wait_ge(gate_e, 1)
            do(V.scalar_tensor_tensor(g3, rank, 2.0, ex3, ALU.is_lt, ALU.mult))
            do(V.tensor_reduce(st1[:], g3, AX.X, ALU.add))
            do(V.reciprocal(st1[:], st1[:]))
            do(V.tensor_tensor(g3, g3, st1[:].rearrange("p (t a) -> p t a", a=1).broadcast_to((P, NB, NE)), ALU.mult))

            dve.sem_inc(y_taken, 2)
            with dve.Fori(0, NB) as t:
                hold(dve, out_free, t + 1)
                for e in range(NE):
                    dve.wait_ge(y_psum, t * NE + (e + 3))
                    if e:
                        dve.wait_ge(y_taken, t * NE + (e + 2))
                    V.scalar_tensor_tensor(outb, ps[:, 6 + e % 2, 0:D], gate[:, bass.ds(t * NE + e, 1)],
                                           outb if e else nodes(x_sb, t), ALU.mult, ALU.add).then_inc(y_taken, 1)

        @block.scalar
        def _(act):
            A = nc.scalar.activation

            def std(n):
                act.wait_ge(var_ready[n], 1)
                A(st2[:], var[:], ACT.Sqrt).then_inc(std_ready[n], 1)

            std(0)

            def take_xt(at_least):
                act.wait_ge(xt_psum, at_least)
                A(xnT, ps[:, 3, 0:D], ACT.Copy).then_inc(xt_ready, 1)

            take_xt(1)

            def take_block(t, last=False):
                act.wait_ge(kv_psum, t + 1)
                act.wait_ge(ctx_used, t + 1)
                A(kexp, ps[:, 5, 0:D], ACT.Exp).then_inc(kexp_ready, 1)
                A(vv, ps[:, 5, D:2 * D], ACT.Copy).then_inc(v_ready, 1)
                hold(act, w_psum, t + 1)
                A(nodes(acc, t), ps[:, 4, 0:D], ACT.Copy)
                act.wait_ge(msg_free, t + 1)
                A(msgb, ps[:, 4, D:2 * D], ACT.Copy).then_inc(msg_ready, 1)
                act.wait_ge(q_psum, t + 1)
                A(qexp, ps[:, 7, 0:D], ACT.Exp).then_inc(qexp_ready, 1)
                if not last:
                    take_xt(t + 2)

            with act.Fori(0, NB - 1) as t:
                take_block(t)
            take_block(NB - 1, last=True)

            def scale_column(g, n, k):
                s = sorts[g]
                col = bass.ds(n + k, 1)
                hold(act, s["onehots"], n * 2 + 2 * (k + 1))
                A(put_hi[k % RING][:], lo1h[k % RING][:], ACT.Copy, scale=hi[g][:, col])
                A(put_lo[k % RING][:], lo1h[k % RING][:], ACT.Copy, scale=lo[g][:, col]).then_inc(s["puts"], 1)

            with act.Fori(0, NB) as t:
                for k in range(CONV.per_turn):
                    scale_column(CONV, t * CONV.per_turn, k)

            act.wait_ge(cp_ready, 2)
            act.wait_ge(q_stored, 16 * NB)
            act.wait_ge(sorts[CONV]["sorted"], 1)

            def stage(st_, g, h, at, staged):
                A(st_[:, h * HALF:(h + 1) * HALF], idx[g][:, bass.ds(at, HALF)], ACT.Copy).then_inc(staged, 1)

            for h in range(2):
                stage(st_conv, CONV, h, h * HALF, conv_staged)
            with act.Fori(0, GAT.turns) as i:
                for k in range(GAT.per_turn):
                    scale_column(GAT, i * GAT.per_turn, k)
                    for h in range(2):
                        if k == (h + 1) * GAT.per_turn // 2 - 1:
                            hold(act, conv_psum, i * G + ((h + 1) * HALF + RING))
                            stage(st_conv, CONV, h, i * G + (G + h * HALF), conv_staged)

            std(1)

            def take_xt2(t, k):
                act.wait_ge(xt2_psum, t + 3)
                act.wait_ge(xt2_free, t + 1)
                act.wait_ge(h_psum, t + 1)
                A(xnT2[k], ps[:, 3 + k, 0:D], ACT.Copy).then_inc(xt2_ready, 1)

            with act.Fori(0, NB // 2) as u:
                for k in range(2):
                    take_xt2(u * 2 + k, k)
            take_xt2(NB - 1, 0)
            act.wait_ge(hrow_ready, 1)
            for h in range(2):
                stage(st_gat, GAT, h, h * HALF, gat_staged)
            rg3 = rg.rearrange("p (j r) -> p j r", r=ROW)
            sb3 = sbf.rearrange("p (j h) -> p j h", h=GH)
            with act.Fori(0, GAT.NT // G) as i:
                for h in range(2):
                    for k in range(h * HALF, (h + 1) * HALF):
                        hold(act, gat_in[k], i * 16 + 16)
                    w = HALF * ROW
                    A(rows_all[:, bass.ds(i * (G * ROW) + h * w, w)], rg[:, h * w:(h + 1) * w], ACT.Copy)
                    act.wait_ge(max_psum, i * G + (h + 1) * HALF)
                    A(sb3[:, h * HALF:(h + 1) * HALF, :], rg3[:, h * HALF:(h + 1) * HALF, HW:ROW],
                      ACT.Copy).then_inc(gat_kept, 1)
                    stage(st_gat, GAT, h, i * G + (G + h * HALF), gat_staged)
            act.wait_ge(dm_ready, 1)
            A(eself, ad_tmp[:, 0:NB * GH], ACT.Exp).then_inc(self_e, 1)

            def copy_turned(b, at):
                act.wait_ge(ohT_psum, b + 1)
                if at >= 2:
                    act.wait_ge(dm_psum, b - 1)
                A(ohT[at % 2], ps_b[:, 2 + at % 2, :], ACT.Copy).then_inc(ohT_ready, 1)

            def exps(b, at):
                act.wait_ge(z_ready, b + 2)
                A(ee[at % 2], zz[at % 2], ACT.Exp).then_inc(ee_ready, 1)

            copy_turned(0, 0)
            copy_turned(1, 1)
            with act.Fori(0, HALVES // 2 - 1) as u:
                for k in range(2):
                    copy_turned(u * 2 + (k + 2), k + 2)
                    exps(u * 2 + k, k)
            for b in range(HALVES - 2, HALVES):
                exps(b, b)
            act.wait_ge(gvar, 1)
            A(st1[:], st2[:], ACT.Sqrt).then_inc(gstd, 1)
            act.wait_ge(gate_z, 1)
            A(eself, eself, ACT.Exp).then_inc(gate_e, 1)

            act.wait_ge(small_in, 16 * 6)
            with act.Fori(0, NB) as t:
                for e in range(NE):
                    act.wait_ge(hid_psum, t * NE + (e + 1))
                    act.wait_ge(y_psum, t * NE + (e + 1))
                    for c in range(FC):
                        ins = A(hT[:, (e % 2) * F + c * P:(e % 2) * F + (c + 1) * P],
                                ps[:, 4 + e % 2, c * P:(c + 1) * P], ACT.Gelu, bias=b1_col[:, e * FC + c:e * FC + c + 1])
                    ins.then_inc(hid_ready, 1)

        @block.tensor
        def _(pe):
            M = nc.tensor.matmul

            def transposed(src, bank=3):
                for c in range(C):
                    ins = nc.tensor.transpose(ps[:, bank, c * P:(c + 1) * P], src[:, c * P:(c + 1) * P], ident[:])
                return ins

            def chunks(out, left, right):
                for c in range(C):
                    ins = M(out, left[c], right[c], start=(c == 0), stop=(c == C - 1))
                return ins

            def cut(ap, w):
                return [ap[:, c * w:(c + 1) * w] for c in range(C)]

            def sort_offsets(g):
                s = sorts[g]
                pe.wait_ge(s["counted"], 1)
                M(ps[:, 2, 0:NB], before[:], cnt[:], start=True, stop=True)
                M(ps[:, 2, 64:64 + NB], ones[:], cnt[:], start=True, stop=True).then_inc(s["prefix"], 1)
                pe.wait_ge(s["based"], 1)
                M(ps[0:NB, 2, 128:129], base[0:1, :], ones[0:1, 0:1], start=True, stop=True).then_inc(s["basecol"], 1)
                pe.wait_ge(s["compared"], 1)
                for q, (a, w) in enumerate(g.chunks):
                    ins = M(ps[0:1, 3 + q, 0:w], ones16[0:NB, 0:1], cmpb[0:NB, a:a + w], start=True, stop=True)
                ins.then_inc(s["blocks"], 1)

            def clear(bank, w):
                return M(ps[:, bank, 0:w], zero16[:], iota_t[:, 0:w], start=True, stop=False, skip_group_check=True)

            def sort_begin(g):
                pe.sem_inc(sorts[g]["placed"], RING)
                for q, (a, w) in enumerate(g.chunks):
                    clear(q, w)

            def place_column(g, n, k):
                s = sorts[g]
                pe.wait_ge(s["puts"], n + (k + 1))
                for put in (put_hi[k % RING], put_lo[k % RING]):
                    for q, (a, w) in enumerate(g.chunks):
                        ins = M(ps[:, q, 0:w], put[:], slot1h[k % RING][:, a:a + w], start=False, stop=False,
                                skip_group_check=True)
                ins.then_inc(s["placed"], 1)

            def sort_end(g):
                M(ps[:, 0, 0:1], zero16[:], iota_t[:, 0:1], start=False, stop=True,
                  skip_group_check=True).then_inc(sorts[g]["placed"], 1)

            pe.wait_ge(const_ready, CONSTS)
            sort_offsets(CONV)

            pe.wait_ge(w_in, 16 * 6)
            pe.wait_ge(sorts[CONV]["block_known"], 1)
            M(ps[:, 6, :], zero16[:], iota_t[:, 0:BANK], start=True, stop=False, skip_group_check=True)
            pe.sem_inc(ctx_used, 1)
            pe.wait_ge(xn_ready, 1)
            transposed(xn).then_inc(xt_psum, 1)

            def project(t, rows_, last=False):
                pe.wait_ge(xt_ready, t + 1)
                chunks(ps[:, 5, :], cut(xnT, P), cut(w_kv, 512)).then_inc(kv_psum, 1)
                pe.wait_ge(msg_ready, t + 1)
                chunks(ps[:, 4, :], cut(xnT, P), cut(w_wk, 512)).then_inc(w_psum, 1)
                pe.wait_ge(q_ready, t + 1)
                for o in range(C):
                    ins = chunks(ps[:, 7, o * P:(o + 1) * P],
                                 [w_q[:, c * D + o * P:c * D + (o + 1) * P] for c in range(C)], cut(xnT, P))
                ins.then_inc(q_psum, 1)
                if not last:
                    pe.wait_ge(xn_ready, t + 2)
                    transposed(xn).then_inc(xt_psum, 1)
                pe.wait_ge(k_ready, t + 1)
                pe.wait_ge(v_ready, t + 1)
                for c in range(C):
                    one = slice(c * P, (c + 1) * P)
                    M(ps[:, 6, c * P:(c + 1) * P], vv[0:rows_, one], kk[0:rows_, one], start=False, stop=last,
                      skip_group_check=True)
                    ins = M(ps[:, 6, 256 + c:257 + c], kk[0:rows_, one], ones[0:rows_, 0:1], start=False, stop=last,
                            skip_group_check=True)
                ins.then_inc(ctx_used, 1)

            pe.sem_inc(msg_ready, 1)
            pe.sem_inc(q_ready, 1)
            with pe.Fori(0, NB - 1) as t:
                project(t, P)
            project(NB - 1, TAIL, last=True)
            pe.wait_ge(ctx_used, NB + 1)
            pe.sem_inc(ctx_done, 1)

            sort_offsets(GAT)

            pe.wait_ge(ctx_masked, 1)
            M(ps[:, 3, 0:D], cbt[:, 0:P], w_p[:, 0:D], start=True, stop=True)
            M(ps[:, 7, 0:D], cbt[:, P:2 * P], w_p[:, D:2 * D], start=True, stop=True).then_inc(cp_psum, 1)
            sort_begin(CONV)
            with pe.Fori(0, NB) as t:
                for k in range(CONV.per_turn):
                    place_column(CONV, t * CONV.per_turn, k)
            sort_end(CONV)
            pe.wait_ge(cp_ready, 2)
            pe.wait_ge(sorts[CONV]["sorted"], 1)

            sort_begin(GAT)
            M(ps[:, 4 + RING - 1, 0:D], zero16[:], iota_t[:, 0:D], start=True, stop=True).then_inc(conv_psum, 1)
            pe.wait_ge(conv_psum, 1)
            pe.sem_inc(conv_psum, RING - 1)

            def conv_turn(i, attention):
                sorted_ = 0
                for k in range(G):
                    pe.wait_ge(conv_oh, i * G + (k + 1))
                    pe.wait_ge(row_in[k], i * 16 + 16)
                    pe.wait_ge(conv_added, i * G + (k + 1))
                    M(ps[:, 4 + k % RING, 0:D], oh1[k % RING], rows[:, k * D:(k + 1) * D], start=True,
                      stop=True).then_inc(conv_psum, 1)
                    if attention and k == 1:
                        pe.wait_ge(q_back, i * 16 + 16)
                        pe.wait_ge(at_added, i + 1)
                        for c in range(C):
                            ins = M(ps[:, 3, c * P:(c + 1) * P], ks[:, c * P:(c + 1) * P],
                                    qexp[:, c * P:(c + 1) * P], start=True, stop=True)
                        ins.then_inc(den_psum, 1)
                    if attention and k == 9:
                        pe.wait_ge(qn_ready, i + 2)
                        for c in range(C):
                            M(ps[:, 3, 0:D], kk[:, c * P:(c + 1) * P], cpw[:, c * D:(c + 1) * D], start=(c == 0),
                              stop=False)
                        M(ps[:, 3, 0:D], ones[0:1, :], bp_row[:], start=False, stop=True).then_inc(at_psum, 1)
                    while sorted_ < GAT.per_turn * (k + 1) // G:
                        place_column(GAT, i * GAT.per_turn, sorted_)
                        sorted_ += 1

            with pe.Fori(0, NB) as i:
                conv_turn(i, True)
            with pe.Fori(NB, GAT.turns) as i:
                conv_turn(i, False)
            sort_end(GAT)

            pe.wait_ge(sorts[GAT]["sorted"], 1)
            flat = ps[:, 0:2, :].rearrange("p b n -> p (b n)")
            pe.wait_ge(wg_in, 16)
            pe.sem_inc(xt2_psum, 2)
            pe.sem_inc(h_psum, 2)

            def transpose_xn2(t, k):
                pe.wait_ge(xn2_ready, t + 1)
                transposed(xn2[k], 3 + k).then_inc(xt2_psum, 1)

            def node_rows(t, k):
                pe.wait_ge(xt2_ready, t + 1)
                chunks(flat[:, bass.ds(t * HW, HW)], cut(xnT2[k], P), cut(w_g, HW)).then_inc(h_psum, 1)

            transpose_xn2(0, 0)
            with pe.Fori(0, NB // 2) as u:
                for k in range(2):
                    transpose_xn2(u * 2 + (k + 1), 1 - k)
                    node_rows(u * 2 + k, k)
            node_rows(NB - 1, 0)
            pe.wait_ge(hrow_ready, 1)
            clear(0, BANK)
            clear(1, BANK)
            pe.sem_inc(max_psum, G)
            four = ident_big[:].rearrange("p (a n) -> p a n", a=1).broadcast_to((P, GH, P))
            with pe.Fori(0, GAT.NT // G) as i:
                for k in range(G):
                    bank = 4 + k % 4
                    pe.wait_ge(gat_noh, i * G + (k + 1))
                    pe.wait_ge(max_taken, i * (2 * G) + (2 * k + 1))
                    if k % HALF == 0:
                        pe.wait_ge(gat_kept, i * 2 + (k // HALF + 1))
                    M(ps[:, bank, :].rearrange("p (h n) -> p h n", h=GH), nohb[k % 4], four, start=True, stop=False)
                    for h in range(GH):
                        s1 = sbf[:, k * GH + h:k * GH + h + 1].broadcast_to((P, P))
                        ins = M(ps[:, bank, h * P:(h + 1) * P], s1, ident_b[:], start=False, stop=(h == GH - 1))
                    ins.then_inc(max_psum, 1)

            pe.wait_ge(self_e, 1)
            pe.sem_inc(sum_done, 3)
            pe.sem_inc(z_ready, 1)

            def turn_onehots(b, at):
                pe.wait_ge(oh_ready, b + 1)
                for k in range(HALF):
                    ins = nc.tensor.transpose(ps_b[:, 2 + at % 2, k * P:(k + 1) * P],
                                              ohb[at % OH_RING][:, k * P:(k + 1) * P], ident_b[:])
                ins.then_inc(ohT_psum, 1)

            dmb3 = dmb.rearrange("p (q n) -> p q n", q=PARTS)

            def fetch(bank, k, turned, col):
                w = PARTS * 2 * GH
                return M(ps[:, bank, k * w:(k + 1) * w].rearrange("p (q n) -> p q n", q=PARTS),
                         turned[:, k * P:(k + 1) * P], dmb3[:, :, bass.ds(col, 2 * GH)], start=True, stop=True)

            def fetch_targets(b, at):
                ats = columns(PE, dm_at, b * HALF, HALF, dm_most)
                pe.wait_ge(z_ready, b)
                pe.wait_ge(ohT_ready, b + 1)
                for k in range(HALF):
                    ins = fetch(6 + at % 2, k, ohT[at % 2], ats[k])
                ins.then_inc(dm_psum, 1)

            def sum_messages(b, at):
                ats = columns(PE, sum_at, b * HALF, HALF, sum_most)
                pe.wait_ge(m_ready, b + 1)
                for k in range(HALF):
                    for q in range(PARTS):
                        a = (q * HALF + k) * ROW
                        ins = M(flat[:, bass.ds(ats[k], ROW)], ohb[at % OH_RING][:, k * P:(k + 1) * P],
                                msgb3[at % 2][:, a:a + ROW], start=False, stop=False, skip_group_check=True)
                ins.then_inc(sum_done, 1)

            def pass2_step(b, at, first=False, last=False):
                if not first:
                    sum_messages(b - 2, at - 2)
                if not last or at + 2 < HALVES:
                    turn_onehots(b + 2, at + 2)
                if not last or at + 1 < HALVES:
                    fetch_targets(b + 1, at + 1)

            turn_onehots(0, 0)
            turn_onehots(1, 1)
            ats0 = columns(PE, dm_at, 0, HALF, dm_most)
            pe.wait_ge(ohT_ready, 1)
            for k in range(HALF):
                ins = fetch(6, k, ohT[0], ats0[k])
            ins.then_inc(dm_psum, 1)
            for b in range(2):
                pass2_step(b, b, first=True)
            with pe.Fori(0, PASS2_TURNS) as u:
                for k in range(OH_RING):
                    pass2_step(u * OH_RING + (k + 2), k + 2)
            for b in range(2 + PASS2_TURNS * OH_RING, HALVES):
                pass2_step(b, b, last=True)
            for b in range(HALVES - 2, HALVES):
                sum_messages(b, b)

            pe.wait_ge(ffn_in, 48)
            pe.sem_inc(y_psum, 2)
            x3 = xt3.rearrange("p (b c n) -> p b c n", b=2, c=C)

            def hidden(e, par):
                for f in range(FC):
                    at = e * F + f * P
                    ins = chunks(ps[:, 4 + e % 2, f * P:(f + 1) * P],
                                 [w1[:, c * NE * F + at:c * NE * F + at + P] for c in range(C)],
                                 [x3[:, par, c, :] for c in range(C)])
                ins.then_inc(hid_psum, 1)

            def outputs(e, n):
                pe.wait_ge(hid_ready, n + 1)
                pe.wait_ge(y_taken, n + 1)
                for f in range(FC):
                    M(ps[:, 6 + e % 2, 0:D], hT[:, (e % 2) * F + f * P:(e % 2) * F + (f + 1) * P],
                      w2[:, (e * FC + f) * D:(e * FC + f + 1) * D], start=(f == 0), stop=False)
                M(ps[:, 6 + e % 2, 0:D], ones[0:1, :], b2_row[:, e * D:(e + 1) * D], start=False,
                  stop=True).then_inc(y_psum, 1)

            pe.wait_ge(xt3_in[0], 16)
            hidden(0, 0)
            with pe.Fori(0, NB // 2) as u:
                for k in range(2):
                    for e in range(NE):
                        if e < NE - 1:
                            hidden(e + 1, k)
                        else:
                            if k == 0:
                                pe.wait_ge(xt3_in[1], u * 16 + 16)
                            else:
                                pe.wait_ge(xt3_in[0], u * 16 + 32)
                            hidden(0, 1 - k)
                        outputs(e, u * (2 * NE) + (k * NE + e))
            for e in range(NE):
                if e < NE - 1:
                    hidden(e + 1, 0)
                outputs(e, (NB - 1) * NE + e)


def kernel(x, src, dst, L0_gnn_w0, L0_gnn_w1, L0_mix_Wq, L0_mix_Wkv, L0_mix_Wproj, L0_mix_bproj, L0_ffn_W_gat,
           L0_ffn_att_src, L0_ffn_att_dst, L0_ffn_b_gat, L0_ffn_ln_gamma, L0_ffn_ln_beta, L0_ffn_W1, L0_ffn_b1,
           L0_ffn_W2, L0_ffn_b2, L0_ffn_edge_index):
    import numpy as np
    import concourse.bacc as bacc
    from concourse.bass_utils import run_bass_kernel_spmd as run

    c = np.ascontiguousarray
    ei = np.asarray(L0_ffn_edge_index)
    w1 = np.asarray(L0_ffn_W1)
    arrays = {
        "x": c(x), "conv_target": c(src), "conv_source": c(dst), "gat_source": c(ei[0]), "gat_target": c(ei[1]),
        "w0": c(L0_gnn_w0), "w1": c(L0_gnn_w1), "WqT": c(np.asarray(L0_mix_Wq).T), "WkvT": c(np.asarray(L0_mix_Wkv).T),
        "WprojT": c(np.asarray(L0_mix_Wproj).T), "bproj": c(L0_mix_bproj), "W_gat": c(L0_ffn_W_gat),
        "att_src": c(L0_ffn_att_src).reshape(-1), "att_dst": c(L0_ffn_att_dst).reshape(-1), "b_gat": c(L0_ffn_b_gat),
        "gamma": c(L0_ffn_ln_gamma), "beta": c(L0_ffn_ln_beta),
        "W1": c(w1.transpose(1, 0, 2).reshape(D, NE * F)), "b1T": c(np.asarray(L0_ffn_b1).reshape(NE * FC, P).T),
        "W2": c(L0_ffn_W2).reshape(NE * F, D), "b2": c(L0_ffn_b2),
    }
    nc = bacc.Bacc("TRN2", target_bir_lowering=False, num_devices=1)
    io = {}
    for name, a in arrays.items():
        io[name] = nc.dram_tensor(f"in_{name}", a.shape, mybir.dt.from_np(a.dtype), kind="ExternalInput").ap()
    io["out"] = nc.dram_tensor("out", (N, D), F32, kind="ExternalOutput").ap()
    io["edges"] = {CONV: (io["conv_target"], io["conv_source"]), GAT: (io["gat_target"], io["gat_source"])}
    layer(nc, io)
    r = run(nc, [{f"in_{k}": a for k, a in arrays.items()}], core_ids=[0])
    return r.results[0]["out"]
```

```python
from contextlib import ExitStack

import concourse.bass as bass
from concourse import mybir

F32, I32, I16, F16, BF16, U16 = (mybir.dt.float32, mybir.dt.int32, mybir.dt.int16, mybir.dt.float16,
                                 mybir.dt.bfloat16, mybir.dt.uint16)
DVE, PE = mybir.EngineType.DVE, mybir.EngineType.PE
ALU, ACT, AX = mybir.AluOpType, mybir.ActivationFunctionType, mybir.AxisListType

P = 128
BANK = 512
N, D = 6250, 256
NB = -(-N // P)
TAIL = N - (NB - 1) * P
NPAD = NB * P
C = D // P
HEAD = 32
EPS = 1e-5
NE, F = 4, 512
FC = F // P
GH, GC = 4, 4
HW = GH * GC
ROW = HW + GH
G = 16
BIG = 1e30
SCAT = 4
HALF = 8
RING = 4
PARTS = 3
LAG = 2
OH_RING = 6
PER_BANK = 25


class Graph:

    def __init__(self, edges, turns):
        self.E = edges
        self.turns = turns
        self.per_turn = 2 * -(-edges // (2 * P * turns))
        self.placed = self.per_turn - SCAT
        self.T = self.per_turn * turns
        most = (edges + NB * (P - 1)) // P
        self.NT = -(-most // G) * G
        self.chunks = [(a, min(BANK, self.NT - a)) for a in range(0, self.NT, BANK)]
        self.full = edges // self.T
        self.rest = edges - self.full * self.T


CONSTS = 10 + 2 + P // HEAD + 5
CONV = Graph(100000, NB)
GAT = Graph(131072, CONV.NT // G)
HALVES = GAT.NT // HALF
PASS2_TURNS = (HALVES - 3 - 2) // OH_RING
PASS1_TURNS = GAT.NT // G
EARLY = PASS1_TURNS // 3 * 2
LATE = NB - EARLY
FIN = 4
FIN_TAIL = EARLY // 2 - FIN * LATE
assert PASS1_TURNS % 3 == 1 and FIN == NE and 0 <= FIN_TAIL <= FIN
TM, NTM = max(CONV.T, GAT.T), max(CONV.NT, GAT.NT)


class Carve:

    def __init__(self, tensor, words):
        self.tensor, self.words, self.at = tensor, words, 0

    def take(self, n, dtype=F32):
        words = n if dtype in (F32, I32) else -(-n // 2)
        a = self.at
        self.at += words
        assert self.at <= self.words, (self.at, self.words)
        ap = self.tensor[:, a:a + words]
        return ap if dtype is F32 else ap.bitcast(dtype)[:, 0:n]


class Steps:

    def __init__(self, eng, sem):
        self.eng, self.sem, self.base, self.k, self.turn = eng, sem, 0, 0, None

    def value(self):
        return self.base + self.k if self.turn is None else self.turn + (self.base + self.k)

    def did(self, ins):
        ins.then_inc(self.sem, 1)
        self.k += 1

    def settle(self):
        self.eng.wait_ge(self.sem, self.value())

    def do(self, ins):
        self.did(ins)
        self.settle()

    def note(self, ins):
        self.did(ins)
        return self.value()

    def after(self, value):
        self.eng.wait_ge(self.sem, value)

    def enter(self, i, per_turn):
        self.base, self.k, self.turn = self.base + self.k, 0, i * per_turn

    def leave(self, turns, per_turn):
        assert self.k == per_turn, (self.k, per_turn)
        self.base, self.k, self.turn = self.base + turns * per_turn, 0, None


def layer(nc, io):
    ctx = ExitStack()
    with ctx:
        sem_names = []

        def sem(name):
            sem_names.append(name)
            return ctx.enter_context(nc.semaphore(name))

        def sb(name, cols, dtype=F32, rows=P):
            return ctx.enter_context(nc.sbuf_tensor(name, [rows, cols], dtype))

        msg_d = nc.dram_tensor("messages", (NPAD, D), F32, kind="Internal").ap()
        q_d = nc.dram_tensor("q_t", (P, C * NPAD), F32, kind="Internal").ap()
        xt_d = nc.dram_tensor("x2n_t", (P, C * NPAD), F32, kind="Internal").ap()
        x2_d = nc.dram_tensor("x2", (NPAD, D), F32, kind="Internal").ap()
        y_d = nc.dram_tensor("experts_out", (EARLY * P, NE * D), F32, kind="Internal").ap()
        row_d = nc.dram_tensor("gat_rows", (NPAD, ROW), F32, kind="Internal").ap()
        slot_d = {g: nc.dram_tensor(nm, (P * (g.NT + 1) + NTM + 2 + P * SCAT, 1), F32, kind="Internal").ap()
                  for g, nm in ((CONV, "conv_slots"), (GAT, "gat_slots"))}
        slot_rows = {g: slot_d[g][0:P * (g.NT + 1), :].rearrange("(p n) a -> p (n a)", p=P) for g in (CONV, GAT)}
        q_dv = q_d.rearrange("p (c n) -> p c n", c=C)
        xt_dv = xt_d.rearrange("p (c n) -> p c n", c=C)

        x_sb = sb("x_sb", NB * D)
        sort_words = 3 * TM + TM // 2 + NTM + TM + (3 * (CONV.T + GAT.T)) // 2 + 2 * (CONV.T + GAT.T)
        arena_words = max(NB * D + sort_words, GAT.NT * ROW)
        arena_t = sb("arena", arena_words)
        arena = Carve(arena_t, arena_words)
        acc = arena.take(NB * D)
        tg, sr, tmp = (arena.take(TM, I32) for _ in range(3))
        oh = arena.take(TM, F16)
        cum = arena.take(NTM)
        pos = arena.take(TM)
        bk = {g: arena.take(g.T, F16) for g in (CONV, GAT)}
        slo = {g: arena.take(g.T, F16) for g in (CONV, GAT)}
        shi = {g: arena.take(g.T, F16) for g in (CONV, GAT)}
        hi = {g: arena.take(g.T) for g in (CONV, GAT)}
        lo = {g: arena.take(g.T) for g in (CONV, GAT)}
        rows_all = arena_t[:, 0:GAT.NT * ROW]
        ffn = Carve(x_sb, NB * D)
        w1 = ffn.take(C * NE * F)
        w2 = ffn.take(NE * FC * D)
        b2_f = ffn.take(NE * D)[0:PARTS, :]
        b2_b = ffn.take(NE * D, BF16)[0:PARTS, :]
        xt3 = ffn.take(2 * C * P)
        hT = ffn.take(2 * F)
        y_out = ffn.take(NE * D)
        part_tmp = [a[0:PARTS, :].bitcast(BF16) for a in (hT[:, 0:F], hT[:, F:])]
        fin = Carve(arena_t, arena_words)
        res = [fin.take(2 * D) for _ in range(FIN)]
        y_back = [fin.take(2 * NE * D) for _ in range(FIN)]
        res_late = [fin.take(D) for _ in range(2)]

        idx = {CONV: sb("conv_idx", CONV.NT + G, I32), GAT: sb("gat_idx", GAT.NT + G, I32)}
        dlo = {CONV: sb("conv_dlo", CONV.NT + G, F16), GAT: sb("gat_dlo", GAT.NT + G, F16)}
        conv_at = sb("conv_at", CONV.NT + LAG, I16, 1)
        dm_at = sb("dm_at", GAT.NT, I16, 1)
        sum_at = sb("sum_at", GAT.NT, I16, 1)
        iota_t = sb("iota_t", NTM, F16)
        slot_words = RING * -(-NTM // 2)
        slot_t = sb("slot1h", slot_words)
        slots_ = Carve(slot_t, slot_words)
        slot1h = [slots_.take(NTM, F16) for _ in range(RING)]
        lo1h = [sb(f"lo1h{k}", P, F16) for k in range(RING)]
        put_hi = [sb(f"put_hi{k}", P, F16) for k in range(RING)]
        put_lo = [sb(f"put_lo{k}", P, F16) for k in range(RING)]
        iota_p = sb("iota_p", P, F16)
        iota_b = sb("iota_b", NB)
        zero16 = sb("zero16", P, F16)
        ident = sb("ident", P)
        ident_b = sb("ident_b", P, BF16)
        ident_big = sb("ident_big", P, BF16)
        ones = sb("ones", P)
        ones_b = sb("ones_b", P, BF16, PARTS)
        ones16 = sb("ones16", 1, F16)
        before = sb("before", P)
        headmask = sb("headmask", P)
        cnt, off, til, cumt, base, totf = (sb(n, NB) for n in ("cnt", "off", "til", "cumt", "base", "totf"))
        tot = sb("tot", NB, I32)
        bcol = sb("bcol", 1)
        cmpb = slot1h[0]
        scat_at, scat_val = sb("scat_at", SCAT, I32), sb("scat_val", SCAT)
        scat_past, scat_tmp, scat_col = (sb(n, SCAT) for n in ("scat_past", "scat_tmp", "scat_col"))
        signal_word = sb("signal_word", 1)
        stat = cum[:, 0:NB * 6]
        mean, var, rstd, st1, st2 = (sb(n, NB) for n in ("mean", "var", "rstd", "st1", "st2"))

        shared_words = 6416
        shared_t = sb("shared", shared_words)
        ph = Carve(shared_t, shared_words)
        xn, kk, qexp = (ph.take(D) for _ in range(3))
        ks = ph.take(C * P)
        cpw = ph.take(C * D)
        bp_row = ph.take(D)[0:1, :]
        cv = Carve(shared_t, shared_words)
        cv.at = ph.at
        w_wk = ph.take(C * 512)
        w_kv = ph.take(C * 512)
        w_q = ph.take(C * D)
        w_p = ph.take(C * D)
        xnT, kexp, vv, qq, msgb = (ph.take(D) for _ in range(5))
        cbt = ph.take(C * P)
        rows = cv.take(G * D)
        oh1 = [cv.take(P) for _ in range(RING)]
        st_conv = cv.take(G, I32)
        ga = Carve(shared_t, shared_words)
        hrow = ga.take(NB * ROW)
        ad_tmp = ga.take(NB * HW)
        dm = ga.take(NB * 2 * GH)
        st_gat = ga.take(G, I32)
        den = ga.take(NB * GH)
        eself = ga.take(NB * GH)
        gate = ga.take(NB * NE)
        g2 = Carve(shared_t, shared_words)
        g2.at = ga.at
        w_g = ga.take(C * HW)
        xn2, xnT2 = ([ga.take(D) for _ in range(RING)] for _ in range(2))
        rg = ga.take(G * ROW)
        sbf = ga.take(G * GH, BF16)
        nohb = [ga.take(P, BF16) for _ in range(RING)]
        mx = ga.take(RING * GH)
        zz, ee = ([g2.take(HALF * GH) for _ in range(2)] for _ in range(2))
        msg = [g2.take(HALF * ROW) for _ in range(2)]
        past = Carve(arena_t, arena_words)
        past.at = GAT.NT * ROW
        over_slots = Carve(slot_t, slot_words)
        ohb = [past.take(HALF * P, BF16) for _ in range(OH_RING)]
        ohT = [over_slots.take(HALF * P, BF16) for _ in range(2)]
        dmb = g2.take(PARTS * NB * 2 * GH, BF16)
        dm_rest = g2.take(NB * 2 * GH)
        dsum = [g2.take(HALF * 2 * GH) for _ in range(2)]
        msgb3 = [g2.take(PARTS * HALF * ROW, BF16) for _ in range(2)]
        b1_col = sb("b1_col", NE * FC)
        smalls = sb("smalls", 5 * HW)

        ps = ctx.enter_context(nc.psum_tensor("ps", [P, 8, BANK], F32))

        ps_b = ps[:].bitcast(BF16)

        def nodes(ap, t, w=D):
            return ap[:, bass.ds(t * w, w)]

        const_ready = sem("const_ready")
        edges_in = {CONV: sem("conv_edges_in"), GAT: sem("gat_edges_in")}
        pads_set = {CONV: sem("conv_pads_set"), GAT: sem("gat_pads_set")}
        x_in, w_in, wg_in, small_in = (sem(n) for n in ("x_in", "w_in", "wg_in", "small_in"))
        w1_in, w2_in, b2_in, b2_ready = sem("w1_in"), sem("w2_in"), sem("b2_in"), sem("b2_ready")
        x_pad, zeros_set, zeros_in = sem("x_pad"), sem("zeros_set"), sem("zeros_in")
        dve_step, act_step, marks = sem("dve_step"), sem("act_step"), sem("marks")
        sorts = {}
        for g, nm in ((CONV, "conv"), (GAT, "gat")):
            sorts[g] = {k: sem(f"{nm}_{k}") for k in
                        ("unpacked", "offsets", "sums",
                         "block_known", "onehots", "puts", "placed", "sorted", "scat_staged", "scat_free",
                         "scattered", "back_ready", "back_in")}
        var_ready, std_ready = [sem("var1"), sem("var2")], [sem("std1"), sem("std2")]
        xn_ready, xt_psum, xt_ready = sem("xn_ready"), sem("xt_psum"), sem("xt_ready")
        kv_psum, w_psum, q_psum = sem("kv_psum"), sem("w_psum"), sem("q_psum")
        kexp_ready, v_ready, k_ready, qexp_ready, q_ready = (sem(n) for n in (
            "kexp_ready", "v_ready", "k_ready", "qexp_ready", "q_ready"))
        msg_ready, msg_stored, msg_free, q_stored, q_free = (sem(n) for n in (
            "msg_ready", "msg_stored", "msg_free", "q_stored", "q_free"))
        ctx_used, ctx_done = sem("ctx_used"), sem("ctx_done")
        ctx_masked, cp_psum, cp_ready = sem("ctx_masked"), sem("cp_psum"), sem("cp_ready")
        q_back, den_psum, qn_ready, at_psum, at_added = (sem(n) for n in (
            "q_back", "den_psum", "qn_ready", "at_psum", "at_added"))
        conv_staged = sem("conv_staged")
        row_in = [sem(f"row_in{k}") for k in range(G)]
        conv_oh, conv_psum, conv_added = sem("conv_oh"), sem("conv_psum"), sem("conv_added")
        x2_ready = sem("x2_ready")
        xn2_ready, xt2_psum, xt2_ready, xt2_free, h_psum = (sem(n) for n in (
            "xn2_ready", "xt2_psum", "xt2_ready", "xt2_free", "h_psum"))
        xt2_stored = [sem(f"xt2_stored{k}") for k in range(RING)]
        hrow_ready, hrow_stored = sem("hrow_ready"), sem("hrow_stored")
        gat_staged = sem("gat_staged")
        gat_kept, gat_noh, max_psum, max_taken = (sem(n) for n in (
            "gat_kept", "gat_noh", "max_psum", "max_taken"))
        dm_ready = sem("dm_ready")
        oh_ready, ohT_psum, ohT_ready, dm_psum, z_ready, ee_ready, m_ready, sum_done = (sem(n) for n in (
            "oh_ready", "ohT_psum", "ohT_ready", "dm_psum", "z_ready", "ee_ready", "m_ready", "sum_done"))
        self_e, gate_z, gate_e, gvar, gstd, gates_ready = (sem(n) for n in (
            "self_e", "gate_z", "gate_e", "gvar", "gstd", "gates_ready"))
        xt3_in = [sem("xt3_in0"), sem("xt3_in1")]
        early_hid, early_act, early_y, early_kept, early_free, early_stored = (sem(n) for n in (
            "early_hid", "early_act", "early_y", "early_kept", "early_free", "early_stored"))
        x2_stored = sem("x2_stored")
        hid_psum, hid_ready, y_psum, y_taken, combined = (sem(n) for n in (
            "hid_psum", "hid_ready", "y_psum", "y_taken", "combined"))
        back_in, out_stored = ([sem(f"{n}{k}") for k in range(FIN)] for n in ("back_in", "out_stored"))
        late_in, late_stored = ([sem(f"{n}{k}") for k in range(2)] for n in ("late_in", "late_stored"))

        block = ctx.enter_context(nc.Block())

        def hold(eng, s, value):
            eng.wait_ge(s, value)
            eng.sem_inc(marks, 1)

        def columns(engine, row, at, n, most):
            return nc.values_load_multi_w_load_instructions(
                row[0:1, bass.ds(at, n)], engines=[engine], min_val=0, max_val=most,
                skip_runtime_bounds_check_because="they are columns of blocks, below the last block by construction")[1]

        dm_most = (NB - 1) * 2 * GH
        sum_most = (NB - 1) * ROW + BANK - PER_BANK * ROW

        @block.sync
        def _(sp):
            def load_edges(g):
                t, s = io["edges"][g]
                for dst, src in ((tg, t), (sr, s)):
                    sp.dma_start(dst[0:g.full, 0:g.T],
                                 src[0:g.full * g.T].rearrange("(p t) -> p t", t=g.T)).then_inc(edges_in[g], 16)
                    if g.rest:
                        sp.dma_start(dst[g.full:g.full + 1, 0:g.rest],
                                     src[g.full * g.T:g.E].rearrange("(p t) -> p t", t=g.rest)
                                     ).then_inc(edges_in[g], 16)

            sp.wait_ge(pads_set[CONV], 2)
            load_edges(CONV)
            sp.wait_ge(zeros_set, 1)
            for g in (CONV, GAT):
                sp.dma_start(slot_rows[g], acc[:, 0:g.NT + 1]).then_inc(zeros_in, 16)
            sp.wait_ge(x_pad, 1)
            sp.dma_start(x_sb[:, 0:(NB - 1) * D].rearrange("p (t f) -> p t f", f=D),
                         io["x"][0:(NB - 1) * P, :].rearrange("(t p) f -> p t f", p=P)).then_inc(x_in, 16)
            sp.dma_start(x_sb[0:TAIL, (NB - 1) * D:], io["x"][(NB - 1) * P:N, :]).then_inc(x_in, 16)
            chunked = "(c p) n -> p c n"
            wk = w_wk.rearrange("p (c n) -> p c n", c=C)
            sp.dma_start(wk[:, :, 0:D], io["w0"].rearrange(chunked, p=P)).then_inc(w_in, 16)
            sp.dma_start(wk[:, :, D:], io["w1"].rearrange(chunked, p=P)).then_inc(w_in, 16)
            for dst, src in ((w_kv, "WkvT"), (w_q, "WqT"), (w_p, "WprojT")):
                sp.dma_start(dst.rearrange("p (c n) -> p c n", c=C), io[src].rearrange(chunked, p=P)).then_inc(w_in, 16)
            sp.dma_start(bp_row[:], io["bproj"].rearrange("(a n) -> a n", a=1)).then_inc(w_in, 16)
            sp.dma_start(b1_col[:], io["b1T"]).then_inc(small_in, 16)
            for k, name in enumerate(("att_src", "att_dst", "b_gat", "gamma", "beta")):
                src = io[name].rearrange("(a n) -> a n", a=1).broadcast_to((P, HW))
                sp.dma_start(smalls[:, k * HW:(k + 1) * HW], src).then_inc(small_in, 16)

            sp.wait_ge(pads_set[GAT], 2)
            load_edges(GAT)
            sp.sem_inc(msg_free, 1)
            sp.sem_inc(q_free, 1)
            with sp.Fori(0, NB) as t:
                hold(sp, msg_ready, t + 2)
                sp.dma_start(msg_d[bass.ds(t * P, P), :], msgb).then_inc(msg_stored, 16)
                hold(sp, q_ready, t + 2)
                sp.dma_start(q_dv[:, :, bass.ds(t * P, P)], qq.rearrange("p (c n) -> p c n", c=C)).then_inc(q_stored, 16)
                hold(sp, msg_stored, t * 16 + 16)
                sp.sem_inc(msg_free, 1)
                hold(sp, q_stored, t * 16 + 16)
                sp.sem_inc(q_free, 1)
            def slots_back(g):
                s = sorts[g]
                sp.wait_ge(s["scattered"], 16 * SCAT * g.turns)
                sp.wait_ge(s["back_ready"], 1)
                sp.dma_start(cum[:, 0:g.NT], slot_rows[g][:, 0:g.NT]).then_inc(s["back_in"], 16)

            slots_back(CONV)
            with sp.Fori(0, NB) as t:
                hold(sp, qn_ready, t + 1)
                sp.dma_start(qexp.rearrange("p (c n) -> p c n", c=C), q_dv[:, :, bass.ds(t * P, P)]).then_inc(q_back, 16)
                hold(sp, q_back, t * 16 + 16)
            slots_back(GAT)
            sp.wait_ge(x2_ready, 1)
            sp.dma_start(w_g.rearrange("p (c n) -> p c n", c=C), io["W_gat"].rearrange(chunked, p=P)).then_inc(wg_in, 16)
            sp.sem_inc(xt2_free, RING)

            def store_xt2(t, k):
                hold(sp, xt2_ready, t + 1)
                sp.dma_start(xt_dv[:, :, bass.ds(t * P, P)],
                             xnT2[k].rearrange("p (c n) -> p c n", c=C)).then_inc(xt2_stored[k], 16)
                sp.dma_start(x2_d[bass.ds(t * P, P), :], nodes(x_sb, t)).then_inc(x2_stored, 16)

            def xt2_done(k, u):
                hold(sp, xt2_stored[k], u * 16 + 16)
                sp.sem_inc(xt2_free, 1)

            with sp.Fori(0, NB // RING) as u:
                for k in range(RING):
                    store_xt2(u * RING + k, k)
                    if k >= 2:
                        xt2_done(k - 2, u)
                for k in range(RING - 2, RING):
                    xt2_done(k, u)
            store_xt2(NB - 1, 0)
            sp.wait_ge(xt2_stored[0], 16 * (NB // RING + 1))
            sp.wait_ge(hrow_ready, 1)
            sp.dma_start(row_d.rearrange("(t p) r -> p t r", p=P), hrow.rearrange("p (t r) -> p t r", r=ROW)).then_inc(hrow_stored, 16)
            sp.wait_ge(x2_stored, 16 * NB)
            sp.wait_ge(xn2_ready, NB)
            sp.dma_start(b2_f, io["b2"].rearrange("e n -> (e n)").rearrange("(a n) -> a n", a=1).broadcast_to(
                (PARTS, NE * D))).then_inc(b2_in, 16)
            sp.dma_start(w1.rearrange("p (c n) -> p c n", c=C), io["W1"].rearrange(chunked, p=P)).then_inc(w1_in, 16)
            x3 = xt3.rearrange("p (b c n) -> p b c n", b=2, c=C)
            sp.dma_start(x3[:, 0], xt_dv[:, :, 0:P]).then_inc(xt3_in[0], 16)
            sp.dma_start(w2.rearrange("p (c n) -> p c n", c=NE * FC), io["W2"].rearrange(chunked, p=P)).then_inc(w2_in, 16)
            sp.sem_inc(early_free, 1)
            with sp.Fori(0, EARLY) as u:
                hold(sp, early_hid, u * NE + NE)
                sp.dma_start(x3[:, 0], xt_dv[:, :, bass.ds(u * P + P, P)]).then_inc(xt3_in[0], 16)
                hold(sp, early_kept, u * NE + (NE + 1))
                sp.dma_start(y_d[bass.ds(u * P, P), :], y_out).then_inc(early_stored, 16)
                hold(sp, early_stored, u * 16 + 16)
                sp.sem_inc(early_free, 1)

            def pair(d, at):
                return d[bass.ds(at * (2 * P), 2 * P), :].rearrange("(t p) f -> p t f", p=P)

            def load_pair(n, k):
                sp.dma_start(res[k].rearrange("p (t f) -> p t f", t=2), pair(x2_d, n)).then_inc(back_in[k], 16)
                sp.dma_start(y_back[k].rearrange("p (t f) -> p t f", t=2), pair(y_d, n)).then_inc(back_in[k], 16)

            def store_pair(n, k):
                hold(sp, combined, n * 2 + 2)
                sp.dma_start(pair(io["out"], n), res[k].rearrange("p (t f) -> p t f", t=2)).then_inc(out_stored[k], 16)

            def load_late(v, k):
                sp.dma_start(res_late[k], x2_d[bass.ds(v * P + EARLY * P, P), :]).then_inc(late_in[k], 16)

            def next_input(v, k):
                hold(sp, hid_psum, v * NE + 1)
                sp.dma_start(x3[:, 1 - k], xt_dv[:, :, bass.ds(v * P + (EARLY + 1) * P, P)]).then_inc(xt3_in[1 - k], 16)

            sp.wait_ge(m_ready, -(-fin.at // (HALF * ROW)))
            for k in range(FIN):
                load_pair(k, k)
            load_late(0, 0)
            for v in range(LATE):
                if v < LATE - 1:
                    load_late(v + 1, (v + 1) % 2)
                    next_input(v, v % 2)
                for k in range(FIN):
                    store_pair(v * FIN + k, k)
                    if v * FIN + k + FIN < EARLY // 2:
                        sp.wait_ge(out_stored[k], 16 * (v + 1))
                        load_pair((v + 1) * FIN + k, k)
                rows_ = P if v < LATE - 1 else TAIL
                sp.wait_ge(y_taken, v * NE + (NE + 2))
                sp.dma_start(io["out"][(EARLY + v) * P:(EARLY + v) * P + rows_, :], res_late[v % 2][0:rows_, :]
                             ).then_inc(late_stored[v % 2], 16)
                if v < LATE - 1:
                    sp.wait_ge(late_stored[v % 2], 16 * (v // 2 + 1))
            for k in range(FIN_TAIL):
                store_pair(LATE * FIN + k, k)
            for k in range(FIN):
                sp.wait_ge(out_stored[k], 16 * (LATE + (k < FIN_TAIL)))
            for k in range(2):
                sp.wait_ge(late_stored[k], 16 * ((LATE + 1 - k) // 2))

        @block.gpsimd
        def _(pool):
            gp = nc.gpsimd

            def iota(out, n):
                gp.iota(out, pattern=[[1, n]], base=0, channel_multiplier=0,
                        allow_small_or_imprecise_dtypes=True).then_inc(const_ready, 1)

            gp.memset(tg[:], 8191).then_inc(pads_set[CONV], 1)
            gp.memset(sr[:], 0).then_inc(pads_set[CONV], 1)
            gp.memset(x_sb[:, (NB - 1) * D:], 0.0).then_inc(x_pad, 1)
            gp.memset(acc[:, 0:NTM + 1], 0.0).then_inc(zeros_set, 1)
            iota(iota_t[:], NTM)
            iota(iota_p[:], P)
            iota(iota_b[:], NB)
            gp.iota(scat_past[:], pattern=[[1, SCAT]], base=NTM + 2, channel_multiplier=SCAT,
                    allow_small_or_imprecise_dtypes=True).then_inc(const_ready, 1)
            for ap, val in ((zero16, 0.0), (ones, 1.0), (ones16, 1.0), (headmask, 0.0)):
                gp.memset(ap[:], val).then_inc(const_ready, 1)
            pool.wait_ge(const_ready, 8)
            gp.affine_select(out=before[:], in_=ones[:], compare_op=ALU.is_gt, fill=0.0, base=0,
                             pattern=[[1, P]], channel_multiplier=-1).then_inc(const_ready, 1)
            gp.affine_select(out=ident[:], in_=ones[:], compare_op=ALU.is_equal, fill=0.0, base=0,
                             pattern=[[1, P]], channel_multiplier=-1).then_inc(const_ready, 1)
            pool.wait_ge(const_ready, 10)
            gp.tensor_copy(ident_b[:], ident[:]).then_inc(const_ready, 1)
            gp.tensor_scalar(ident_big[:], ident[:], BIG, None, ALU.mult).then_inc(const_ready, 1)
            for h in range(P // HEAD):
                pool.wait_ge(const_ready, 12 + h)
                gp.memset(headmask[h * HEAD:(h + 1) * HEAD, h * HEAD:(h + 1) * HEAD], 1.0).then_inc(const_ready, 1)

            pool.wait_ge(const_ready, 12 + P // HEAD)
            gp.memset(ones_b[:], 1.0).then_inc(const_ready, 1)
            for g in (CONV, GAT):
                gp.memset(idx[g][:], 0).then_inc(const_ready, 1)
                gp.memset(dlo[g][:], -1.0).then_inc(const_ready, 1)

            def scatter(g, i):
                s = sorts[g]
                hold(pool, s["scat_staged"], i + 1)
                for k in range(SCAT):
                    gp.indirect_dma_start(
                        out=slot_d[g],
                        out_offset=bass.IndirectOffsetOnAxis(ap=scat_at[:, k:k + 1], axis=0),
                        in_=scat_val[:, k:k + 1], in_offset=None,
                    ).then_inc(s["scattered"], 16)

            def scatter_done(g, i):
                hold(pool, sorts[g]["scattered"], i * (16 * SCAT) + 16 * SCAT)
                pool.sem_inc(sorts[g]["scat_free"], 1)

            def gather(g, table, width, dest, stage, staged, arrived, other=None):
                with pool.Fori(0, g.NT // G) as i:
                    for k in range(G):
                        if k % HALF == 0:
                            hold(pool, staged, i * 2 + (k // HALF + 1))
                        gp.indirect_dma_start(
                            out=dest[:, k * width:(k + 1) * width], out_offset=None, in_=table,
                            in_offset=bass.IndirectOffsetOnAxis(ap=stage[:, k:k + 1], axis=0),
                        ).then_inc(arrived[k], 16)
                        if other and k == HALF - 1:
                            scatter(other, i)
                    if other:
                        scatter_done(other, i)

            pool.wait_ge(sorts[CONV]["unpacked"], 1)
            gp.memset(tg[:], 8191).then_inc(pads_set[GAT], 1)
            gp.memset(sr[:], 0).then_inc(pads_set[GAT], 1)
            pool.wait_ge(msg_stored, 16 * NB)
            pool.wait_ge(zeros_in, 32)
            with pool.Fori(0, NB) as t:
                scatter(CONV, t)
                scatter_done(CONV, t)
            gather(CONV, msg_d, D, rows, st_conv, conv_staged, row_in, other=GAT)
            pool.wait_ge(hrow_stored, 16)
            gather(GAT, row_d, ROW, rg, st_gat, gat_staged, row_in)

        @block.vector
        def _(dve):
            V = nc.vector
            st = Steps(dve, dve_step)
            do = st.do

            def unpack_edges(g):
                s, T = sorts[g], g.T
                tg_, sr_, tmp_, cum_ = (a[:, 0:T] for a in (tg, sr, tmp, cum))
                dve.wait_ge(edges_in[g], 64 if g.rest else 32)
                do(V.tensor_scalar(tmp_, tg_, 7, None, ALU.logical_shift_right))
                do(V.tensor_copy(bk[g], tmp_))
                do(V.tensor_scalar(tg_, tg_, P - 1, None, ALU.bitwise_and))
                do(V.tensor_scalar(lo[g], tg_, 1.0, 1 / 2048, ALU.add, ALU.mult))
                do(V.tensor_scalar(sr_, sr_, float(N - 1), None, ALU.min))
                do(V.tensor_scalar(tmp_, sr_, 7, None, ALU.bitwise_and))
                do(V.tensor_scalar(cum_, tmp_, 256 / 2048, None, ALU.mult))
                do(V.tensor_tensor(lo[g], lo[g], cum_, ALU.add))
                do(V.tensor_scalar(tmp_, sr_, 3, None, ALU.logical_shift_right))
                V.tensor_copy(hi[g], tmp_).then_inc(s["unpacked"], 1)

            def count_block(g, b, out=oh):
                st.did(V.tensor_scalar(out[:, 0:g.T], bk[g], iota_b[:, bass.ds(b, 1)], 0.0, ALU.is_equal, ALU.add,
                                       accum_out=cnt[:, bass.ds(b, 1)]))

            def block_offsets(g):
                s = sorts[g]
                V.tensor_copy(off[:], cnt[:]).then_inc(s["offsets"], 1)
                dve.wait_ge(s["sums"], 1)
                do(V.tensor_scalar(tot[:], ps[:, 2, 64:64 + NB], 127.0, None, ALU.add))
                do(V.tensor_scalar(tot[:], tot[:], 7, None, ALU.logical_shift_right))
                do(V.tensor_copy(til[:], tot[:]))
                do(V.tensor_tensor_scan(cumt[:], til[:], til[:], 0.0, ALU.add, ALU.max))
                do(V.tensor_tensor(base[:], cumt[:], til[:], ALU.subtract))
                V.scalar_tensor_tensor(off[:], base[:], float(P), ps[:, 2, 0:NB], ALU.mult, ALU.add
                                       ).then_inc(s["offsets"], 1)
                dve.wait_ge(s["offsets"], 2)
                dve.wait_ge(s["sums"], 2)
                do(V.tensor_copy(bcol[0:NB, :], ps[0:NB, 2, 128:129]))
                V.tensor_scalar(cmpb[0:NB, 0:g.NT], iota_t[0:NB, 0:g.NT], bcol[0:NB, :], None, ALU.is_ge
                                ).then_inc(s["offsets"], 1)
                dve.wait_ge(s["sums"], 3)
                for q, (a, w) in enumerate(g.chunks):
                    blk = ps[0:1, 3 + q, 0:w]
                    if g is CONV:
                        do(V.tensor_scalar(conv_at[:, a + LAG:a + LAG + w], blk, -1.0, float(D), ALU.add, ALU.mult))
                    else:
                        do(V.tensor_scalar(dm_at[:, a:a + w], blk, -1.0, float(2 * GH), ALU.add, ALU.mult))
                        do(V.tensor_scalar(cum[0:1, 0:w], blk, float(PER_BANK), float(BANK - PER_BANK * ROW),
                                           ALU.is_gt, ALU.mult))
                        do(V.tensor_scalar(tmp[0:1, 0:w], blk, -1.0, float(ROW), ALU.add, ALU.mult))
                        do(V.tensor_tensor(sum_at[:, a:a + w], cum[0:1, 0:w], tmp[0:1, 0:w], ALU.add))
                if g is CONV:
                    do(V.memset(conv_at[:, 0:LAG], 0))
                V.memset(signal_word[:], 0.0).then_inc(s["block_known"], 1)
                do(V.memset(pos[:], 0.0))

            def slots_of_block(g, b):
                oh_, cum_, pos_ = oh[:, 0:g.T], cum[:, 0:g.T], pos[:, 0:g.T]
                st.settle()
                st.did(V.tensor_scalar(oh_, bk[g], iota_b[:, bass.ds(b, 1)], None, ALU.is_equal))
                yield
                st.settle()
                st.did(V.tensor_tensor_scan(cum_, oh_, oh_, off[:, bass.ds(b, 1)], ALU.add, ALU.max))
                yield
                hold(dve, dve_step, st.value())
                st.did(V.copy_predicated(pos_, oh_.bitcast(U16), cum_))
                yield

            def split_slots(g):
                T = g.T
                st.settle()
                do(V.tensor_scalar(tmp[:, 0:T], pos[:, 0:T], -1.0, None, ALU.add))
                do(V.tensor_scalar(tg[:, 0:T], tmp[:, 0:T], P - 1, None, ALU.bitwise_and))
                do(V.tensor_copy(slo[g], tg[:, 0:T]))
                do(V.tensor_scalar(tmp[:, 0:T], tmp[:, 0:T], 7, None, ALU.arith_shift_right))
                do(V.tensor_copy(shi[g], tmp[:, 0:T]))

            def stage_scatter(g, i):
                s = sorts[g]
                col = bass.ds(i * g.per_turn + g.placed, SCAT)
                dve.wait_ge(s["scat_free"], i + 1)
                V.tensor_tensor(scat_val[:], hi[g][:, col], lo[g][:, col], ALU.add)
                st.did(V.scalar_tensor_tensor(scat_tmp[:], shi[g][:, col], 0.0, scat_past[:], ALU.is_lt, ALU.mult))
                st.did(V.scalar_tensor_tensor(scat_col[:], slo[g][:, col], float(g.NT + 1), shi[g][:, col],
                                              ALU.mult, ALU.add))
                st.settle()
                V.tensor_tensor(scat_at[:], scat_col[:], scat_tmp[:], ALU.add).then_inc(s["scat_staged"], 1)

            def place_column(g, i, k):
                s = sorts[g]
                col = bass.ds(i * g.per_turn + k, 1)
                dve.wait_ge(s["placed"], i * g.placed + (k + 1))
                V.tensor_scalar(slot1h[k % RING][:, 0:g.NT], iota_t[:, 0:g.NT], shi[g][:, col], None,
                                ALU.is_equal).then_inc(s["onehots"], 1)
                V.tensor_scalar(lo1h[k % RING][:], iota_p[:], slo[g][:, col], None, ALU.is_equal
                                ).then_inc(s["onehots"], 1)

            def take_sorted(g):
                s = sorts[g]
                V.memset(signal_word[:], 0.0).then_inc(s["back_ready"], 1)
                dve.wait_ge(s["placed"], g.placed * g.turns + RING + 1)
                dve.wait_ge(s["back_in"], 16)
                for q, (a, w) in enumerate(g.chunks):
                    do(V.tensor_tensor(cum[:, a:a + w], ps[:, q, 0:w], cum[:, a:a + w], ALU.add))
                do(V.tensor_scalar(cum[:, 0:g.NT], cum[:, 0:g.NT], 2048.0, None, ALU.mult))
                do(V.tensor_copy(idx[g][:, 0:g.NT], cum[:, 0:g.NT]))
                for a, w in g.chunks:
                    do(V.tensor_scalar(tmp[:, 0:w], idx[g][:, a:a + w], 255, None, ALU.bitwise_and))
                    do(V.tensor_scalar(dlo[g][:, a:a + w], tmp[:, 0:w], -1.0, None, ALU.add))
                V.tensor_scalar(idx[g][:, 0:g.NT], idx[g][:, 0:g.NT], 8, None, ALU.logical_shift_right
                                ).then_inc(s["sorted"], 1)

            def layernorm_stats(n):
                dve_s = stat.rearrange("p (t s) -> p t s", s=6)
                with dve.Fori(0, NB // 7) as u:
                    st.enter(u, 7)
                    for k in range(7):
                        st.did(V.bn_stats(stat[:, bass.ds(u * 42 + k * 6, 6)], nodes(x_sb, u * 7 + k)))
                st.leave(NB // 7, 7)
                st.settle()
                me, mo, ve, vo = dve_s[:, :, 1], dve_s[:, :, 4], dve_s[:, :, 2], dve_s[:, :, 5]
                do(V.tensor_tensor(st1[:], me, mo, ALU.add))
                do(V.tensor_scalar(mean[:], st1[:], 0.5, None, ALU.mult))
                do(V.tensor_tensor(st1[:], me, mo, ALU.subtract))
                do(V.tensor_scalar(st1[:], st1[:], 0.5, None, ALU.mult))
                do(V.tensor_tensor(st1[:], st1[:], st1[:], ALU.mult))
                do(V.tensor_tensor(st2[:], ve, vo, ALU.add))
                do(V.tensor_scalar(st2[:], st2[:], 1 / D, EPS, ALU.mult, ALU.add))
                V.tensor_tensor(var[:], st2[:], st1[:], ALU.add).then_inc(var_ready[n], 1)
                dve.wait_ge(std_ready[n], 1)
                do(V.reciprocal(rstd[:], st2[:]))

            def normalise(out, t):
                return V.tensor_scalar(out, nodes(x_sb, t), mean[:, bass.ds(t, 1)], rstd[:, bass.ds(t, 1)],
                                       ALU.subtract, ALU.mult)

            dve.wait_ge(const_ready, CONSTS)
            unpack_edges(CONV)
            spare = pos[:, 0:TM // 2].bitcast(F16)
            do(V.memset(spare, 0.0))
            with dve.Fori(0, NB // 7) as u:
                st.enter(u, 7)
                for k in range(7):
                    if k:
                        st.after(st.value() + -1)
                    else:
                        st.settle()
                    count_block(CONV, u * 7 + k, (oh, spare)[k % 2])
            st.leave(NB // 7, 7)
            st.settle()
            block_offsets(CONV)
            dve.wait_ge(x_in, 32)
            layernorm_stats(0)
            unpack_edges(GAT)
            dve.wait_ge(sorts[GAT]["unpacked"], 1)

            normalise(xn, 0).then_inc(xn_ready, 1)

            def elu_parts(t, last=False):
                if not last:
                    dve.wait_ge(xt_psum, t + 1)
                    normalise(xn, t + 1).then_inc(xn_ready, 1)
                for _ in slots_of_block(CONV, t):
                    pass
                st.settle()
                dve.wait_ge(kexp_ready, t + 1)
                do(V.tensor_scalar(kexp, kexp, 1.0, None, ALU.min))
                dve.wait_ge(ctx_used, t + 1)
                dve.wait_ge(v_ready, t + 1)
                V.scalar_tensor_tensor(kk, ps[:, 5, 0:D], 0.0, kexp, ALU.max, ALU.add).then_inc(k_ready, 1)
                count_block(GAT, t)
                dve.wait_ge(qexp_ready, t + 1)
                do(V.tensor_scalar(qexp, qexp, 1.0, None, ALU.min))
                dve.wait_ge(q_free, t + 1)
                V.scalar_tensor_tensor(qq, ps[:, 7, 0:D], 0.0, qexp, ALU.max, ALU.add).then_inc(q_ready, 1)

            with dve.Fori(0, NB - 1) as t:
                st.enter(t, 6)
                elu_parts(t)
            st.leave(NB - 1, 6)
            elu_parts(NB - 1, last=True)
            split_slots(CONV)
            block_offsets(GAT)

            dve.wait_ge(ctx_done, 1)
            for c in range(C):
                do(V.tensor_tensor(cbt[:, c * P:(c + 1) * P], ps[:, 6, c * P:(c + 1) * P], headmask[:], ALU.mult))
                do(V.tensor_scalar(ks[:, c * P:(c + 1) * P], headmask[:], ps[:, 6, 256 + c:257 + c], None, ALU.mult))
            V.memset(signal_word[:], 0.0).then_inc(ctx_masked, 1)
            dve.wait_ge(cp_psum, 1)
            V.tensor_copy(cpw[:, 0:D], ps[:, 3, 0:D]).then_inc(cp_ready, 1)
            V.tensor_copy(cpw[:, D:], ps[:, 7, 0:D]).then_inc(cp_ready, 1)
            dve.sem_inc(qn_ready, 1)

            for g in (CONV, GAT):
                dve.sem_inc(sorts[g]["scat_free"], 1)
            with dve.Fori(0, NB) as t:
                st.enter(t, 5)
                slots = slots_of_block(GAT, t)
                stage_scatter(CONV, t)
                for k in range(CONV.placed):
                    place_column(CONV, t, k)
                    if k in (1, 5, 9):
                        next(slots)
            st.leave(NB, 5)
            take_sorted(CONV)
            split_slots(GAT)

            dve.wait_ge(msg_stored, 16 * NB)
            dve.wait_ge(q_stored, 16 * NB)
            dve.sem_inc(conv_added, RING - LAG)
            dve.sem_inc(at_added, 1)

            def conv_onehot(i, k):
                dve.wait_ge(conv_psum, i * G + (k + 1))
                V.tensor_scalar(oh1[k % RING], iota_p[:], dlo[CONV][:, bass.ds(i * G + k, 1)], None,
                                ALU.is_equal).then_inc(conv_oh, 1)

            def conv_add(i, k, at):
                dst = acc[:, bass.ds(at, D)]
                dve.wait_ge(conv_psum, i * G + (k + 1 + RING))
                dve.wait_ge(conv_added, i * G + (k + RING))
                V.tensor_tensor(dst, dst, ps[:, 4 + k % RING, 0:D], ALU.add).then_inc(conv_added, 1)

            def conv_turn(i, attention):
                ats = columns(DVE, conv_at, i * G, G, (NB - 1) * D)
                sorted_ = 0
                for k in range(G):
                    conv_onehot(i, k + 2)
                    if k == 2:
                        stage_scatter(GAT, i)
                    while sorted_ < GAT.placed * (k + 1) // G:
                        place_column(GAT, i, sorted_)
                        sorted_ += 1
                    conv_add(i, k - LAG, ats[k])
                    if attention and k == 4:
                        dve.wait_ge(den_psum, i + 1)
                        st.did(V.tensor_scalar(xn, ps[:, 3, 0:D], 1e-6, None, ALU.max))
                    if attention and k in (5, 6, 7, 8):
                        part_ = xn[:, (k - 5) * 64:(k - 4) * 64]
                        st.settle()
                        st.did(V.reciprocal(part_, part_))
                    if attention and k == 9:
                        st.settle()
                        dve.wait_ge(q_back, i * 16 + 16)
                        V.tensor_tensor(kk, qexp, xn, ALU.mult).then_inc(qn_ready, 1)
                    if attention and k == 14:
                        dve.wait_ge(at_psum, i + 1)
                        V.tensor_tensor(nodes(x_sb, i), nodes(x_sb, i), ps[:, 3, 0:D], ALU.add).then_inc(at_added, 1)

            conv_onehot(0, 0)
            conv_onehot(0, 1)
            with dve.Fori(0, NB) as i:
                st.enter(i, 7)
                conv_turn(i, True)
            st.leave(NB, 7)
            with dve.Fori(0, GAT.turns - NB) as i:
                st.enter(i, 2)
                conv_turn(i + NB, False)
            st.leave(GAT.turns - NB, 2)
            last_at = columns(DVE, conv_at, CONV.NT, LAG, (NB - 1) * D)
            for j in range(LAG):
                conv_add(0, CONV.NT - LAG + j, last_at[j])
            dve.wait_ge(conv_added, CONV.NT + RING)
            dve.wait_ge(at_added, NB + 1)
            V.scalar_tensor_tensor(x_sb[:], acc, 0.0, x_sb[:], ALU.max, ALU.add).then_inc(x2_ready, 1)

            take_sorted(GAT)
            dve.wait_ge(x2_ready, 1)
            layernorm_stats(1)

            def normalise_x2(t, k):
                dve.wait_ge(xt2_psum, t + 1)
                normalise(xn2[k], t).then_inc(xn2_ready, 1)

            with dve.Fori(0, NB // RING) as u:
                for k in range(RING):
                    normalise_x2(u * RING + k, k)
            normalise_x2(NB - 1, 0)
            dve.wait_ge(h_psum, NB + RING)
            hr = hrow.rearrange("p (t r) -> p t r", r=ROW)
            split = BANK // HW
            for q, (a, b) in enumerate(((0, split), (split, NB))):
                do(V.tensor_copy(hr[:, a:b, 0:HW], ps[:, q, 0:(b - a) * HW].rearrange("p (t r) -> p t r", r=HW)))
            dve.wait_ge(small_in, 16 * 6)
            tmp3 = ad_tmp.rearrange("p (t r) -> p t r", r=HW)
            tmp4 = ad_tmp.rearrange("p (t h c) -> p t h c", h=GH, c=GC)
            dm2 = dm.rearrange("p (t r) -> p t r", r=2 * GH)

            def param(k):
                return smalls[:, k * HW:(k + 1) * HW].rearrange("p (a r) -> p a r", a=1).broadcast_to((P, NB, HW))

            for k, dst in ((0, hr[:, :, HW:ROW]), (1, dm2[:, :, 0:GH])):
                do(V.tensor_tensor(tmp3, hr[:, :, 0:HW], param(k), ALU.mult))
                do(V.tensor_reduce(dst, tmp4, AX.X, ALU.add))
            V.tensor_copy(dm2[:, :, GH:], hr[:, :, HW:ROW]).then_inc(hrow_ready, 1)
            dve.wait_ge(hrow_ready, 1)

            dve.sem_inc(max_taken, 2 * RING)

            def not_target(at, k):
                V.tensor_scalar(nohb[k % RING], iota_p[:], dlo[GAT][:, bass.ds(at, 1)], 1.0,
                                ALU.is_equal, ALU.subtract).then_inc(gat_noh, 1)

            for k in range(RING):
                not_target(k, k)
            dve.wait_ge(b2_in, 16)
            one = [ident[0:PARTS, q:q + 1] for q in range(PARTS)]
            do(V.tensor_copy(part_tmp[0], b2_f))
            do(V.tensor_tensor(b2_f, b2_f, part_tmp[0], ALU.subtract))
            do(V.tensor_copy(part_tmp[1], b2_f))
            do(V.tensor_tensor(b2_f, b2_f, part_tmp[1], ALU.subtract))
            do(V.tensor_scalar(b2_b, b2_f, one[2], None, ALU.mult))
            do(V.scalar_tensor_tensor(b2_b, part_tmp[0], one[0], b2_b, ALU.mult, ALU.add))
            V.scalar_tensor_tensor(b2_b, part_tmp[1], one[1], b2_b, ALU.mult, ALU.add).then_inc(b2_ready, 1)
            with dve.Fori(0, GAT.NT // G) as i:
                ats = columns(DVE, dm_at, i * G, G, dm_most)
                for k in range(G):
                    m4 = mx[:, (k % RING) * GH:(k % RING + 1) * GH]
                    dst = dm[:, bass.ds(ats[k] + GH, GH)]
                    dve.wait_ge(max_psum, i * G + (k + 1 + G))
                    V.tensor_reduce(m4, ps[:, 4 + k % RING, :].rearrange("p (h e) -> p h e", h=GH), AX.X,
                                    ALU.max).then_inc(max_taken, 1)
                    not_target(i * G + (k + RING), k)
                    dve.wait_ge(max_taken, i * (2 * G) + (2 * k + 1 + 2 * RING))
                    V.tensor_tensor(dst, dst, m4, ALU.max).then_inc(max_taken, 1)
            dve.wait_ge(max_taken, 2 * GAT.NT + 2 * RING)
            t4 = ad_tmp[:, 0:NB * GH].rearrange("p (t h) -> p t h", h=GH)
            do(V.tensor_tensor(t4, dm2[:, :, GH:], dm2[:, :, 0:GH], ALU.add))
            do(V.scalar_tensor_tensor(dm2[:, :, GH:], t4, 0.2, t4, ALU.mult, ALU.max))
            do(V.tensor_tensor(t4, hr[:, :, HW:ROW], dm2[:, :, 0:GH], ALU.add))
            do(V.scalar_tensor_tensor(t4, t4, 0.2, t4, ALU.mult, ALU.max))
            do(V.tensor_tensor(t4, t4, dm2[:, :, GH:], ALU.subtract))
            w = NB * 2 * GH
            rest = dm_rest
            do(V.tensor_copy(dmb[:, 0:w], dm))
            do(V.tensor_tensor(rest, dm, dmb[:, 0:w], ALU.subtract))
            do(V.tensor_copy(dmb[:, w:2 * w], rest))
            V.tensor_tensor(dmb[:, 2 * w:], rest, dmb[:, w:2 * w], ALU.subtract).then_inc(dm_ready, 1)
            dve.wait_ge(self_e, 1)

            z3, e3 = ([a.rearrange("p (j h) -> p j h", h=GH) for a in b] for b in (zz, ee))
            mg = [a.rearrange("p (j r) -> p j r", r=ROW) for a in msg]
            dmp = [ps[:, 6 + k, 0:HALF * PARTS * 2 * GH].rearrange("p (j q r) -> p j r q", q=PARTS, r=2 * GH)
                   for k in range(2)]
            ds3 = [a.rearrange("p (j r) -> p j r", r=2 * GH) for a in dsum]
            part = [[a[:, q * HALF * ROW:(q + 1) * HALF * ROW] for q in range(PARTS)] for a in msgb3]

            def onehots(b, at, ks):
                for k in ks:
                    ins = V.tensor_scalar(ohb[at % OH_RING][:, k * P:(k + 1) * P], iota_p[:],
                                          dlo[GAT][:, bass.ds(b * HALF + k, 1)], None, ALU.is_equal)
                if HALF - 1 in ks:
                    ins.then_inc(oh_ready, 1)

            def rows_of(b):
                return rows_all[:, bass.ds(b * (HALF * ROW), HALF * ROW)].rearrange("p (j r) -> p j r", r=ROW)

            def exponents(b, at):
                z, d = z3[at % 2], ds3[at % 2]
                dve.wait_ge(dm_psum, b + 1)
                v = st.note(V.tensor_reduce(d, dmp[at % 2], AX.X, ALU.add))
                yield
                st.after(v)
                v = st.note(V.tensor_tensor(z, rows_of(b)[:, :, HW:ROW], d[:, :, 0:GH], ALU.add))
                yield
                st.after(v)
                v = st.note(V.scalar_tensor_tensor(z, z, 0.2, z, ALU.mult, ALU.max))
                yield
                st.after(v)
                V.tensor_tensor(z, z, d[:, :, GH:], ALU.subtract).then_inc(z_ready, 1)
                yield

            def messages(b, at):
                e, m, (hi_, mid_, lo_) = e3[at % 2], mg[at % 2], part[at % 2]
                flat_m = msg[at % 2]
                dve.wait_ge(ee_ready, b + 1)
                V.tensor_copy(m[:, :, HW:ROW], e)
                v = st.note(V.tensor_tensor(m[:, :, 0:HW].rearrange("p j (h c) -> p j h c", h=GH),
                                            rows_of(b)[:, :, 0:HW].rearrange("p j (h c) -> p j h c", h=GH),
                                            e.rearrange("p j (h a) -> p j h a", a=1).broadcast_to((P, HALF, GH, GC)),
                                            ALU.mult))
                yield
                st.after(v)
                v = st.note(V.tensor_copy(hi_, flat_m))
                yield
                st.after(v)
                v = st.note(V.tensor_tensor(flat_m, flat_m, hi_, ALU.subtract))
                yield
                st.after(v)
                v = st.note(V.tensor_copy(mid_, flat_m))
                yield
                st.after(v)
                V.tensor_tensor(lo_, flat_m, mid_, ALU.subtract).then_inc(m_ready, 1)
                yield

            def pass2_step(b, at, first=False, last=False):
                z_steps = exponents(b, at)
                next(z_steps)
                dve.wait_ge(sum_done, b + 1)
                m_steps = messages(b - 1, at - 1) if not first else iter(())
                for _ in range(3):
                    next(m_steps, None)
                    next(z_steps)
                next(m_steps, None)
                more = not last or at + 3 < HALVES
                if more:
                    onehots(b + 3, at + 3, range(HALF // 2))
                next(m_steps, None)
                if more:
                    onehots(b + 3, at + 3, range(HALF // 2, HALF))

            for b in range(3):
                onehots(b, b, range(HALF))
            for b in range(2):
                pass2_step(b, b, first=(b == 0))
            with dve.Fori(0, PASS2_TURNS) as u:
                st.enter(u, 7 * OH_RING)
                for k in range(OH_RING):
                    pass2_step(u * OH_RING + (k + 2), k + 2)
            st.leave(PASS2_TURNS, 7 * OH_RING)
            for b in range(2 + PASS2_TURNS * OH_RING, HALVES):
                pass2_step(b, b, last=True)
            dve.wait_ge(sum_done, HALVES + 1)
            for _ in messages(HALVES - 1, HALVES - 1):
                pass

            dve.wait_ge(sum_done, HALVES + 3)
            es3, den3 = (a.rearrange("p (t h) -> p t h", h=GH) for a in (eself, den))

            def spread(ap):
                return ap.rearrange("p t (h a) -> p t h a", a=1).broadcast_to((P, NB, GH, GC))

            do(V.tensor_tensor(tmp4, hr[:, :, 0:HW].rearrange("p t (h c) -> p t h c", h=GH), spread(es3), ALU.mult))
            for q, (a, b) in enumerate(((0, PER_BANK), (PER_BANK, NB))):
                sums = ps[:, q, 0:(b - a) * ROW].rearrange("p (t r) -> p t r", r=ROW)
                do(V.tensor_tensor(tmp3[:, a:b], tmp3[:, a:b], sums[:, :, 0:HW], ALU.add))
                do(V.tensor_tensor(den3[:, a:b], es3[:, a:b], sums[:, :, HW:ROW], ALU.add))
            do(V.tensor_scalar(den, den, 1e-16, None, ALU.add))
            do(V.reciprocal(den, den))
            do(V.tensor_tensor(tmp4, tmp4, spread(den3), ALU.mult))
            do(V.tensor_tensor(tmp3, tmp3, param(2), ALU.add))

            def per_node(ap):
                return ap.rearrange("p (t a) -> p t a", a=1).broadcast_to((P, NB, HW))

            sq = hrow[:, 0:NB * HW]
            do(V.tensor_reduce(st1[:], tmp3, AX.X, ALU.add))
            do(V.tensor_scalar(st1[:], st1[:], 1 / HW, None, ALU.mult))
            do(V.tensor_tensor(tmp3, tmp3, per_node(st1[:]), ALU.subtract))
            do(V.tensor_tensor(sq, ad_tmp, ad_tmp, ALU.mult))
            do(V.tensor_reduce(st2[:], sq.rearrange("p (t r) -> p t r", r=HW), AX.X, ALU.add))
            V.tensor_scalar(st2[:], st2[:], 1 / HW, EPS, ALU.mult, ALU.add).then_inc(gvar, 1)
            dve.wait_ge(gstd, 1)
            do(V.reciprocal(st1[:], st1[:]))
            do(V.tensor_tensor(tmp3, tmp3, per_node(st1[:]), ALU.mult))
            do(V.tensor_tensor(tmp3, tmp3, param(3), ALU.mult))
            do(V.tensor_tensor(tmp3, tmp3, param(4), ALU.add))
            do(V.tensor_reduce(den3, ad_tmp.rearrange("p (t h c) -> p t c h", h=GH, c=GC), AX.X, ALU.add))
            do(V.tensor_scalar(den, den, 1 / GH, None, ALU.mult))
            do(V.tensor_reduce(st1[:], den3, AX.X, ALU.max))
            ex3 = es3
            do(V.tensor_tensor(ex3, den3, st1[:].rearrange("p (t a) -> p t a", a=1).broadcast_to((P, NB, GH)),
                               ALU.subtract))
            V.memset(signal_word[:], 0.0).then_inc(gate_z, 1)
            rank = hrow[:, 0:NB * NE].rearrange("p (t e) -> p t e", e=NE)
            do(V.memset(hrow[:, 0:NB * NE], 0.0))
            for e in range(NE):
                for j in range(NE):
                    if j != e:
                        do(V.tensor_tensor(st2[:], den3[:, :, j], den3[:, :, e], ALU.is_ge if j < e else ALU.is_gt))
                        do(V.tensor_tensor(rank[:, :, e], rank[:, :, e], st2[:], ALU.add))
            g3 = gate.rearrange("p (t e) -> p t e", e=NE)
            dve.wait_ge(gate_e, 1)
            do(V.scalar_tensor_tensor(g3, rank, 2.0, ex3, ALU.is_lt, ALU.mult))
            do(V.tensor_reduce(st1[:], g3, AX.X, ALU.add))
            do(V.reciprocal(st1[:], st1[:]))
            do(V.tensor_tensor(g3, g3, st1[:].rearrange("p (t a) -> p t a", a=1).broadcast_to((P, NB, NE)), ALU.mult))

            dve.sem_inc(y_taken, 2)

            def weigh(out, term, t, e):
                return V.scalar_tensor_tensor(out, term, gate[:, bass.ds(t * NE + e, 1)], out, ALU.mult, ALU.add)

            def combine_pair(n, k, loads):
                dve.wait_ge(back_in[k], loads)
                before_ = [None, None]
                for e in range(NE):
                    for j in range(2):
                        out = res[k][:, j * D:(j + 1) * D]
                        if e:
                            st.after(before_[j])
                        ins = weigh(out, y_back[k][:, (j * NE + e) * D:(j * NE + e + 1) * D], n * 2 + j, e)
                        if e < NE - 1:
                            before_[j] = st.note(ins)
                        else:
                            ins.then_inc(combined, 1)

            def late_term(v, e):
                n = v * NE + e
                dve.wait_ge(y_psum, n + 3)
                if e:
                    dve.wait_ge(y_taken, n + 2)
                weigh(res_late[v % 2], ps[:, 6 + e % 2, 0:D], v + EARLY, e).then_inc(y_taken, 1)

            for v in range(LATE):
                dve.wait_ge(late_in[v % 2], 16 * (v // 2 + 1))
                for k in range(FIN):
                    combine_pair(v * FIN + k, k, 32 * (v + 1))
                    late_term(v, k)
            for k in range(FIN_TAIL):
                combine_pair(LATE * FIN + k, k, 32 * (LATE + 1))

        @block.scalar
        def _(act):
            A = nc.scalar.activation

            def std(n):
                act.wait_ge(var_ready[n], 1)
                A(st2[:], var[:], ACT.Sqrt).then_inc(std_ready[n], 1)

            std(0)

            def take_xt(at_least):
                act.wait_ge(xt_psum, at_least)
                A(xnT, ps[:, 3, 0:D], ACT.Copy).then_inc(xt_ready, 1)

            act.wait_ge(zeros_in, 32)
            take_xt(1)

            def take_block(t, last=False):
                act.wait_ge(kv_psum, t + 1)
                act.wait_ge(ctx_used, t + 1)
                A(kexp, ps[:, 5, 0:D], ACT.Exp).then_inc(kexp_ready, 1)
                A(vv, ps[:, 5, D:2 * D], ACT.Copy).then_inc(v_ready, 1)
                hold(act, w_psum, t + 1)
                A(nodes(acc, t), ps[:, 4, 0:D], ACT.Copy)
                act.wait_ge(msg_free, t + 1)
                A(msgb, ps[:, 4, D:2 * D], ACT.Copy).then_inc(msg_ready, 1)
                act.wait_ge(q_psum, t + 1)
                A(qexp, ps[:, 7, 0:D], ACT.Exp).then_inc(qexp_ready, 1)
                if not last:
                    take_xt(t + 2)

            with act.Fori(0, NB - 1) as t:
                take_block(t)
            take_block(NB - 1, last=True)

            def scale_column(g, i, k):
                s = sorts[g]
                col = bass.ds(i * g.per_turn + k, 1)
                hold(act, s["onehots"], i * (2 * g.placed) + 2 * (k + 1))
                A(put_hi[k % RING][:], lo1h[k % RING][:], ACT.Copy, scale=hi[g][:, col])
                A(put_lo[k % RING][:], lo1h[k % RING][:], ACT.Copy, scale=lo[g][:, col]).then_inc(s["puts"], 1)

            with act.Fori(0, NB) as t:
                for k in range(CONV.placed):
                    scale_column(CONV, t, k)

            act.wait_ge(cp_ready, 2)
            act.wait_ge(q_stored, 16 * NB)
            act.wait_ge(sorts[CONV]["sorted"], 1)

            def stage(st_, g, h, at, staged):
                A(st_[:, h * HALF:(h + 1) * HALF], idx[g][:, bass.ds(at, HALF)], ACT.Copy).then_inc(staged, 1)

            for h in range(2):
                stage(st_conv, CONV, h, h * HALF, conv_staged)
            with act.Fori(0, GAT.turns) as i:
                for k in range(GAT.placed):
                    scale_column(GAT, i, k)
                    for h in range(2):
                        if k == (h + 1) * GAT.placed // 2 - 1:
                            hold(act, conv_psum, i * G + ((h + 1) * HALF + RING))
                            stage(st_conv, CONV, h, i * G + (G + h * HALF), conv_staged)

            act.wait_ge(small_in, 16 * 6)
            std(1)

            def take_xt2(t, k):
                act.wait_ge(xt2_psum, t + (RING + 1))
                act.wait_ge(xt2_free, t + 1)
                act.wait_ge(h_psum, t + 1)
                A(xnT2[k], ps[:, 3 + k, 0:D], ACT.Copy).then_inc(xt2_ready, 1)

            with act.Fori(0, NB // RING) as u:
                for k in range(RING):
                    take_xt2(u * RING + k, k)
            take_xt2(NB - 1, 0)
            act.wait_ge(hrow_ready, 1)
            for h in range(2):
                stage(st_gat, GAT, h, h * HALF, gat_staged)
            rg3 = rg.rearrange("p (j r) -> p j r", r=ROW)
            sb3 = sbf.rearrange("p (j h) -> p j h", h=GH)

            def keep_rows(i, h):
                for k in range(h * HALF, (h + 1) * HALF):
                    hold(act, row_in[k], i * 16 + 16 * (CONV.NT // G + 1))
                w = HALF * ROW
                A(rows_all[:, bass.ds(i * (G * ROW) + h * w, w)], rg[:, h * w:(h + 1) * w], ACT.Copy)
                act.wait_ge(max_psum, i * G + (h + 1) * HALF)
                A(sb3[:, h * HALF:(h + 1) * HALF, :], rg3[:, h * HALF:(h + 1) * HALF, HW:ROW],
                  ACT.Copy).then_inc(gat_kept, 1)
                stage(st_gat, GAT, h, i * G + (G + h * HALF), gat_staged)

            def gelus(par, bank, e):
                for c in range(FC):
                    ins = A(hT[:, par * F + c * P:par * F + (c + 1) * P],
                            ps[:, bank, c * P:(c + 1) * P], ACT.Gelu, bias=b1_col[:, e * FC + c:e * FC + c + 1])
                return ins

            def keep_expert(e, n):
                hold(act, early_y, n)
                A(y_out[:, e * D:(e + 1) * D], ps[:, 3, 0:D], ACT.Copy).then_inc(early_kept, 1)

            events = sorted([(8 * h - 2.5, "rows", h) for h in range(6)] + [(6 * j + 3, "gelu", j) for j in range(2 * NE)]
                            + [(6 * j, "keep", j) for j in range(2 * NE)])
            with act.Fori(0, PASS1_TURNS // 3) as u:
                for _, what, j in events:
                    if what == "rows":
                        keep_rows(u * 3 + j // 2, j % 2)
                    elif what == "keep":
                        if j % NE == 1:
                            act.wait_ge(early_free, u * 2 + (j // NE + 1))
                        keep_expert((j - 1) % NE, u * (2 * NE) + (j + 1))
                    else:
                        act.wait_ge(early_hid, u * (2 * NE) + (j + 1))
                        gelus(0, 2, j % NE).then_inc(early_act, 1)
            keep_rows(PASS1_TURNS - 1, 0)
            keep_expert(NE - 1, EARLY * NE + 1)
            keep_rows(PASS1_TURNS - 1, 1)
            act.wait_ge(dm_ready, 1)
            A(eself, ad_tmp[:, 0:NB * GH], ACT.Exp).then_inc(self_e, 1)

            def copy_turned(b, at):
                act.wait_ge(ohT_psum, b + 1)
                if at >= 2:
                    act.wait_ge(dm_psum, b - 1)
                A(ohT[at % 2], ps_b[:, 2 + at % 2, :], ACT.Copy).then_inc(ohT_ready, 1)

            def exps(b, at):
                act.wait_ge(z_ready, b + 2)
                A(ee[at % 2], zz[at % 2], ACT.Exp).then_inc(ee_ready, 1)

            copy_turned(0, 0)
            copy_turned(1, 1)
            with act.Fori(0, HALVES // 2 - 1) as u:
                for k in range(2):
                    copy_turned(u * 2 + (k + 2), k + 2)
                    exps(u * 2 + k, k)
            for b in range(HALVES - 2, HALVES):
                exps(b, b)
            act.wait_ge(gvar, 1)
            A(st1[:], st2[:], ACT.Sqrt).then_inc(gstd, 1)
            act.wait_ge(gate_z, 1)
            A(eself, eself, ACT.Exp).then_inc(gate_e, 1)

            with act.Fori(0, LATE) as t:
                for e in range(NE):
                    act.wait_ge(hid_psum, t * NE + (e + 1))
                    act.wait_ge(y_psum, t * NE + (e + 1))
                    gelus(e % 2, 4 + e % 2, e).then_inc(hid_ready, 1)

        @block.tensor
        def _(pe):
            M = nc.tensor.matmul

            def transposed(src, bank=3):
                for c in range(C):
                    ins = nc.tensor.transpose(ps[:, bank, c * P:(c + 1) * P], src[:, c * P:(c + 1) * P], ident[:])
                return ins

            def chunks(out, left, right):
                for c in range(C):
                    ins = M(out, left[c], right[c], start=(c == 0), stop=(c == C - 1))
                return ins

            def cut(ap, w):
                return [ap[:, c * w:(c + 1) * w] for c in range(C)]

            def sort_offsets(g):
                s = sorts[g]
                pe.wait_ge(s["offsets"], 1)
                M(ps[:, 2, 0:NB], before[:], cnt[:], start=True, stop=True)
                M(ps[:, 2, 64:64 + NB], ones[:], cnt[:], start=True, stop=True).then_inc(s["sums"], 1)
                pe.wait_ge(s["offsets"], 2)
                M(ps[0:NB, 2, 128:129], base[0:1, :], ones[0:1, 0:1], start=True, stop=True).then_inc(s["sums"], 1)
                pe.wait_ge(s["offsets"], 3)
                for q, (a, w) in enumerate(g.chunks):
                    ins = M(ps[0:1, 3 + q, 0:w], ones16[0:NB, 0:1], cmpb[0:NB, a:a + w], start=True, stop=True)
                ins.then_inc(s["sums"], 1)

            def clear(bank, w):
                return M(ps[:, bank, 0:w], zero16[:], iota_t[:, 0:w], start=True, stop=False, skip_group_check=True)

            def sort_begin(g):
                pe.sem_inc(sorts[g]["placed"], RING)
                for q, (a, w) in enumerate(g.chunks):
                    clear(q, w)

            def place_column(g, i, k):
                s = sorts[g]
                pe.wait_ge(s["puts"], i * g.placed + (k + 1))
                for put in (put_hi[k % RING], put_lo[k % RING]):
                    for q, (a, w) in enumerate(g.chunks):
                        ins = M(ps[:, q, 0:w], put[:], slot1h[k % RING][:, a:a + w], start=False, stop=False,
                                skip_group_check=True)
                ins.then_inc(s["placed"], 1)

            def sort_end(g):
                M(ps[:, 0, 0:1], zero16[:], iota_t[:, 0:1], start=False, stop=True,
                  skip_group_check=True).then_inc(sorts[g]["placed"], 1)

            pe.wait_ge(const_ready, CONSTS)
            sort_offsets(CONV)

            pe.wait_ge(w_in, 16 * 6)
            pe.wait_ge(sorts[CONV]["block_known"], 1)
            M(ps[:, 6, :], zero16[:], iota_t[:, 0:BANK], start=True, stop=False, skip_group_check=True)
            pe.sem_inc(ctx_used, 1)
            pe.wait_ge(xn_ready, 1)
            transposed(xn).then_inc(xt_psum, 1)

            def project(t, rows_, last=False):
                pe.wait_ge(xt_ready, t + 1)
                chunks(ps[:, 5, :], cut(xnT, P), cut(w_kv, 512)).then_inc(kv_psum, 1)
                pe.wait_ge(msg_ready, t + 1)
                chunks(ps[:, 4, :], cut(xnT, P), cut(w_wk, 512)).then_inc(w_psum, 1)
                pe.wait_ge(q_ready, t + 1)
                for o in range(C):
                    ins = chunks(ps[:, 7, o * P:(o + 1) * P],
                                 [w_q[:, c * D + o * P:c * D + (o + 1) * P] for c in range(C)], cut(xnT, P))
                ins.then_inc(q_psum, 1)
                if not last:
                    pe.wait_ge(xn_ready, t + 2)
                    transposed(xn).then_inc(xt_psum, 1)
                pe.wait_ge(k_ready, t + 1)
                pe.wait_ge(v_ready, t + 1)
                for c in range(C):
                    one = slice(c * P, (c + 1) * P)
                    M(ps[:, 6, c * P:(c + 1) * P], vv[0:rows_, one], kk[0:rows_, one], start=False, stop=last,
                      skip_group_check=True)
                    ins = M(ps[:, 6, 256 + c:257 + c], kk[0:rows_, one], ones[0:rows_, 0:1], start=False, stop=last,
                            skip_group_check=True)
                ins.then_inc(ctx_used, 1)

            pe.sem_inc(msg_ready, 1)
            pe.sem_inc(q_ready, 1)
            with pe.Fori(0, NB - 1) as t:
                project(t, P)
            project(NB - 1, TAIL, last=True)
            pe.wait_ge(ctx_used, NB + 1)
            pe.sem_inc(ctx_done, 1)

            sort_offsets(GAT)

            pe.wait_ge(ctx_masked, 1)
            M(ps[:, 3, 0:D], cbt[:, 0:P], w_p[:, 0:D], start=True, stop=True)
            M(ps[:, 7, 0:D], cbt[:, P:2 * P], w_p[:, D:2 * D], start=True, stop=True).then_inc(cp_psum, 1)
            sort_begin(CONV)
            with pe.Fori(0, NB) as t:
                for k in range(CONV.placed):
                    place_column(CONV, t, k)
            sort_end(CONV)
            pe.wait_ge(cp_ready, 2)
            pe.wait_ge(sorts[CONV]["sorted"], 1)

            sort_begin(GAT)
            for j in range(LAG):
                M(ps[:, 4 + RING - 1 - j, 0:D], zero16[:], iota_t[:, 0:D], start=True, stop=True).then_inc(conv_psum, 1)
            pe.wait_ge(conv_psum, LAG)
            pe.sem_inc(conv_psum, RING - LAG)

            def conv_turn(i, attention):
                sorted_ = 0
                for k in range(G):
                    pe.wait_ge(conv_oh, i * G + (k + 1))
                    pe.wait_ge(row_in[k], i * 16 + 16)
                    pe.wait_ge(conv_added, i * G + (k + 1))
                    M(ps[:, 4 + k % RING, 0:D], oh1[k % RING], rows[:, k * D:(k + 1) * D], start=True,
                      stop=True).then_inc(conv_psum, 1)
                    if attention and k == 1:
                        pe.wait_ge(q_back, i * 16 + 16)
                        pe.wait_ge(at_added, i + 1)
                        for c in range(C):
                            ins = M(ps[:, 3, c * P:(c + 1) * P], ks[:, c * P:(c + 1) * P],
                                    qexp[:, c * P:(c + 1) * P], start=True, stop=True)
                        ins.then_inc(den_psum, 1)
                    if attention and k == 11:
                        pe.wait_ge(qn_ready, i + 2)
                        for c in range(C):
                            M(ps[:, 3, 0:D], kk[:, c * P:(c + 1) * P], cpw[:, c * D:(c + 1) * D], start=(c == 0),
                              stop=False)
                        M(ps[:, 3, 0:D], ones[0:1, :], bp_row[:], start=False, stop=True).then_inc(at_psum, 1)
                    while sorted_ < GAT.placed * (k + 1) // G:
                        place_column(GAT, i, sorted_)
                        sorted_ += 1

            with pe.Fori(0, NB) as i:
                conv_turn(i, True)
            with pe.Fori(NB, GAT.turns) as i:
                conv_turn(i, False)
            sort_end(GAT)

            pe.wait_ge(sorts[GAT]["sorted"], 1)
            flat = ps[:, 0:2, :].rearrange("p b n -> p (b n)")
            pe.wait_ge(wg_in, 16)
            pe.sem_inc(xt2_psum, RING)
            pe.sem_inc(h_psum, RING)

            def transpose_xn2(t, k):
                pe.wait_ge(xn2_ready, t + 1)
                transposed(xn2[k], 3 + k).then_inc(xt2_psum, 1)

            def node_rows(t, k):
                pe.wait_ge(xt2_ready, t + 1)
                chunks(flat[:, bass.ds(t * HW, HW)], cut(xnT2[k], P), cut(w_g, HW)).then_inc(h_psum, 1)

            transpose_xn2(0, 0)
            with pe.Fori(0, NB // RING) as u:
                for k in range(RING):
                    transpose_xn2(u * RING + (k + 1), (k + 1) % RING)
                    node_rows(u * RING + k, k)
            node_rows(NB - 1, 0)
            pe.wait_ge(hrow_ready, 1)
            clear(0, BANK)
            clear(1, BANK)
            pe.sem_inc(max_psum, G)
            four = ident_big[:].rearrange("p (a n) -> p a n", a=1).broadcast_to((P, GH, P))

            def max_tile(i, k):
                bank = 4 + k % RING
                pe.wait_ge(gat_noh, i * G + (k + 1))
                pe.wait_ge(max_taken, i * (2 * G) + (2 * k + 1))
                if k % HALF == 0:
                    pe.wait_ge(gat_kept, i * 2 + (k // HALF + 1))
                M(ps[:, bank, :].rearrange("p (h n) -> p h n", h=GH), nohb[k % RING], four, start=True, stop=False)
                for h in range(GH):
                    s1 = sbf[:, k * GH + h:k * GH + h + 1].broadcast_to((P, P))
                    ins = M(ps[:, bank, h * P:(h + 1) * P], s1, ident_b[:], start=False, stop=(h == GH - 1))
                ins.then_inc(max_psum, 1)

            x3 = xt3.rearrange("p (b c n) -> p b c n", b=2, c=C)

            def hidden(bank, e, par):
                for f in range(FC):
                    at = e * F + f * P
                    ins = chunks(ps[:, bank, f * P:(f + 1) * P],
                                 [w1[:, c * NE * F + at:c * NE * F + at + P] for c in range(C)],
                                 [x3[:, par, c, :] for c in range(C)])
                return ins

            def outputs(bank, e, par):
                for f in range(FC):
                    ins = M(ps[:, bank, 0:D], hT[:, par * F + f * P:par * F + (f + 1) * P],
                            w2[:, (e * FC + f) * D:(e * FC + f + 1) * D], start=(f == 0), stop=False)
                return M(ps[:, bank, 0:D], ones_b[0:PARTS, :], b2_b[:, e * D:(e + 1) * D], start=False, stop=True)

            pe.wait_ge(b2_ready, 1)
            M(ps[:, 3, 0:D], zero16[:], iota_t[:, 0:D], start=True, stop=True).then_inc(early_y, 1)
            pe.sem_inc(early_act, 1)
            pe.wait_ge(w1_in, 16)
            pe.wait_ge(w2_in, 16)
            with pe.Fori(0, PASS1_TURNS // 3) as u:
                def three_tiles(first):
                    for k in range(first, first + 3):
                        max_tile(u * 3 + k // G, k % G)

                for j in range(2 * NE):
                    e, n = j % NE, u * (2 * NE) + j
                    three_tiles(6 * j)
                    pe.wait_ge(early_act, n + 1)
                    if e == 0:
                        pe.wait_ge(xt3_in[0], u * 32 + (j // NE + 1) * 16)
                    hidden(2, e, 0).then_inc(early_hid, 1)
                    three_tiles(6 * j + 3)
                    pe.wait_ge(early_act, n + 2)
                    pe.wait_ge(early_kept, n + 1)
                    outputs(3, e, 0).then_inc(early_y, 1)
            for k in range(G):
                max_tile(PASS1_TURNS - 1, k)

            pe.wait_ge(self_e, 1)
            pe.sem_inc(sum_done, 3)
            pe.sem_inc(z_ready, 1)

            def turn_onehots(b, at):
                pe.wait_ge(oh_ready, b + 1)
                for k in range(HALF):
                    ins = nc.tensor.transpose(ps_b[:, 2 + at % 2, k * P:(k + 1) * P],
                                              ohb[at % OH_RING][:, k * P:(k + 1) * P], ident_b[:])
                ins.then_inc(ohT_psum, 1)

            dmb3 = dmb.rearrange("p (q n) -> p q n", q=PARTS)

            def fetch(bank, k, turned, col):
                w = PARTS * 2 * GH
                return M(ps[:, bank, k * w:(k + 1) * w].rearrange("p (q n) -> p q n", q=PARTS),
                         turned[:, k * P:(k + 1) * P], dmb3[:, :, bass.ds(col, 2 * GH)], start=True, stop=True)

            def fetch_targets(b, at):
                ats = columns(PE, dm_at, b * HALF, HALF, dm_most)
                pe.wait_ge(z_ready, b)
                pe.wait_ge(ohT_ready, b + 1)
                for k in range(HALF):
                    ins = fetch(6 + at % 2, k, ohT[at % 2], ats[k])
                ins.then_inc(dm_psum, 1)

            def sum_messages(b, at):
                ats = columns(PE, sum_at, b * HALF, HALF, sum_most)
                pe.wait_ge(m_ready, b + 1)
                for k in range(HALF):
                    for q in range(PARTS):
                        a = (q * HALF + k) * ROW
                        ins = M(flat[:, bass.ds(ats[k], ROW)], ohb[at % OH_RING][:, k * P:(k + 1) * P],
                                msgb3[at % 2][:, a:a + ROW], start=False, stop=False, skip_group_check=True)
                ins.then_inc(sum_done, 1)

            def pass2_step(b, at, first=False, last=False):
                if not first:
                    sum_messages(b - 2, at - 2)
                if not last or at + 2 < HALVES:
                    turn_onehots(b + 2, at + 2)
                if not last or at + 1 < HALVES:
                    fetch_targets(b + 1, at + 1)

            turn_onehots(0, 0)
            turn_onehots(1, 1)
            ats0 = columns(PE, dm_at, 0, HALF, dm_most)
            pe.wait_ge(ohT_ready, 1)
            for k in range(HALF):
                ins = fetch(6, k, ohT[0], ats0[k])
            ins.then_inc(dm_psum, 1)
            for b in range(2):
                pass2_step(b, b, first=True)
            with pe.Fori(0, PASS2_TURNS) as u:
                for k in range(OH_RING):
                    pass2_step(u * OH_RING + (k + 2), k + 2)
            for b in range(2 + PASS2_TURNS * OH_RING, HALVES):
                pass2_step(b, b, last=True)
            for b in range(HALVES - 2, HALVES):
                sum_messages(b, b)

            pe.sem_inc(y_psum, 2)

            def late_hidden(e, par):
                hidden(4 + e % 2, e, par).then_inc(hid_psum, 1)

            def late_outputs(e, n):
                pe.wait_ge(hid_ready, n + 1)
                pe.wait_ge(y_taken, n + 1)
                outputs(6 + e % 2, e, e % 2).then_inc(y_psum, 1)

            pe.wait_ge(xt3_in[0], 16 * (EARLY + 1))
            late_hidden(0, 0)

            for v in range(LATE):
                for e in range(NE):
                    if e < NE - 1:
                        late_hidden(e + 1, v % 2)
                    elif v < LATE - 1:
                        pe.wait_ge(xt3_in[(v + 1) % 2], 16 * ((v + 1) // 2 + EARLY + 1 if v % 2 else v // 2 + 1))
                        late_hidden(0, (v + 1) % 2)
                    late_outputs(e, v * NE + e)


def kernel(x, src, dst, L0_gnn_w0, L0_gnn_w1, L0_mix_Wq, L0_mix_Wkv, L0_mix_Wproj, L0_mix_bproj, L0_ffn_W_gat,
           L0_ffn_att_src, L0_ffn_att_dst, L0_ffn_b_gat, L0_ffn_ln_gamma, L0_ffn_ln_beta, L0_ffn_W1, L0_ffn_b1,
           L0_ffn_W2, L0_ffn_b2, L0_ffn_edge_index):
    import numpy as np
    import concourse.bacc as bacc
    from concourse.bass_utils import run_bass_kernel_spmd as run

    c = np.ascontiguousarray
    ei = np.asarray(L0_ffn_edge_index)
    w1 = np.asarray(L0_ffn_W1)
    arrays = {
        "x": c(x), "conv_target": c(src), "conv_source": c(dst), "gat_source": c(ei[0]), "gat_target": c(ei[1]),
        "w0": c(L0_gnn_w0), "w1": c(L0_gnn_w1), "WqT": c(np.asarray(L0_mix_Wq).T), "WkvT": c(np.asarray(L0_mix_Wkv).T),
        "WprojT": c(np.asarray(L0_mix_Wproj).T), "bproj": c(L0_mix_bproj), "W_gat": c(L0_ffn_W_gat),
        "att_src": c(L0_ffn_att_src).reshape(-1), "att_dst": c(L0_ffn_att_dst).reshape(-1), "b_gat": c(L0_ffn_b_gat),
        "gamma": c(L0_ffn_ln_gamma), "beta": c(L0_ffn_ln_beta),
        "W1": c(w1.transpose(1, 0, 2).reshape(D, NE * F)), "b1T": c(np.asarray(L0_ffn_b1).reshape(NE * FC, P).T),
        "W2": c(L0_ffn_W2).reshape(NE * F, D), "b2": c(L0_ffn_b2),
    }
    nc = bacc.Bacc("TRN2", target_bir_lowering=False, num_devices=1)
    io = {}
    for name, a in arrays.items():
        io[name] = nc.dram_tensor(f"in_{name}", a.shape, mybir.dt.from_np(a.dtype), kind="ExternalInput").ap()
    io["out"] = nc.dram_tensor("out", (N, D), F32, kind="ExternalOutput").ap()
    io["edges"] = {CONV: (io["conv_target"], io["conv_source"]), GAT: (io["gat_target"], io["gat_source"])}
    layer(nc, io)
    r = run(nc, [{f"in_{k}": a for k, a in arrays.items()}], core_ids=[0])
    return r.results[0]["out"]
```
